# Optimizing a Trainium2 kernel written in Bass

```python
import numpy as np
import jax
import jax.numpy as jnp

def _softmax(x, axis=-1):
    return jax.nn.softmax(x, axis=axis)
def _gelu(x):
    return jax.nn.gelu(x, approximate=True)
def _silu(x):
    return jax.nn.silu(x)
def _sigmoid(x):
    return jax.nn.sigmoid(x)
def _layernorm(x, axis=-1, eps=1e-5):
    m = jnp.mean(x, axis=axis, keepdims=True)
    v = jnp.var(x, axis=axis, keepdims=True)
    return (x - m) / jnp.sqrt(v + eps)
def _scatter_add(tgt, idx, src, axis=0):
    return tgt.at[idx].add(src)
def _segment_sum(src, seg, n):
    return jax.ops.segment_sum(src, seg, n)

kernel_name = 'mk_conv_attn_hybrid_d2_conv_nchw256_356722'

def setup_inputs(seed: int = 0):
    np.random.seed(seed)
    _w = jnp.asarray
    def _rec_inputs():
        import jax
        import jax.numpy as jnp
        _gk = jax.random.key(seed)
        x = -0.0009438 + 1 * jax.random.normal(jax.random.fold_in(_gk, 1), (2, 256, 48, 48), jnp.float32)
        return x
    x = _rec_inputs()
    def _L0_conv_setup():
        import jax, jax.numpy as jnp
        import numpy as np

        def _ln(x, g, b, eps=1e-05):
            m = jnp.mean(x, -1, keepdims=True)
            xc = x - m
            v = jnp.mean(xc * xc, -1, keepdims=True)
            return xc * jax.lax.rsqrt(v + eps) * g + b

        def _ss2d(x, in_W, conv_W, conv_b, x_proj_W, dt_W, dt_b, A_logs, Ds, og, ob, out_W):
            B, H, Wd, _ = x.shape
            Di = in_W.shape[1]
            K = x_proj_W.shape[0]
            R = dt_W.shape[2]
            N = (x_proj_W.shape[1] - R) // 2
            x = x @ in_W
            x = x.transpose(0, 3, 1, 2)
            x = jax.lax.conv_general_dilated(x, conv_W, (1, 1), 'SAME', feature_group_count=Di, dimension_numbers=('NCHW', 'OIHW', 'NCHW'))
            x = jax.nn.silu(x + conv_b[None, :, None, None])
            L = H * Wd
            x0 = x.reshape(B, Di, L)
            x1 = x.transpose(0, 1, 3, 2).reshape(B, Di, L)
            xs = jnp.stack([x0, x1, x0[..., ::-1], x1[..., ::-1]], 1)
            dbl = jnp.einsum('bkdl,kcd->bkcl', xs, x_proj_W)
            dts, Bmat, Cmat = jnp.split(dbl, [R, R + N], axis=2)
            delta = jax.nn.softplus(jnp.einsum('bkrl,kdr->bkdl', dts, dt_W) + dt_b[None, :, :, None])
            A = -jnp.exp(A_logs).reshape(K, Di, N)
            d_t = delta.transpose(3, 0, 1, 2)
            u_t = xs.transpose(3, 0, 1, 2)
            B_t = Bmat.transpose(3, 0, 1, 2)
            C_t = Cmat.transpose(3, 0, 1, 2)

            def step(h, inp):
                d, u, Bv, Cv = inp
                dA = jnp.exp(d[..., None] * A)
                h = h * dA + (d * u)[..., None] * Bv[:, :, None, :]
                return (h, jnp.einsum('bkdn,bkn->bkd', h, Cv))
            h0 = jnp.zeros((B, K, Di, N), x.dtype)
            _, ys = jax.lax.scan(step, h0, (d_t, u_t, B_t, C_t))
            ys = ys.transpose(1, 2, 3, 0)
            ys = ys + xs * Ds.reshape(1, K, Di, 1)
            y = ys[:, 0] + ys[:, 2, :, ::-1]
            y2 = ys[:, 1] + ys[:, 3, :, ::-1]
            y = y + y2.reshape(B, Di, Wd, H).transpose(0, 1, 3, 2).reshape(B, Di, L)
            y = y.reshape(B, Di, H, Wd).transpose(0, 2, 3, 1)
            y = _ln(y, og, ob)
            return y @ out_W

        def _pvm(x, ln_g, ln_b, skip_scale, proj_W, proj_b, in_W, conv_W, conv_b, x_proj_W, dt_W, dt_b, A_logs, Ds, onorm_g, onorm_b, out_W):
            x = x.transpose(0, 2, 3, 1)
            xn = _ln(x, ln_g, ln_b)
            branches = jnp.split(xn, 4, axis=3)
            outs = [_ss2d(xi, in_W, conv_W, conv_b, x_proj_W, dt_W, dt_b, A_logs, Ds, onorm_g, onorm_b, out_W) + skip_scale * xi for xi in branches]
            y = jnp.concatenate(outs, -1)
            y = _ln(y, ln_g, ln_b)
            y = y @ proj_W + proj_b
            return y.transpose(0, 3, 1, 2)
        key = jax.random.key(seed)
        ks = jax.random.split(key, 16)
        B, C, H, W = (2, 256, 48, 48)
        Dm, Di, R, N, K, Co = (C // 4, C // 2, 4, 16, 4, 256)
        dt = jax.random.uniform(ks[10], (K, Di), minval=0.001, maxval=0.1)
        return {'x': jax.random.normal(ks[0], (B, C, H, W), jnp.float32), 'ln_g': jnp.ones((C,), jnp.float32), 'ln_b': jnp.zeros((C,), jnp.float32), 'skip_scale': jnp.ones((1,), jnp.float32), 'proj_W': jax.random.normal(ks[1], (C, Co), jnp.float32) * C ** (-0.5), 'proj_b': jnp.zeros((Co,), jnp.float32), 'in_W': jax.random.normal(ks[2], (Dm, Di), jnp.float32) * Dm ** (-0.5), 'conv_W': jax.random.normal(ks[3], (Di, 1, 3, 3), jnp.float32) * 0.2, 'conv_b': jax.random.normal(ks[4], (Di,), jnp.float32) * 0.02, 'x_proj_W': jax.random.normal(ks[5], (K, R + 2 * N, Di), jnp.float32) * Di ** (-0.5), 'dt_W': jax.random.normal(ks[6], (K, Di, R), jnp.float32) * R ** (-0.5), 'dt_b': dt + jnp.log(-jnp.expm1(-dt)), 'A_logs': jnp.log(jnp.tile(jnp.arange(1, N + 1, dtype=jnp.float32), (K * Di, 1))), 'Ds': jnp.ones((K * Di,), jnp.float32), 'onorm_g': jnp.ones((Di,), jnp.float32), 'onorm_b': jnp.zeros((Di,), jnp.float32), 'out_W': jax.random.normal(ks[7], (Di, Dm), jnp.float32) * Di ** (-0.5)}
    _L0_conv_all = _L0_conv_setup()
    _L0_conv_in = {k: v for k, v in _L0_conv_all.items() if k in ('ln_g', 'ln_b', 'skip_scale', 'proj_W', 'proj_b', 'in_W', 'conv_W', 'conv_b', 'x_proj_W', 'dt_W', 'dt_b', 'A_logs', 'Ds', 'onorm_g', 'onorm_b', 'out_W', )}
    del _L0_conv_all

    def _L1_attn_setup():
        import jax, jax.numpy as jnp
        import numpy as np
        TEMPERATURE = 1.0
        W_BLEND = 0.8
        EPS = 1e-12

        def _l2norm(x):
            n = jnp.sqrt(jnp.sum(x * x, axis=-1, keepdims=True))
            return x / jnp.maximum(n, EPS)
        key = jax.random.key(seed)
        feats = jax.random.normal(key, (4, 2048, 256), dtype=jnp.float32)
        return {'feats': feats}
    _L1_attn_all = _L1_attn_setup()
    _L1_attn_in = {k: v for k, v in _L1_attn_all.items() if k in ()}
    del _L1_attn_all

    def _L1_ffn_setup():
        import jax, jax.numpy as jnp
        import numpy as np
        B, T, D, H, E = (16, 4096, 256, 512, 8)
        key = jax.random.key(seed)
        ks = jax.random.split(key, 5)
        x = jax.random.normal(ks[0], (B, T, D), dtype=jnp.float32)
        gate_w = jax.random.normal(ks[1], (D, E), dtype=jnp.float32) * 0.02
        gate_b = jnp.zeros((E,), dtype=jnp.float32)
        W1 = jax.random.normal(ks[2], (E, D, H), dtype=jnp.float32) * 0.02
        b1 = jnp.zeros((E, H), dtype=jnp.float32)
        W2 = jax.random.normal(ks[3], (E, H, D), dtype=jnp.float32) * 0.02
        b2 = jnp.zeros((E, D), dtype=jnp.float32)
        return {'x': x, 'gate_w': gate_w, 'gate_b': gate_b, 'W1': W1, 'b1': b1, 'W2': W2, 'b2': b2}
    _L1_ffn_all = _L1_ffn_setup()
    _L1_ffn_in = {k: v for k, v in _L1_ffn_all.items() if k in ('gate_w', 'gate_b', 'W1', 'b1', 'W2', 'b2', )}
    del _L1_ffn_all

    return {
        "x": x,
        "L0_conv_ln_g": _L0_conv_in["ln_g"],
        "L0_conv_ln_b": _L0_conv_in["ln_b"],
        "L0_conv_skip_scale": _L0_conv_in["skip_scale"],
        "L0_conv_proj_W": _L0_conv_in["proj_W"],
        "L0_conv_proj_b": _L0_conv_in["proj_b"],
        "L0_conv_in_W": _L0_conv_in["in_W"],
        "L0_conv_conv_W": _L0_conv_in["conv_W"],
        "L0_conv_conv_b": _L0_conv_in["conv_b"],
        "L0_conv_x_proj_W": _L0_conv_in["x_proj_W"],
        "L0_conv_dt_W": _L0_conv_in["dt_W"],
        "L0_conv_dt_b": _L0_conv_in["dt_b"],
        "L0_conv_A_logs": _L0_conv_in["A_logs"],
        "L0_conv_Ds": _L0_conv_in["Ds"],
        "L0_conv_onorm_g": _L0_conv_in["onorm_g"],
        "L0_conv_onorm_b": _L0_conv_in["onorm_b"],
        "L0_conv_out_W": _L0_conv_in["out_W"],
        "L1_ffn_gate_w": _L1_ffn_in["gate_w"],
        "L1_ffn_gate_b": _L1_ffn_in["gate_b"],
        "L1_ffn_W1": _L1_ffn_in["W1"],
        "L1_ffn_b1": _L1_ffn_in["b1"],
        "L1_ffn_W2": _L1_ffn_in["W2"],
        "L1_ffn_b2": _L1_ffn_in["b2"],
    }

def reference(x, L0_conv_ln_g, L0_conv_ln_b, L0_conv_skip_scale, L0_conv_proj_W, L0_conv_proj_b, L0_conv_in_W, L0_conv_conv_W, L0_conv_conv_b, L0_conv_x_proj_W, L0_conv_dt_W, L0_conv_dt_b, L0_conv_A_logs, L0_conv_Ds, L0_conv_onorm_g, L0_conv_onorm_b, L0_conv_out_W, L1_ffn_gate_w, L1_ffn_gate_b, L1_ffn_W1, L1_ffn_b1, L1_ffn_W2, L1_ffn_b2):
    import jax
    import jax.numpy as jnp
    def _L0_conv_ref(x, ln_g, ln_b, skip_scale, proj_W, proj_b, in_W, conv_W, conv_b, x_proj_W, dt_W, dt_b, A_logs, Ds, onorm_g, onorm_b, out_W):
        import jax, jax.numpy as jnp
        import numpy as np

        def _ln(x, g, b, eps=1e-05):
            m = jnp.mean(x, -1, keepdims=True)
            xc = x - m
            v = jnp.mean(xc * xc, -1, keepdims=True)
            return xc * jax.lax.rsqrt(v + eps) * g + b

        def _ss2d(x, in_W, conv_W, conv_b, x_proj_W, dt_W, dt_b, A_logs, Ds, og, ob, out_W):
            B, H, Wd, _ = x.shape
            Di = in_W.shape[1]
            K = x_proj_W.shape[0]
            R = dt_W.shape[2]
            N = (x_proj_W.shape[1] - R) // 2
            x = x @ in_W
            x = x.transpose(0, 3, 1, 2)
            x = jax.lax.conv_general_dilated(x, conv_W, (1, 1), 'SAME', feature_group_count=Di, dimension_numbers=('NCHW', 'OIHW', 'NCHW'))
            x = jax.nn.silu(x + conv_b[None, :, None, None])
            L = H * Wd
            x0 = x.reshape(B, Di, L)
            x1 = x.transpose(0, 1, 3, 2).reshape(B, Di, L)
            xs = jnp.stack([x0, x1, x0[..., ::-1], x1[..., ::-1]], 1)
            dbl = jnp.einsum('bkdl,kcd->bkcl', xs, x_proj_W)
            dts, Bmat, Cmat = jnp.split(dbl, [R, R + N], axis=2)
            delta = jax.nn.softplus(jnp.einsum('bkrl,kdr->bkdl', dts, dt_W) + dt_b[None, :, :, None])
            A = -jnp.exp(A_logs).reshape(K, Di, N)
            d_t = delta.transpose(3, 0, 1, 2)
            u_t = xs.transpose(3, 0, 1, 2)
            B_t = Bmat.transpose(3, 0, 1, 2)
            C_t = Cmat.transpose(3, 0, 1, 2)

            def step(h, inp):
                d, u, Bv, Cv = inp
                dA = jnp.exp(d[..., None] * A)
                h = h * dA + (d * u)[..., None] * Bv[:, :, None, :]
                return (h, jnp.einsum('bkdn,bkn->bkd', h, Cv))
            h0 = jnp.zeros((B, K, Di, N), x.dtype)
            _, ys = jax.lax.scan(step, h0, (d_t, u_t, B_t, C_t))
            ys = ys.transpose(1, 2, 3, 0)
            ys = ys + xs * Ds.reshape(1, K, Di, 1)
            y = ys[:, 0] + ys[:, 2, :, ::-1]
            y2 = ys[:, 1] + ys[:, 3, :, ::-1]
            y = y + y2.reshape(B, Di, Wd, H).transpose(0, 1, 3, 2).reshape(B, Di, L)
            y = y.reshape(B, Di, H, Wd).transpose(0, 2, 3, 1)
            y = _ln(y, og, ob)
            return y @ out_W

        def _pvm(x, ln_g, ln_b, skip_scale, proj_W, proj_b, in_W, conv_W, conv_b, x_proj_W, dt_W, dt_b, A_logs, Ds, onorm_g, onorm_b, out_W):
            x = x.transpose(0, 2, 3, 1)
            xn = _ln(x, ln_g, ln_b)
            branches = jnp.split(xn, 4, axis=3)
            outs = [_ss2d(xi, in_W, conv_W, conv_b, x_proj_W, dt_W, dt_b, A_logs, Ds, onorm_g, onorm_b, out_W) + skip_scale * xi for xi in branches]
            y = jnp.concatenate(outs, -1)
            y = _ln(y, ln_g, ln_b)
            y = y @ proj_W + proj_b
            return y.transpose(0, 3, 1, 2)
        return _pvm(x, ln_g, ln_b, skip_scale, proj_W, proj_b, in_W, conv_W, conv_b, x_proj_W, dt_W, dt_b, A_logs, Ds, onorm_g, onorm_b, out_W)

    def _L1_attn_ref(feats):
        import jax, jax.numpy as jnp
        import numpy as np
        TEMPERATURE = 1.0
        W_BLEND = 0.8
        EPS = 1e-12

        def _l2norm(x):
            n = jnp.sqrt(jnp.sum(x * x, axis=-1, keepdims=True))
            return x / jnp.maximum(n, EPS)
        B, N, C = feats.shape
        f = _l2norm(feats.reshape(B * N, C))
        scores = jnp.matmul(f, f.T) / TEMPERATURE
        attn = jax.nn.softmax(scores, axis=-1)
        feats_att = jnp.matmul(attn, f)
        feats_fcm = f * W_BLEND + feats_att * (1.0 - W_BLEND)
        return _l2norm(feats_fcm.reshape(B, N, C))

    def _L1_ffn_ref(x, gate_w, gate_b, W1, b1, W2, b2):
        import jax, jax.numpy as jnp
        import numpy as np
        B, T, D, H, E = (16, 4096, 256, 512, 8)
        Bb, Tt, Dd = x.shape
        Ee = gate_w.shape[1]
        xf = x.reshape(-1, Dd)
        N = xf.shape[0]
        logits = xf @ gate_w + gate_b
        probs = jax.nn.softmax(logits, axis=-1)
        top2_vals, top2_idx = jax.lax.top_k(probs, 2)
        cw = jnp.zeros((N, Ee), dtype=xf.dtype).at[jnp.arange(N)[:, None], top2_idx].add(top2_vals)

        def step(acc, params):
            w1, bb1, w2, bb2, we = params
            h = jax.nn.gelu(xf @ w1 + bb1, approximate=False)
            y = h @ w2 + bb2
            return (acc + we[:, None] * y, None)
        out, _ = jax.lax.scan(step, jnp.zeros_like(xf), (W1, b1, W2, b2, cw.T))
        return out.reshape(Bb, Tt, Dd)

    def _gn(v, G=32, eps=1e-5):
        B_, C_, H_, W_ = v.shape
        g = v.reshape(B_, G, C_ // G, H_, W_)
        m = jnp.mean(g, axis=(2, 3, 4), keepdims=True)
        s = jnp.var(g, axis=(2, 3, 4), keepdims=True)
        return ((g - m) / jnp.sqrt(s + eps)).reshape(v.shape)

    def _ln_c(v, eps=1e-6):
        m = jnp.mean(v, axis=1, keepdims=True)
        s = jnp.var(v, axis=1, keepdims=True)
        return (v - m) / jnp.sqrt(s + eps)

    def _ln_t(v, eps=1e-5):
        m = jnp.mean(v, axis=-1, keepdims=True)
        s = jnp.var(v, axis=-1, keepdims=True)
        return (v - m) / jnp.sqrt(s + eps)

    def _to_tokens(v):
        B_, C_, H_, W_ = v.shape
        return v.reshape(B_, C_, H_ * W_).transpose(0, 2, 1)
    def _from_tokens(t, like):
        B_, C_, H_, W_ = like.shape
        return t.transpose(0, 2, 1).reshape(B_, C_, H_, W_)

    x = _L0_conv_ref(x, L0_conv_ln_g, L0_conv_ln_b, L0_conv_skip_scale, L0_conv_proj_W, L0_conv_proj_b, L0_conv_in_W, L0_conv_conv_W, L0_conv_conv_b, L0_conv_x_proj_W, L0_conv_dt_W, L0_conv_dt_b, L0_conv_A_logs, L0_conv_Ds, L0_conv_onorm_g, L0_conv_onorm_b, L0_conv_out_W)
    t = _to_tokens(x)
    t = t + _L1_attn_ref(_ln_t(t))
    t = t + _L1_ffn_ref(_ln_t(t), L1_ffn_gate_w, L1_ffn_gate_b, L1_ffn_W1, L1_ffn_b1, L1_ffn_W2, L1_ffn_b2)
    x = _from_tokens(t, x)
    return x


_drawn_inputs = setup_inputs


def setup_inputs(seed=0):
    import zlib

    import numpy as np

    out = dict(_drawn_inputs(seed))
    spreads = {'L0_conv_ln_g': (1.0, 0.2),
     'L0_conv_ln_b': (0.0, 0.1),
     'L0_conv_proj_b': (0.0, 0.1),
     'L0_conv_Ds': (1.0, 0.6),
     'L0_conv_onorm_g': (1.0, 0.2),
     'L0_conv_onorm_b': (0.0, 0.1),
     'L1_ffn_gate_b': (0.0, 0.666),
     'L1_ffn_b1': (0.0, 0.8),
     'L1_ffn_b2': (0.0, 0.364)}
    factors = {'L0_conv_x_proj_W': 4.426,
     'L0_conv_dt_W': 8.0,
     'L0_conv_dt_b': 8.0,
     'L0_conv_A_logs': 6.862,
     'L1_ffn_W1': 3.347,
     'L1_ffn_W2': 3.122}
    for name, (base, spread) in spreads.items():
        noise = np.random.default_rng([zlib.crc32(name.encode()), seed]).standard_normal(out[name].shape)
        drawn = base * np.exp(spread * noise) if base else spread * noise
        out[name] = jnp.asarray(drawn.astype(out[name].dtype))
    for name, factor in factors.items():
        out[name] = (out[name] * factor).astype(out[name].dtype)
    return out
```

```python
import math
from contextlib import ExitStack

import concourse.bass as bass
from concourse import mybir

F32 = mybir.dt.float32
BF16 = mybir.dt.bfloat16
U32 = mybir.dt.uint32
ALU = mybir.AluOpType
ACT = mybir.ActivationFunctionType
AX = mybir.AxisListType

B, C, H, W = 2, 256, 48, 48
L = H * W
NT = B * L
BR = 4
U = B * BR
DM = C // BR
D = 128
K = 4
R, N = 4, 16
WC = 768
NCH = L // WC
HW_ = WC // 2
STEPS = K * NCH
NKC = U * STEPS
J = 128 // N
G = D // J
TT = 384
NTT = NT // TT
TPI = L // TT
KB = NT // 128
E, HF = 8, 512
HB = HF // 128


class Space:

    def __init__(self, nc, ctx, tag):
        self.nc, self.ctx, self.tag = nc, ctx, tag

    def sb(self, name, shape, dt=F32):
        return self.ctx.enter_context(self.nc.sbuf_tensor(f"{self.tag}_{name}", shape, dt))

    def ps(self, name, shape, dt=F32):
        return self.ctx.enter_context(self.nc.psum_tensor(f"{self.tag}_{name}", shape, dt))

    def sem(self, name):
        return self.ctx.enter_context(self.nc.semaphore(f"{self.tag}_{name}"))


def setup_phase(nc, P, w, keep):
    with ExitStack() as ctx:
        s = Space(nc, ctx, "setup")
        dts_rows = s.sb("dts_rows", [R, K, D])
        dtw_t = s.sb("dtw_t", [R, K, D])
        bc_rows = s.sb("bc_rows", [2 * N, K, D])
        conv_taps = s.sb("conv_taps", [128, D, 9])
        in_w2 = s.sb("in_w2", [128, D])
        ds4 = s.sb("ds4", [D, K])
        a_log = s.sb("a_log", [128, K, G])
        a_exp = s.sb("a_exp", [128, K, G])
        ps_w = s.ps("ps_w", [128, 4, 512])
        loaded, ones_set, ident_set = s.sem("loaded"), s.sem("ones_set"), s.sem("ident_set")
        weff_ps, bc_ps, exp_done, a_done = s.sem("weff_ps"), s.sem("bc_ps"), s.sem("exp_done"), s.sem("a_done")
        rec_out, pool_set, dve_done = s.sem("rec_out"), s.sem("pool_set"), s.sem("dve_done")
        loads = []
        loads.append((dts_rows[:, :, :], w["x_proj_W"][:, 0:R, :].rearrange("k c d -> c k d")))
        loads.append((dtw_t[:, :, :], w["dt_W"].rearrange("k d r -> r k d")))
        loads.append((bc_rows[:, :, :], w["x_proj_W"][:, R:, :].rearrange("k c d -> c k d")))
        for half in range(2):
            loads.append((in_w2[64 * half:64 * half + 64, :], w["in_W"]))
        loads.append((conv_taps[:, :, :], w["conv_W"].rearrange("d a y x -> (a d) (y x)").partition_broadcast(128)))
        loads.append((ds4[:, :], w["Ds"].rearrange("(k d) -> d k", k=K)))
        loads.append((keep["dt_b"][:, :], w["dt_b"].rearrange("k d -> d k")))
        loads.append((keep["conv_b"][:, :], w["conv_b"].rearrange("(d a) -> d a", a=1)))
        loads.append((keep["onorm_g"][:, :], w["onorm_g"].rearrange("(d a) -> d a", a=1)))
        loads.append((keep["onorm_b"][:, :], w["onorm_b"].rearrange("(d a) -> d a", a=1)))
        loads.append((keep["out_W"][:, :], w["out_W"]))
        loads.append((keep["ln_g"][:, :], w["ln_g"].rearrange("(h p) -> p h", h=2)))
        loads.append((keep["ln_b"][:, :], w["ln_b"].rearrange("(h p) -> p h", h=2)))
        loads.append((keep["proj_b"][:, :], w["proj_b"].rearrange("(h p) -> p h", h=2)))
        loads.append((keep["proj_W"][:, :, :], w["proj_W"].rearrange("(h p) n -> p h n", h=2)))
        loads.append((keep["skip"][:, :], w["skip_scale"].partition_broadcast(64)))
        a_src = w["A_logs"].rearrange("(k g j) n -> j n k g", k=K, j=J)
        for j in range(J):
            for k in range(K):
                loads.append((a_log[N * j:N * j + N, k, :], a_src[j, :, k, :]))
        n_loads = len(loads)
        block = ctx.enter_context(nc.Block())

        @block.sync
        def _(sp):
            for dst, src in loads:
                sp.dma_start(dst, src, allow_slow_non_contiguous=True).then_inc(loaded, 16)
            sp.wait_ge(a_done, 1)
            sp.wait_ge(dve_done, 1)
            with sp.Fori(0, U) as u:
                sp.dma_start(P["rec"][u].rearrange("s p f -> p s f"), keep["rec"][:, :, :]).then_inc(rec_out, 16)
            sp.wait_ge(rec_out, 16 * U)

        @block.gpsimd
        def _(pool):
            pool.memset(keep["ident"][:, :], 0.0).then_inc(ones_set, 1)
            pool.memset(keep["ones_c"][:, :], 1.0 / C).then_inc(pool_set, 1)
            pool.memset(keep["ones_d"][:, :], 1.0 / D).then_inc(pool_set, 1)
            pool.memset(keep["ones"][:, :], 1.0).then_inc(pool_set, 1)
            pool.memset(keep["eps"][:, :], 1e-5).then_inc(pool_set, 1)
            pool.memset(keep["ln_2_20"][:, :], 20 * math.log(2.0))
            pool.memset(keep["parts_sel"][:, :, :, :], 0.0).then_inc(ones_set, 1)
            pool.memset(keep["sum_sel"][:, :], 1.0).then_inc(ones_set, 1)
            pool.memset(keep["exp_sel"][:, :, :], 0.0).then_inc(ones_set, 1)
            pool.wait_ge(ones_set, 4)
            pool.affine_select(out=keep["ident"][:, :], in_=keep["ident"][:, :], compare_op=ALU.not_equal,
                               fill=1.0, base=0, pattern=[[-1, 128]], channel_multiplier=1).then_inc(ident_set, 1)
            for part in range(3):
                pool.wait_ge(ident_set, part + 1)
                v = keep["parts_sel"][:, :, :, :]
                pool.affine_select(out=v, in_=v, compare_op=ALU.not_equal, fill=1.0, base=-32 * part,
                                   pattern=[[-J, 4], [-1, J], [0, N]], channel_multiplier=1).then_inc(ident_set, 1)
            v = keep["sum_sel"][:, :]
            pool.affine_select(out=v, in_=v, compare_op=ALU.is_ge, fill=0.0, base=N * (D - J),
                               pattern=[[-N, 2 * D - J]], channel_multiplier=1).then_inc(ident_set, 1)
            pool.wait_ge(ident_set, 5)
            pool.affine_select(out=v, in_=v, compare_op=ALU.is_ge, fill=0.0, base=N - 1 - N * (D - J),
                               pattern=[[N, 2 * D - J]], channel_multiplier=-1).then_inc(ident_set, 1)
            v = keep["exp_sel"][:, :, :]
            pool.affine_select(out=v, in_=v, compare_op=ALU.not_equal, fill=1.0, base=0,
                               pattern=[[-1, E], [0, 128]], channel_multiplier=1).then_inc(ident_set, 1)

        @block.tensor
        def _(pe):
            pe.wait_ge(loaded, 16 * n_loads)
            for k in range(K):
                mm = pe.matmul(ps_w[:, k, 0:D], dts_rows[:, k, :], dtw_t[:, k, :], start=True, stop=True)
            mm.then_inc(weff_ps, 1)
            pe.wait_ge(ident_set, 1)
            pe.wait_ge(dve_done, 1)
            for k in range(K):
                mm = pe.transpose(ps_w[:, k, 256:256 + 2 * N], bc_rows[:, k, :], keep["ident"][0:2 * N, 0:2 * N])
            mm.then_inc(bc_ps, 1)

        @block.scalar
        def _(act):
            act.wait_ge(loaded, 16 * n_loads)
            act.activation(a_exp[:, :, :], a_log[:, :, :], ACT.Exp).then_inc(exp_done, 1)

        @block.vector
        def _(dve):
            dve.memset(keep["rec"][:, :, G:G + 1], 1.0).then_inc(pool_set, 1)
            dve.wait_ge(weff_ps, 1)
            dve.tensor_copy(keep["w_eff"][:, :, :], ps_w[:, :, 0:D]).then_inc(dve_done, 1)
            dve.wait_ge(exp_done, 1)
            dve.wait_ge(pool_set, 5)
            for c in range(NCH):
                rec = keep["rec"][:, :, :].rearrange("p (k c) f -> p k c f", c=NCH)
                last = dve.tensor_scalar(rec[:, :, c, 0:G], a_exp[:, :, :], -1.0, None, ALU.mult)
            dve.memset(rec[:, :, NCH - 1, G:G + 1], 0.0).then_inc(a_done, 1)
            for dy in range(3):
                for half in range(2):
                    p = slice(64 * half, 64 * half + 64)
                    dve.tensor_tensor(keep["w_pair"][p, dy, :], in_w2[p, :], conv_taps[p, :, 3 * dy + half], ALU.mult)
                dve.tensor_tensor(keep["w_one"][:, dy, :], in_w2[0:64, :], conv_taps[0:64, :, 3 * dy + 2], ALU.mult)
            dve.tensor_reduce(keep["d_sum"][:, :], ds4[:, :], AX.X, ALU.add)
            dve.wait_ge(bc_ps, 1)
            dve.tensor_copy(keep["w_bc"][:, :, :], ps_w[:, :, 256:256 + 2 * N])


def norm_phase(nc, tag, src, dst, keep):
    LN = 3
    with ExitStack() as ctx:
        s = Space(nc, ctx, tag)
        x = s.sb("x", [128, LN, 2, TT])
        xc = s.sb("xc", [128, LN, 2, TT])
        sq = s.sb("sq", [128, LN, 2, TT])
        sd = s.sb("sd", [128, LN, TT])
        rs = s.sb("rs", [128, LN, TT])
        ps_m = s.ps("ps_m", [128, LN, 512])
        ps_v = s.ps("ps_v", [128, LN, 512])
        came = [s.sem(f"came{i}") for i in range(LN)]
        link = [s.sem(f"link{i}") for i in range(LN)]
        gone = [s.sem(f"gone{i}") for i in range(LN)]
        STEP = 8
        block = ctx.enter_context(nc.Block())
        sv = src.rearrange("b (h p) (i t) -> b i p h t", h=2, t=TT)
        dv = dst.rearrange("b (h p) (i t) -> b i p h t", h=2, t=TT)

        @block.sync
        def _(sp):
            for ln in range(LN):
                sp.sem_inc(link[ln], 1)
                sp.sem_inc(gone[ln], 16)
            with sp.Fori(0, B) as b:
                with sp.Fori(0, TPI // LN) as i:
                    for ln in range(LN):
                        sp.wait_ge(link[ln], b * (STEP * TPI // LN) + i * STEP + 1)
                        sp.dma_start(x[:, ln, :, :], sv[b, i * LN + ln]).then_inc(came[ln], 16)
                    for ln in range(LN):
                        sp.wait_ge(link[ln], b * (STEP * TPI // LN) + i * STEP + STEP + 1)
                        sp.dma_start(dv[b, i * LN + ln], sq[:, ln, :, :]).then_inc(gone[ln], 16)
            for ln in range(LN):
                sp.wait_ge(gone[ln], 16 * (NTT // LN) + 16)

        @block.tensor
        def _(pe):
            with pe.Fori(0, NTT // LN) as i:
                for ln in range(LN):
                    pe.wait_ge(came[ln], i * 16 + 16)
                    for h in range(2):
                        mm = pe.matmul(ps_m[:, ln, 0:TT], keep["ones_c"][:, :], x[:, ln, h, :], start=h == 0, stop=h == 1)
                    mm.then_inc(link[ln], 1)
                for ln in range(LN):
                    pe.wait_ge(link[ln], i * STEP + 4)
                    for h in range(2):
                        mm = pe.matmul(ps_v[:, ln, 0:TT], keep["ones_c"][:, :], sq[:, ln, h, :], start=h == 0, stop=h == 1)
                    mm.then_inc(link[ln], 1)

        @block.vector
        def _(dve):
            with dve.Fori(0, NTT // LN) as i:
                for ln in range(LN):
                    dve.wait_ge(link[ln], i * STEP + 2)
                    mean = ps_m[:, ln, 0:TT].unsqueeze(1).to_broadcast([128, 2, TT])
                    dve.tensor_tensor(xc[:, ln, :, :], x[:, ln, :, :], mean, ALU.subtract).then_inc(link[ln], 1)
                for ln in range(LN):
                    dve.wait_ge(link[ln], i * STEP + 7)
                    inv = rs[:, ln, :].unsqueeze(1).to_broadcast([128, 2, TT])
                    dve.tensor_tensor(xc[:, ln, :, :], xc[:, ln, :, :], inv, ALU.mult).then_inc(link[ln], 1)

        @block.scalar
        def _(act):
            with act.Fori(0, NTT // LN) as i:
                for ln in range(LN):
                    act.wait_ge(link[ln], i * STEP + 3)
                    act.wait_ge(gone[ln], i * 16 + 16)
                    act.activation(sq[:, ln, :, :], xc[:, ln, :, :], ACT.Square).then_inc(link[ln], 1)
                for ln in range(LN):
                    act.wait_ge(link[ln], i * STEP + 5)
                    act.activation(sd[:, ln, :], ps_v[:, ln, 0:TT], ACT.Ln, bias=keep["eps"][:, 0:1]).then_inc(link[ln], 1)
                for ln in range(LN):
                    act.wait_ge(link[ln], i * STEP + 6)
                    act.activation(rs[:, ln, :], sd[:, ln, :], ACT.Exp, scale=-0.5).then_inc(link[ln], 1)
                for ln in range(LN):
                    act.wait_ge(link[ln], i * STEP + 8)
                    for h in range(2):
                        last = act.activation(sq[:, ln, h, :], xc[:, ln, h, :], ACT.Identity,
                                              scale=keep["ln_g"][:, h:h + 1], bias=keep["ln_b"][:, h:h + 1])
                    last.then_inc(link[ln], 1)


def conv_phase(nc, P, keep, xs):
    with ExitStack() as ctx:
        s = Space(nc, ctx, "conv")
        pad = s.sb("pad", [128, 2, H + 2, W + 2])
        ps_c = s.ps("ps_c", [128, 4, 512])
        cleared, came, full, out = s.sem("cleared"), [s.sem("came0"), s.sem("came1")], s.sem("full"), s.sem("out")
        TU = TPI
        CR = 2 * TU
        block = ctx.enter_context(nc.Block())
        src = P["xn"].rearrange("b (r c) l -> (b r) c l", r=BR)

        @block.sync
        def _(sp):
            sp.wait_ge(cleared, 1)
            with sp.Fori(0, U // 2) as i:
                for k in range(2):
                    sp.wait_ge(out, i * (2 * TU) + (CR - TU + k * TU))
                    img = src[i * 2 + k].rearrange("c (h w) -> c h w", h=H)
                    for half in range(2):
                        sp.dma_start(pad[64 * half:64 * half + 64, k, 1:H + 1, 1 - half:W + 1 - half], img).then_inc(came[k], 16)

        @block.tensor
        def _(pe):
            with pe.Fori(0, U // 2) as i:
                for k in range(2):
                    pe.wait_ge(came[k], i * 32 + 32)
                    for t in range(TU):
                        n = k * TU + t
                        pe.wait_ge(out, i * (2 * TU) + (n + CR - 3))
                        o = ps_c[:, n % 4, 0:TT]
                        r0 = t * (TT // W)
                        for dy in range(3):
                            rows = slice(r0 + dy, r0 + dy + TT // W)
                            pe.matmul(o, keep["w_pair"][:, dy, :], pad[:, k, rows, 0:W], start=dy == 0, stop=False)
                            mm = pe.matmul(o, keep["w_one"][:, dy, :], pad[0:64, k, rows, 2:W + 2], start=False, stop=dy == 2)
                        mm.then_inc(full, 1)

        @block.vector
        def _(dve):
            dve.memset(pad[:, :, :, :], 0.0).then_inc(cleared, 1)

        @block.scalar
        def _(act):
            act.sem_inc(out, CR)
            with act.Fori(0, U // 2) as i:
                for n in range(2 * TU):
                    act.wait_ge(full, i * (2 * TU) + n + 1)
                    act.activation(xs[:, bass.ds(i * (2 * L) + n * TT, TT)], ps_c[:, n % 4, 0:TT], ACT.Silu,
                                   bias=keep["conv_b"][:, 0:1]).then_inc(out, 1)


def scan_order(x, k, at, size):
    if k % 2 == 0:
        return x[:, L - 1 - at:(L - 1 - at - size) if L - 1 - at - size >= 0 else None:-1] if k == 2 else x[:, at:at + size]
    v = x.rearrange("p (h w) -> p w h", h=H)
    w0, nw = at // H, size // H
    if k == 1:
        return v[:, w0:w0 + nw, :]
    lo = W - 1 - w0 - nw
    return v[:, W - 1 - w0:(lo if lo >= 0 else None):-1, ::-1]


def like(x, view):
    return x if len(view.shape) == 2 else x.rearrange("p (a b) -> p a b", b=H)


def delta_phase(nc, P, keep, xs):
    with ExitStack() as ctx:
        s = Space(nc, ctx, "delta")
        xu = s.sb("xu", [128, L])
        two = lambda name, dt=F32: [s.sb(f"{name}{i}", [128, WC], dt) for i in range(2)]
        mag, pos, ex, lg = two("mag"), two("pos"), two("ex"), two("lg")
        dm, co, sm = two("dm"), two("co"), two("sm")
        delta, du, rd, ru = two("delta"), two("du"), two("rd"), two("ru")
        parts = [s.sb(f"parts{i}", [128, 3, 2, WC], BF16) for i in range(2)]
        bc = [s.sb(f"bc{i}", [2 * N, WC]) for i in range(2)]
        ps_a = [s.ps(f"ps_a{i}", [128, 2, 512]) for i in range(2)]
        ps_b = [s.ps(f"ps_b{i}", [2 * N, 2, 512]) for i in range(2)]
        x_here, x_used = s.sem("x_here"), s.sem("x_used")
        a_full, a_read, b_full, b_read = s.sem("a_full"), s.sem("a_read"), s.sem("b_full"), s.sem("b_read")
        mag_done, ex_done, lg_done, hid_done, hiu_done = (s.sem(x) for x in ("mag_done", "ex_done", "lg_done", "hid_done", "hiu_done"))
        dm_done, co_done, sm_done, delta_done, du_done = (s.sem(x) for x in ("dm_done", "co_done", "sm_done", "delta_done", "du_done"))
        rd_done, midd_done, midu_done, ru_done, lo_done = (s.sem(x) for x in ("rd_done", "midd_done", "midu_done", "ru_done", "lo_done"))
        parts_out = [s.sem("parts_out0"), s.sem("parts_out1")]
        bc_out = [s.sem("bc_out0"), s.sem("bc_out1")]
        block = ctx.enter_context(nc.Block())
        HU = STEPS // 2

        @block.sync
        def _(sp):
            with sp.Fori(0, U) as u:
                for st in range(STEPS):
                    sp.wait_ge(b_read, u * STEPS + st + 1 + 2)
                    sp.dma_start(P["bc"][u, st], bc[st % 2][:, :]).then_inc(bc_out[st % 2], 16)
                    sp.wait_ge(lo_done, u * (2 * STEPS) + 2 * st + 2)
                    sp.dma_start(P["parts"][u, st].rearrange("a p t l -> p a (t l)"),
                                 parts[st % 2][:, :, :, :].rearrange("p a t l -> p a (t l)")).then_inc(parts_out[st % 2], 16)
            for k in range(2):
                sp.wait_ge(parts_out[k], 16 * U * HU + 16)
                sp.wait_ge(bc_out[k], 16 * U * HU + 16)

        @block.tensor
        def _(pe):
            with pe.Fori(0, U) as u:
                pe.wait_ge(x_here, u + 1)
                for st in range(STEPS):
                    k, c = divmod(st, NCH)
                    pe.wait_ge(a_read, u * STEPS + st + 1)
                    for h in range(2):
                        v = scan_order(xu[:, :], k, c * WC + h * HW_, HW_)
                        mm = pe.matmul(like(ps_a[st % 2][:, h, 0:HW_], v), keep["w_eff"][:, k, :], v, start=True, stop=True)
                    mm.then_inc(a_full, 1)
                    pe.wait_ge(b_read, u * STEPS + st + 1)
                    for h in range(2):
                        v = scan_order(xu[:, :], k, c * WC + h * HW_, HW_)
                        mm = pe.matmul(like(ps_b[st % 2][:, h, 0:HW_], v), keep["w_bc"][:, k, :], v, start=True, stop=True)
                    mm.then_inc(b_full, 1)

        @block.scalar
        def _(act):
            act.sem_inc(a_read, 2)
            act.sem_inc(b_read, 2)
            for k in range(2):
                act.sem_inc(parts_out[k], 16)
                act.sem_inc(bc_out[k], 16)

            def highs(u, st):
                act.wait_ge(parts_out[st % 2], u * (16 * HU) + 16 * (st // 2) + 16)
                act.wait_ge(delta_done, u * STEPS + st + 1)
                act.activation(parts[st % 2][:, 0, 0, :], delta[st % 2][:, :], ACT.Copy).then_inc(hid_done, 1)
                act.wait_ge(du_done, u * STEPS + st + 1)
                act.activation(parts[st % 2][:, 0, 1, :], du[st % 2][:, :], ACT.Copy).then_inc(hiu_done, 1)

            with act.Fori(0, U) as u:
                for st in range(STEPS):
                    k, i = st // NCH, st % 2
                    act.wait_ge(a_full, u * STEPS + st + 1)
                    halves = lambda x: x[:, :].rearrange("p (a b) -> p a b", a=2)
                    act.activation(halves(mag[i]), ps_a[i][:, :, 0:HW_], ACT.Abs, bias=keep["dt_b"][:, k:k + 1]).then_inc(mag_done, 1)
                    act.activation(halves(pos[i]), ps_a[i][:, :, 0:HW_], ACT.Relu, bias=keep["dt_b"][:, k:k + 1]).then_inc(a_read, 1)
                    act.wait_ge(mag_done, u * STEPS + st + 1)
                    act.activation(ex[i][:, :], mag[i][:, :], ACT.Exp, scale=-1.0).then_inc(ex_done, 1)
                    act.wait_ge(b_full, u * STEPS + st + 1)
                    act.wait_ge(bc_out[i], u * (16 * HU) + 16 * (st // 2) + 16)
                    act.activation(halves(bc[i]), ps_b[i][:, :, 0:HW_], ACT.Copy).then_inc(b_read, 1)
                    if st:
                        highs(u, st - 1)
                    act.wait_ge(dm_done, u * STEPS + st + 1)
                    act.activation(lg[i][:, :], dm[i][:, :], ACT.Ln, bias=1.0).then_inc(lg_done, 1)
                highs(u, STEPS - 1)

        @block.vector
        def _(dve):
            def rest_d(u, st):
                i = st % 2
                dve.wait_ge(hid_done, u * STEPS + st + 1)
                dve.tensor_tensor(rd[i][:, :], delta[i][:, :], parts[i][:, 0, 0, :], ALU.subtract).then_inc(rd_done, 1)

            def mid_d(u, st):
                i = st % 2
                dve.wait_ge(rd_done, u * STEPS + st + 1)
                dve.tensor_copy(parts[i][:, 1, 0, :], rd[i][:, :]).then_inc(midd_done, 1)

            def mid_u(u, st):
                i = st % 2
                dve.wait_ge(ru_done, u * STEPS + st + 1)
                dve.tensor_copy(parts[i][:, 1, 1, :], ru[i][:, :]).then_inc(midu_done, 1)

            with dve.Fori(0, U) as u:
                dve.wait_ge(a_read, u * STEPS + 2)
                dve.wait_ge(b_read, u * STEPS + 2)
                dve.tensor_copy(xu[:, :], xs[:, bass.ds(u * L, L)]).then_inc(x_here, 1)
                for st in range(STEPS):
                    k, c, i = st // NCH, st % NCH, st % 2
                    dve.wait_ge(ex_done, u * STEPS + st + 1)
                    dve.tensor_scalar(dm[i][:, :], ex[i][:, :], 1.0, -1.0, ALU.add, ALU.add).then_inc(dm_done, 1)
                    if st:
                        rest_d(u, st - 1)
                    dve.wait_ge(dm_done, u * STEPS + st + 1)
                    dve.tensor_tensor(co[i][:, :], ex[i][:, :], dm[i][:, :], ALU.subtract).then_inc(co_done, 1)
                    if st:
                        mid_d(u, st - 1)
                    dve.wait_ge(co_done, u * STEPS + st + 1)
                    dve.wait_ge(lg_done, u * STEPS + st + 1)
                    dve.tensor_tensor(sm[i][:, :], co[i][:, :], lg[i][:, :], ALU.add).then_inc(sm_done, 1)
                    if st:
                        mid_u(u, st - 1)
                    dve.wait_ge(sm_done, u * STEPS + st + 1)
                    dve.tensor_tensor(delta[i][:, :], sm[i][:, :], pos[i][:, :], ALU.add).then_inc(delta_done, 1)
                    v = scan_order(xu[:, :], k, c * WC, WC)
                    dve.wait_ge(delta_done, u * STEPS + st + 1)
                    dve.tensor_tensor(like(du[i][:, :], v), like(delta[i][:, :], v), v, ALU.mult).then_inc(du_done, 1)
                rest_d(u, STEPS - 1)
                mid_d(u, STEPS - 1)
                mid_u(u, STEPS - 1)

        @block.gpsimd
        def _(pool):
            with pool.Fori(0, U) as u:
                for st in range(STEPS):
                    i = st % 2
                    pool.wait_ge(hiu_done, u * STEPS + st + 1)
                    pool.tensor_tensor(ru[i][:, :], du[i][:, :], parts[i][:, 0, 1, :], ALU.subtract).then_inc(ru_done, 1)
                    pool.wait_ge(midd_done, u * STEPS + st + 1)
                    pool.tensor_tensor(parts[i][:, 2, 0, :], rd[i][:, :], parts[i][:, 1, 0, :], ALU.subtract).then_inc(lo_done, 1)
                    pool.wait_ge(midu_done, u * STEPS + st + 1)
                    pool.tensor_tensor(parts[i][:, 2, 1, :], ru[i][:, :], parts[i][:, 1, 1, :], ALU.subtract).then_inc(lo_done, 1)


def scan_phase(nc, P, keep):
    with ExitStack() as ctx:
        s = Space(nc, ctx, "scan")
        stack = [s.sb(f"stack{i}", [96, 4, 2, WC], BF16) for i in range(2)]
        b_rep = [s.sb(f"b_rep{i}", [128, WC]) for i in range(2)]
        c_rep = [s.sb(f"c_rep{i}", [128, WC]) for i in range(2)]
        rec = [s.sb(f"rec{i}", [128, G + 1]) for i in range(2)]
        bu = [s.sb(f"bu{i}", [128, WC]) for i in range(4)]
        h = [s.sb(f"h{i}", [128, WC]) for i in range(4)]
        hc = [s.sb(f"hc{i}", [128, WC]) for i in range(4)]
        y = [s.sb(f"y{i}", [128, WC]) for i in range(2)]
        h_last = s.sb("h_last", [128, G])
        ps_d = [s.ps(f"ps_d{i}", [128, 1024]) for i in range(2)]
        ps_u = s.ps("ps_u", [128, 1024])
        ps_y = s.ps("ps_y", [128, 1024])
        came = [s.sem(f"came{i}") for i in range(2)]
        y_out = [s.sem(f"y_out{i}") for i in range(2)]
        u_full, d_full, bu_done, exp_done, scan_done, hc_done, y_full, y_read, zeroed = (
            s.sem(x) for x in ("u_full", "d_full", "bu_done", "exp_done", "scan_done", "hc_done", "y_full", "y_read", "zeroed"))
        LOADS = 3 + 2 * J + 1
        TB = 2 * G
        NI = NKC // 2
        pieces = [(0, 512), (512, WC)]
        block = ctx.enter_context(nc.Block())
        recs = P["rec"].rearrange("u s p f -> (u s) p f")
        partsd = P["parts"].rearrange("u s a (q i) t l -> (u s) a i q t l", q=4)
        bcd = P["bc"].rearrange("u s n l -> (u s) n l")
        yd = P["y"].rearrange("u s p l -> (u s) p l")

        @block.sync
        def _(sp):
            for k in range(2):
                sp.sem_inc(y_out[k], 16)

            def store(i, cc):
                sp.wait_ge(y_read, i * 2 + (cc - 1))
                sp.dma_start(yd[i * 2 + (cc - 2)], y[cc % 2][:, :]).then_inc(y_out[cc % 2], 16)

            def step(i, first):
                for cc in range(2):
                    if not first:
                        sp.wait_ge(hc_done, i * TB + G * (cc - 1) + 3)
                    for a in range(3):
                        sp.dma_start(stack[cc][32 * a:32 * a + 32, :, :, :].rearrange("p q t l -> p q (t l)"),
                                     partsd[i * 2 + cc, a].rearrange("i q t l -> i q (t l)")).then_inc(came[cc], 16)
                    for j in range(J):
                        sp.dma_start(b_rep[cc][N * j:N * j + N, :], bcd[i * 2 + cc, 0:N]).then_inc(came[cc], 16)
                    for j in range(J):
                        sp.dma_start(c_rep[cc][N * j:N * j + N, :], bcd[i * 2 + cc, N:2 * N]).then_inc(came[cc], 16)
                    sp.dma_start(rec[cc][:, :], recs[i * 2 + cc]).then_inc(came[cc], 16)
                    if not first:
                        store(i, cc)

            step(0, True)
            with sp.Fori(1, NI) as i:
                step(i, False)
            store(NI, 0)
            store(NI, 1)
            for k in range(2):
                sp.wait_ge(y_out[k], 16 * NI + 16)

        @block.tensor
        def _(pe):
            def spread(dst, cc, g, which):
                for lo, hi in pieces:
                    mm = pe.matmul(dst[:, lo:hi], keep["parts_sel"][:, g % 4, :, :].rearrange("p j n -> p (j n)"),
                                   stack[cc][:, g // 4, which, lo:hi], start=True, stop=True)
                return mm

            def sum_states(i, t):
                g, cc = t % G, (t % TB) // G
                pe.wait_ge(hc_done, i * TB + t + 1)
                if g == 0:
                    pe.wait_ge(y_read, i * 2 + t // G)
                for lo, hi in pieces:
                    mm = pe.matmul(ps_y[:, lo:hi], keep["sum_sel"][:, D - J - J * g:2 * D - J - J * g],
                                   hc[t % 4][:, lo:hi],
                                   start=g == 0, stop=g == G - 1)
                if g == G - 1:
                    mm.then_inc(y_full, 1)

            def step(i, first):
                for t in range(TB):
                    cc, g = divmod(t, G)
                    if g == 0:
                        pe.wait_ge(came[cc], i * (16 * LOADS) + 16 * LOADS)
                    if t or not first:
                        pe.wait_ge(bu_done, i * TB + t)
                    spread(ps_u, cc, g, 1).then_inc(u_full, 1)
                    if t >= 3 or not first:
                        sum_states(i, t - 3)
                    if t >= 2 or not first:
                        pe.wait_ge(scan_done, i * TB + t - 1)
                    spread(ps_d[t % 2], cc, g, 0).then_inc(d_full, 1)

            step(0, True)
            with pe.Fori(1, NI) as i:
                step(i, False)
            for t in range(-3, 0):
                sum_states(NI, t)

        @block.scalar
        def _(act):
            def read_y(i, cc):
                act.wait_ge(y_full, i * 2 + cc)
                act.wait_ge(y_out[(cc + 1) % 2], i * 16 + 16 * ((cc + 1) // 2))
                act.activation(y[(cc + 1) % 2][:, :], ps_y[:, 0:WC], ACT.Copy).then_inc(y_read, 1)

            def step(i, first):
                for t in range(TB):
                    cc, g = divmod(t, G)
                    if g == 0:
                        act.wait_ge(came[cc], i * (16 * LOADS) + 16 * LOADS)
                    act.wait_ge(d_full, i * TB + t + 1)
                    act.activation(ps_d[t % 2][:, 0:WC], ps_d[t % 2][:, 0:WC], ACT.Exp, scale=rec[cc][:, g:g + 1]).then_inc(exp_done, 1)
                    if t >= 2 or not first:
                        b = (t - 2) % TB
                        act.activation(h_last[:, b % G:b % G + 1], h[b % 4][:, WC - 1:WC], ACT.Copy,
                                       scale=rec[b // G][:, G:G + 1]).then_inc(zeroed, 1)
                    if g == 2 and (cc or not first):
                        read_y(i, cc)

            step(0, True)
            with act.Fori(1, NI) as i:
                step(i, False)
            read_y(NI, 0)

        @block.vector
        def _(dve):
            def scan(i, t):
                b = t % TB
                dve.wait_ge(exp_done, i * TB + t + 1)
                dve.tensor_tensor_scan(h[b % 4][:, :], ps_d[b % 2][:, 0:WC], bu[b % 4][:, :], h_last[:, b % G:b % G + 1],
                                       ALU.mult, ALU.add).then_inc(scan_done, 1)

            def step(i, first):
                for t in range(TB):
                    cc, g = divmod(t, G)
                    if g == 0:
                        dve.wait_ge(came[cc], i * (16 * LOADS) + 16 * LOADS)
                    dve.wait_ge(u_full, i * TB + t + 1)
                    dve.tensor_tensor(bu[t % 4][:, :], ps_u[:, 0:WC], b_rep[cc][:, :], ALU.mult).then_inc(bu_done, 1)
                    if t or not first:
                        scan(i, t - 1)

            dve.memset(h_last[:, :], 0.0).then_inc(zeroed, 1)
            dve.wait_ge(zeroed, 1)
            step(0, True)
            with dve.Fori(1, NI) as i:
                step(i, False)
            dve.wait_ge(bu_done, NI * TB)
            scan(NI, -1)

        @block.gpsimd
        def _(pool):
            with pool.Fori(0, NI) as i:
                for t in range(TB):
                    cc, g = divmod(t, G)
                    if g == 0:
                        pool.wait_ge(came[cc], i * (16 * LOADS) + 16 * LOADS)
                    pool.wait_ge(scan_done, i * TB + t + 1)
                    pool.tensor_tensor(hc[t % 4][:, :], h[t % 4][:, :], c_rep[cc][:, :], ALU.mult).then_inc(hc_done, 1)


def merge_phase(nc, P, keep, xs):
    LN = 3
    LAST = 14
    with ExitStack() as ctx:
        s = Space(nc, ctx, "merge")
        y4 = s.sb("y4", [128, 2, K, L])
        xn = s.sb("xn", [DM, 2, L])
        lane = lambda name, p=128: [s.sb(f"{name}{i}", [p, TT]) for i in range(LN)]
        a, b, yy, yc, sq, sd = (lane(n) for n in ("a", "b", "yy", "yc", "sq", "sd"))
        rs, ya, z = sd, sq, yc
        ps_s = [s.ps(f"ps_s{i}", [128, 512]) for i in range(LN)]
        ps_z = [s.ps(f"ps_z{i}", [128, 512]) for i in range(LN)]
        came = [s.sem(f"came{i}") for i in range(2)]
        link = [s.sem(f"link{i}") for i in range(LN)]
        gone = [s.sem(f"gone{i}") for i in range(LN)]
        TL = TPI // LN
        PU = TL * LAST
        block = ctx.enter_context(nc.Block())
        yd = P["y"].rearrange("u (k c) p l -> u k p c l", k=K)
        xnd = P["xn"].rearrange("b (r c) l -> (b r) c l", r=BR)
        zd = P["z"].rearrange("b (r c) l -> (b r) c l", r=BR)

        @block.sync
        def _(sp):
            for ln in range(LN):
                sp.sem_inc(link[ln], PU + 1)
                sp.sem_inc(gone[ln], 16)
            with sp.Fori(0, U // 2) as i:
                for k in range(2):
                    for ln in range(LN):
                        sp.wait_ge(link[ln], i * (2 * PU) + k * PU + 1)
                    for d in range(K):
                        sp.dma_start(y4[:, k, d, :].rearrange("p (c l) -> p c l", c=NCH), yd[i * 2 + k, d]).then_inc(came[k], 16)
                    sp.dma_start(xn[:, k, :], xnd[i * 2 + k]).then_inc(came[k], 16)

        @block.gpsimd
        def _(pool):
            with pool.Fori(0, U // 2) as i:
                for k in range(2):
                    pool.wait_ge(came[k], i * (16 * (K + 1)) + 16 * (K + 1))
                    for t in range(TPI):
                        ln, n = t % LN, k * PU + (t // LN) * LAST + PU + 1
                        pool.wait_ge(link[ln], i * (2 * PU) + n)
                        v1 = scan_order(y4[:, k, 1, :], 1, t * TT, TT)
                        v3 = scan_order(y4[:, k, 3, :], 3, t * TT, TT)
                        pool.tensor_tensor(like(b[ln][:, :], v1), v1, v3, ALU.add).then_inc(link[ln], 1)

        @block.vector
        def _(dve):
            with dve.Fori(0, U // 2) as i:
                for k in range(2):
                    dve.wait_ge(came[k], i * (16 * (K + 1)) + 16 * (K + 1))
                    for g in range(TL):
                        base = i * (2 * PU) + (k * PU + g * LAST + PU + 1)
                        for ln in range(LN):
                            at = (g * LN + ln) * TT
                            dve.wait_ge(link[ln], base + 1)
                            dve.tensor_tensor(a[ln][:, :], y4[:, k, 0, at:at + TT], scan_order(y4[:, k, 2, :], 2, at, TT), ALU.add).then_inc(link[ln], 1)
                        for ln in range(LN):
                            at = (g * LN + ln) * TT
                            dve.wait_ge(link[ln], base + 2)
                            dve.scalar_tensor_tensor(yy[ln][:, :], xs[:, bass.ds(i * (2 * L) + (k * L + at), TT)], keep["d_sum"][:, 0:1],
                                                     a[ln][:, :], ALU.mult, ALU.add).then_inc(link[ln], 1)
                        for ln in range(LN):
                            dve.wait_ge(link[ln], base + 3)
                            dve.tensor_tensor(a[ln][:, :], yy[ln][:, :], b[ln][:, :], ALU.add).then_inc(link[ln], 1)
                        for ln in range(LN):
                            dve.wait_ge(link[ln], base + 5)
                            dve.wait_ge(gone[ln], i * (32 * TL) + 16 * (k * TL + g) + 16)
                            dve.tensor_tensor(yc[ln][:, :], a[ln][:, :], ps_s[ln][:, 0:TT], ALU.subtract).then_inc(link[ln], 1)
                        for ln in range(LN):
                            dve.wait_ge(link[ln], base + 10)
                            dve.tensor_tensor(yy[ln][:, :], yc[ln][:, :], rs[ln][:, :], ALU.mult).then_inc(link[ln], 1)
                        for ln in range(LN):
                            at = (g * LN + ln) * TT
                            dve.wait_ge(link[ln], base + 13)
                            dve.scalar_tensor_tensor(z[ln][0:DM, :], xn[:, k, at:at + TT], keep["skip"][:, 0:1], ps_z[ln][0:DM, 0:TT],
                                                     ALU.mult, ALU.add).then_inc(link[ln], 1)

        @block.tensor
        def _(pe):
            with pe.Fori(0, U // 2) as i:
                for k in range(2):
                    for g in range(TL):
                        base = i * (2 * PU) + (k * PU + g * LAST + PU + 1)
                        for ln in range(LN):
                            pe.wait_ge(link[ln], base + 4)
                            pe.matmul(ps_s[ln][:, 0:TT], keep["ones_d"][:, :], a[ln][:, :], start=True, stop=True).then_inc(link[ln], 1)
                        for ln in range(LN):
                            pe.wait_ge(link[ln], base + 7)
                            pe.matmul(ps_s[ln][:, 0:TT], keep["ones_d"][:, :], sq[ln][:, :], start=True, stop=True).then_inc(link[ln], 1)
                        for ln in range(LN):
                            pe.wait_ge(link[ln], base + 12)
                            pe.matmul(ps_z[ln][0:DM, 0:TT], keep["out_W"][:, :], ya[ln][:, :], start=True, stop=True).then_inc(link[ln], 1)

        @block.scalar
        def _(act):
            with act.Fori(0, U // 2) as i:
                for k in range(2):
                    for g in range(TL):
                        base = i * (2 * PU) + (k * PU + g * LAST + PU + 1)
                        for ln in range(LN):
                            act.wait_ge(link[ln], base + 6)
                            act.activation(sq[ln][:, :], yc[ln][:, :], ACT.Square).then_inc(link[ln], 1)
                        for ln in range(LN):
                            act.wait_ge(link[ln], base + 8)
                            act.activation(sd[ln][:, :], ps_s[ln][:, 0:TT], ACT.Ln, bias=keep["eps"][:, 0:1]).then_inc(link[ln], 1)
                        for ln in range(LN):
                            act.wait_ge(link[ln], base + 9)
                            act.activation(rs[ln][:, :], sd[ln][:, :], ACT.Exp, scale=-0.5).then_inc(link[ln], 1)
                        for ln in range(LN):
                            act.wait_ge(link[ln], base + 11)
                            act.activation(ya[ln][:, :], yy[ln][:, :], ACT.Identity, scale=keep["onorm_g"][:, 0:1],
                                           bias=keep["onorm_b"][:, 0:1]).then_inc(link[ln], 1)
                        for ln in range(LN):
                            act.wait_ge(link[ln], base + 14)
                            act.dma_start(zd[i * 2 + k, :, (g * LN + ln) * TT:(g * LN + ln + 1) * TT], z[ln][0:DM, :]).then_inc(gone[ln], 16)
            for ln in range(LN):
                act.wait_ge(gone[ln], 16 * U * TL + 16)


def project_phase(nc, P, keep, x1, f_t):
    LN = 2
    LAST = 15
    with ExitStack() as ctx:
        s = Space(nc, ctx, "proj")
        zn = s.sb("zn", [128, LN, 2, TT])
        xc, sq, xh = (s.sb(n, [128, LN, 2, TT]) for n in ("xc", "sq", "xh"))
        sd, rs, ln2, lm, inv = (s.sb(n, [128, LN, TT]) for n in ("sd", "rs", "ln2", "lm", "inv"))
        ps_x = s.ps("ps_x", [128, LN, 2, 512])
        ps_s = s.ps("ps_s", [128, LN, 512])
        came = [s.sem(f"came{i}") for i in range(LN)]
        link = [s.sem(f"link{i}") for i in range(LN)]
        block = ctx.enter_context(nc.Block())
        zv = P["zn"].rearrange("b (h p) (i t) -> b i p h t", h=2, t=TT)
        at = lambda x, i, ln: x[:, :, bass.ds(i * (LN * TT) + ln * TT, TT)]
        both = lambda x: x.unsqueeze(1).to_broadcast([128, 2, TT])

        @block.sync
        def _(sp):
            for ln in range(LN):
                sp.sem_inc(link[ln], 1)
            with sp.Fori(0, B) as b:
                with sp.Fori(0, TPI // LN) as i:
                    for ln in range(LN):
                        sp.wait_ge(link[ln], b * (LAST * TPI // LN) + i * LAST + 1)
                        sp.dma_start(zn[:, ln, :, :], zv[b, i * LN + ln]).then_inc(came[ln], 16)

        @block.tensor
        def _(pe):
            with pe.Fori(0, NTT // LN) as i:
                for ln in range(LN):
                    pe.wait_ge(came[ln], i * 16 + 16)
                    for o in range(2):
                        for h in range(2):
                            mm = pe.matmul(ps_x[:, ln, o, 0:TT], keep["proj_W"][:, h, o * 128:o * 128 + 128], zn[:, ln, h, :],
                                           start=h == 0, stop=h == 1)
                    mm.then_inc(link[ln], 1)
                for ln in range(LN):
                    pe.wait_ge(link[ln], i * LAST + 3)
                    for h in range(2):
                        mm = pe.matmul(ps_s[:, ln, 0:TT], keep["ones_c"][:, :], at(x1, i, ln)[:, h, :], start=h == 0, stop=h == 1)
                    mm.then_inc(link[ln], 1)
                for ln in range(LN):
                    pe.wait_ge(link[ln], i * LAST + 6)
                    for h in range(2):
                        mm = pe.matmul(ps_s[:, ln, 0:TT], keep["ones_c"][:, :], sq[:, ln, h, :], start=h == 0, stop=h == 1)
                    mm.then_inc(link[ln], 1)
                for ln in range(LN):
                    pe.wait_ge(link[ln], i * LAST + 11)
                    for h in range(2):
                        mm = pe.matmul(ps_s[:, ln, 0:TT], keep["ones"][:, :], sq[:, ln, h, :], start=h == 0, stop=h == 1)
                    mm.then_inc(link[ln], 1)

        @block.scalar
        def _(act):
            with act.Fori(0, NTT // LN) as i:
                for ln in range(LN):
                    act.wait_ge(link[ln], i * LAST + 2)
                    for h in range(2):
                        last = act.activation(at(x1, i, ln)[:, h, :], ps_x[:, ln, h, 0:TT], ACT.Identity, bias=keep["proj_b"][:, h:h + 1])
                    last.then_inc(link[ln], 1)
                for ln in range(LN):
                    act.wait_ge(link[ln], i * LAST + 5)
                    act.activation(sq[:, ln, :, :], xc[:, ln, :, :], ACT.Square).then_inc(link[ln], 1)
                for ln in range(LN):
                    act.wait_ge(link[ln], i * LAST + 7)
                    act.activation(sd[:, ln, :], ps_s[:, ln, 0:TT], ACT.Ln, bias=keep["eps"][:, 0:1]).then_inc(link[ln], 1)
                for ln in range(LN):
                    act.wait_ge(link[ln], i * LAST + 8)
                    act.activation(rs[:, ln, :], sd[:, ln, :], ACT.Exp, scale=-0.5).then_inc(link[ln], 1)
                for ln in range(LN):
                    act.wait_ge(link[ln], i * LAST + 10)
                    act.activation(sq[:, ln, :, :], xh[:, ln, :, :], ACT.Square).then_inc(link[ln], 1)
                for ln in range(LN):
                    act.wait_ge(link[ln], i * LAST + 13)
                    act.activation(ln2[:, ln, :], lm[:, ln, :], ACT.Ln, scale=2.0 ** 40).then_inc(link[ln], 1)
                for ln in range(LN):
                    act.wait_ge(link[ln], i * LAST + 14)
                    act.activation(inv[:, ln, :], ln2[:, ln, :], ACT.Exp, scale=-0.5, bias=keep["ln_2_20"][:, 0:1]).then_inc(link[ln], 1)

        @block.vector
        def _(dve):
            with dve.Fori(0, NTT // LN) as i:
                for ln in range(LN):
                    dve.wait_ge(link[ln], i * LAST + 4)
                    dve.tensor_tensor(xc[:, ln, :, :], at(x1, i, ln), both(ps_s[:, ln, 0:TT]), ALU.subtract).then_inc(link[ln], 1)
                for ln in range(LN):
                    dve.wait_ge(link[ln], i * LAST + 9)
                    dve.tensor_tensor(xh[:, ln, :, :], xc[:, ln, :, :], both(rs[:, ln, :]), ALU.mult).then_inc(link[ln], 1)
                for ln in range(LN):
                    dve.wait_ge(link[ln], i * LAST + 12)
                    dve.tensor_scalar(lm[:, ln, :], ps_s[:, ln, 0:TT], 1e-24, None, ALU.max).then_inc(link[ln], 1)
                for ln in range(LN):
                    dve.wait_ge(link[ln], i * LAST + 15)
                    dve.tensor_tensor(at(f_t, i, ln), xh[:, ln, :, :], both(inv[:, ln, :]), ALU.mult).then_inc(link[ln], 1)


def attention_phase(nc, keep, f_t, o_t, den):
    with ExitStack() as ctx:
        s = Space(nc, ctx, "attn")
        f_tok = s.sb("f_tok", [128, KB, C])
        e = [s.sb(f"e{i}", [128, TT]) for i in range(4)]
        ps_s = [s.ps(f"ps_s{i}", [128, 512]) for i in range(4)]
        ps_o = s.ps("ps_o", [128, 2, 512])
        turned, moved = s.sem("turned"), s.sem("moved")
        s_full, e_done, o_full, o_read = s.sem("s_full"), s.sem("e_done"), s.sem("o_full"), s.sem("o_read")
        block = ctx.enter_context(nc.Block())

        @block.tensor
        def _(pe):
            for n in range(KB // 2):
                if n >= 4:
                    pe.wait_ge(moved, n - 3)
                for q in range(4):
                    j, h = 2 * n + q // 2, q % 2
                    mm = pe.transpose(ps_s[n % 4][:, q * 128:q * 128 + 128], f_t[:, h, j * 128:j * 128 + 128], keep["ident"][:, :])
                mm.then_inc(turned, 1)
            pe.wait_ge(moved, KB // 2)

            def scores(q, j):
                for h in range(2):
                    mm = pe.matmul(ps_s[j % 4][:, 0:TT], f_t[:, h, j * 128:j * 128 + 128], f_t[:, h, bass.ds(q * TT, TT)],
                                   start=h == 0, stop=h == 1)
                mm.then_inc(s_full, 1)

            pe.sem_inc(o_read, 1)
            with pe.Fori(0, NTT) as q:
                scores(q, 0)
                scores(q, 1)
                for j in range(KB):
                    if j + 2 < KB:
                        scores(q, j + 2)
                    if j == 0:
                        pe.wait_ge(o_read, q + 1)
                    pe.wait_ge(e_done, q * KB + j + 1)
                    for o in range(2):
                        mm = pe.matmul(ps_o[:, o, 0:TT], f_tok[:, j, o * 128:o * 128 + 128], e[j % 4][:, :],
                                       start=j == 0, stop=j == KB - 1)
                mm.then_inc(o_full, 1)

        @block.scalar
        def _(act):
            with act.Fori(0, NTT) as q:
                for j in range(KB):
                    act.wait_ge(s_full, q * KB + j + 1)
                    act.activation(e[j % 4][:, :], ps_s[j % 4][:, 0:TT], ACT.Exp,
                                   accum_out=den[:, j, bass.ds(q, 1)]).then_inc(e_done, 1)

        @block.vector
        def _(dve):
            for n in range(KB // 2):
                dve.wait_ge(turned, n + 1)
                dve.tensor_copy(f_tok[:, 2 * n:2 * n + 2, :].rearrange("p a c -> p (a c)"), ps_s[n % 4][:, :]).then_inc(moved, 1)
            with dve.Fori(0, NTT) as q:
                dve.wait_ge(o_full, q + 1)
                dve.tensor_copy(o_t[:, :, bass.ds(q * TT, TT)], ps_o[:, :, 0:TT]).then_inc(o_read, 1)


def blend_phase(nc, keep, x1, f_t, o_t, den):
    LN = 2
    LAST = 18
    with ExitStack() as ctx:
        s = Space(nc, ctx, "blend")
        den_sum, den_inv, den_w = (s.sb(n, [128, KB]) for n in ("den_sum", "den_inv", "den_w"))
        dg = s.sb("dg", [128, LN, TT // 128, 128])
        aa, mm_, sq, xc = (s.sb(n, [128, LN, 2, TT]) for n in ("aa", "mm_", "sq", "xc"))
        ln2, lm, inv, sd, rs = (s.sb(n, [128, LN, TT]) for n in ("ln2", "lm", "inv", "sd", "rs"))
        ps_b = s.ps("ps_b", [128, LN, 512])
        ps_s = s.ps("ps_s", [128, LN, 512])
        summed = s.sem("summed")
        link = [s.sem(f"link{i}") for i in range(LN)]
        block = ctx.enter_context(nc.Block())
        at = lambda x, i, ln: x[:, :, bass.ds(i * (LN * TT) + ln * TT, TT)]
        both = lambda x: x.unsqueeze(1).to_broadcast([128, 2, TT])
        BL = TT // 128

        @block.vector
        def _(dve):
            dve.tensor_reduce(den_sum[:, :], den[:, :, :], AX.X, ALU.add).then_inc(summed, 1)
            dve.wait_ge(summed, 1)
            dve.reciprocal(den_inv[:, :], den_sum[:, :]).then_inc(summed, 1)
            dve.wait_ge(summed, 2)
            dve.tensor_scalar(den_w[:, :], den_inv[:, :], 1.0 - 0.8, None, ALU.mult).then_inc(summed, 1)
            dve.wait_ge(summed, 3)
            for ln in range(LN):
                dve.sem_inc(link[ln], 1)
            with dve.Fori(0, NTT // LN) as i:
                for ln in range(LN):
                    dve.wait_ge(link[ln], i * LAST + 1)
                    w = den_w[:, bass.ds(i * (LN * BL) + ln * BL, BL)].unsqueeze(2).to_broadcast([128, BL, 128])
                    eye = keep["ident"][:, :].unsqueeze(1).to_broadcast([128, BL, 128])
                    dve.tensor_tensor(dg[:, ln, :, :], eye, w, ALU.mult).then_inc(link[ln], 1)
                for ln in range(LN):
                    dve.wait_ge(link[ln], i * LAST + 3)
                    dve.tensor_tensor(aa[:, ln, :, :], at(o_t, i, ln), both(ps_b[:, ln, 0:TT]), ALU.mult).then_inc(link[ln], 1)
                for ln in range(LN):
                    dve.wait_ge(link[ln], i * LAST + 4)
                    dve.scalar_tensor_tensor(mm_[:, ln, :, :], at(f_t, i, ln), 0.8, aa[:, ln, :, :], ALU.mult, ALU.add).then_inc(link[ln], 1)
                for ln in range(LN):
                    dve.wait_ge(link[ln], i * LAST + 7)
                    dve.tensor_scalar(lm[:, ln, :], ps_s[:, ln, 0:TT], 1e-24, None, ALU.max).then_inc(link[ln], 1)
                for ln in range(LN):
                    dve.wait_ge(link[ln], i * LAST + 10)
                    dve.tensor_tensor(aa[:, ln, :, :], mm_[:, ln, :, :], both(inv[:, ln, :]), ALU.mult).then_inc(link[ln], 1)
                for ln in range(LN):
                    dve.wait_ge(link[ln], i * LAST + 11)
                    dve.tensor_tensor(at(x1, i, ln), at(x1, i, ln), aa[:, ln, :, :], ALU.add).then_inc(link[ln], 1)
                for ln in range(LN):
                    dve.wait_ge(link[ln], i * LAST + 13)
                    dve.tensor_tensor(xc[:, ln, :, :], at(x1, i, ln), both(ps_s[:, ln, 0:TT]), ALU.subtract).then_inc(link[ln], 1)
                for ln in range(LN):
                    dve.wait_ge(link[ln], i * LAST + 18)
                    dve.tensor_tensor(at(o_t, i, ln), xc[:, ln, :, :], both(rs[:, ln, :]), ALU.mult).then_inc(link[ln], 1)

        @block.tensor
        def _(pe):
            with pe.Fori(0, NTT // LN) as i:
                for ln in range(LN):
                    pe.wait_ge(link[ln], i * LAST + 2)
                    pe.matmul(ps_b[:, ln, 0:TT], keep["ones"][:, :], dg[:, ln, :, :].rearrange("p a b -> p (a b)"),
                              start=True, stop=True).then_inc(link[ln], 1)
                for ln in range(LN):
                    pe.wait_ge(link[ln], i * LAST + 6)
                    for h in range(2):
                        mm = pe.matmul(ps_s[:, ln, 0:TT], keep["ones"][:, :], sq[:, ln, h, :], start=h == 0, stop=h == 1)
                    mm.then_inc(link[ln], 1)
                for ln in range(LN):
                    pe.wait_ge(link[ln], i * LAST + 12)
                    for h in range(2):
                        mm = pe.matmul(ps_s[:, ln, 0:TT], keep["ones_c"][:, :], at(x1, i, ln)[:, h, :], start=h == 0, stop=h == 1)
                    mm.then_inc(link[ln], 1)
                for ln in range(LN):
                    pe.wait_ge(link[ln], i * LAST + 15)
                    for h in range(2):
                        mm = pe.matmul(ps_s[:, ln, 0:TT], keep["ones_c"][:, :], sq[:, ln, h, :], start=h == 0, stop=h == 1)
                    mm.then_inc(link[ln], 1)

        @block.scalar
        def _(act):
            with act.Fori(0, NTT // LN) as i:
                for ln in range(LN):
                    act.wait_ge(link[ln], i * LAST + 5)
                    act.activation(sq[:, ln, :, :], mm_[:, ln, :, :], ACT.Square).then_inc(link[ln], 1)
                for ln in range(LN):
                    act.wait_ge(link[ln], i * LAST + 8)
                    act.activation(ln2[:, ln, :], lm[:, ln, :], ACT.Ln, scale=2.0 ** 40).then_inc(link[ln], 1)
                for ln in range(LN):
                    act.wait_ge(link[ln], i * LAST + 9)
                    act.activation(inv[:, ln, :], ln2[:, ln, :], ACT.Exp, scale=-0.5, bias=keep["ln_2_20"][:, 0:1]).then_inc(link[ln], 1)
                for ln in range(LN):
                    act.wait_ge(link[ln], i * LAST + 14)
                    act.activation(sq[:, ln, :, :], xc[:, ln, :, :], ACT.Square).then_inc(link[ln], 1)
                for ln in range(LN):
                    act.wait_ge(link[ln], i * LAST + 16)
                    act.activation(sd[:, ln, :], ps_s[:, ln, 0:TT], ACT.Ln, bias=keep["eps"][:, 0:1]).then_inc(link[ln], 1)
                for ln in range(LN):
                    act.wait_ge(link[ln], i * LAST + 17)
                    act.activation(rs[:, ln, :], sd[:, ln, :], ACT.Exp, scale=-0.5).then_inc(link[ln], 1)


def expert_phase(nc, w, keep, x1, xl, f_t, out):
    with ExitStack() as ctx:
        s = Space(nc, ctx, "moe")
        w1 = f_t[:, :, :].rearrange("p h t -> p (h t)")[:, 0:E * 2 * HF].rearrange("p (e h n) -> p e h n", e=E, h=2)
        w2 = s.sb("w2", [128, E, HB, C])
        b1 = s.sb("b1", [128, E, HB])
        b2 = s.sb("b2", [E, C])
        gw = s.sb("gw", [128, 2, E])
        gb = s.sb("gb", [128, E])
        cw_t = s.sb("cw_t", [E, NT])
        small = lambda name, n=E, dt=F32: s.sb(name, [128, KB, n], dt)
        lg, top, dif, ex, cw, cw2 = (small(n) for n in ("lg", "top", "dif", "ex", "cw", "cw2"))
        idx = small("idx", E, U32)
        dif2, ex2, v2, pick = (small(n, 2) for n in ("dif2", "ex2", "v2", "pick"))
        sm, inv = small("sm", 1), small("inv", 1)
        iota = s.sb("iota", [128, E])
        hg = [s.sb(f"hg{i}", [128, TT]) for i in range(3)]
        hw = [s.sb(f"hw{i}", [128, TT]) for i in range(3)]
        res = s.sb("res", [128, 2, 2, TT])
        ps_h = [s.ps(f"ps_h{i}", [128, 512]) for i in range(3)]
        ps_w = [s.ps(f"ps_w{i}", [128, 512]) for i in range(2)]
        ps_o = s.ps("ps_o", [128, 2, 512])
        ps_g = s.ps("ps_g", [128, 512])
        loaded, gate_full, step_done, ex_done = s.sem("loaded"), s.sem("gate_full"), s.sem("step_done"), s.sem("ex_done")
        iota_done, turned, moved = s.sem("iota_done"), s.sem("turned"), s.sem("moved")
        h_full, g_done, w_full, hw_done, o_full, o_read = (
            s.sem(n) for n in ("h_full", "g_done", "w_full", "hw_done", "o_full", "o_read"))
        gone = [s.sem(f"gone{k}") for k in range(2)]
        M = E * HB
        block = ctx.enter_context(nc.Block())
        wide = lambda x: x.to_broadcast([128, KB, E])

        @block.sync
        def _(sp):
            sp.dma_start(gw[:, :, :], w["gate_w"].rearrange("(h p) e -> p h e", h=2)).then_inc(loaded, 16)
            sp.dma_start(gb[:, :], w["gate_b"].partition_broadcast(128)).then_inc(loaded, 16)
            sp.dma_start(b2[:, :], w["b2"]).then_inc(loaded, 16)
            for e in range(E):
                sp.dma_start(w1[:, e, :, :], w["W1"][e].rearrange("(h p) n -> p h n", h=2)).then_inc(loaded, 16)
                sp.dma_start(w2[:, e, :, :], w["W2"][e].rearrange("(h p) n -> p h n", h=HB)).then_inc(loaded, 16)
                sp.dma_start(b1[:, e, :], w["b1"][e].rearrange("(h p) -> p h", h=HB), allow_slow_non_contiguous=True).then_inc(loaded, 16)
            ov = out.rearrange("b (h p) y x -> b p h (y x)", h=2)
            sp.sem_inc(o_read, 1)
            for k in range(2):
                sp.sem_inc(gone[k], 16)
            with sp.Fori(0, B) as b:
                with sp.Fori(0, TPI // 2) as i:
                    for k in range(2):
                        sp.wait_ge(o_read, b * TPI + i * 2 + k + 2)
                        sp.dma_start(ov[b, :, :, bass.ds(i * (2 * TT) + k * TT, TT)], res[:, k, :, :]).then_inc(gone[k], 16)
            for k in range(2):
                sp.wait_ge(gone[k], 8 * NTT + 16)

        @block.gpsimd
        def _(pool):
            for n in range(E):
                last = pool.memset(iota[:, n:n + 1], float(n))
            last.then_inc(iota_done, 1)

        @block.tensor
        def _(pe):
            pe.wait_ge(loaded, 16 * (3 + 3 * E))
            for j in range(KB):
                for h in range(2):
                    mm = pe.matmul(ps_g[:, j * E:j * E + E], xl[:, h, j * 128:j * 128 + 128], gw[:, h, :], start=h == 0, stop=h == 1)
            mm.then_inc(gate_full, 1)
            pe.wait_ge(step_done, 12)
            for n in range(KB // 4):
                if n >= 2:
                    pe.wait_ge(moved, n - 1)
                for q in range(4):
                    j = 4 * n + q
                    mm = pe.transpose(ps_w[n % 2][0:E, q * 128:q * 128 + 128], cw[:, j, :], keep["ident"][:, :])
                mm.then_inc(turned, 1)
            pe.wait_ge(moved, KB // 4)

            def up(i, m):
                e, hb = divmod(m, HB)
                if hb == 0:
                    pe.matmul(ps_w[e % 2][:, 0:TT], keep["exp_sel"][:, e, :], cw_t[:, bass.ds(i * TT, TT)],
                              start=True, stop=True).then_inc(w_full, 1)
                for h in range(2):
                    mm = pe.matmul(ps_h[m % 3][:, 0:TT], w1[:, e, h, hb * 128:hb * 128 + 128], xl[:, h, bass.ds(i * TT, TT)],
                                   start=h == 0, stop=h == 1)
                mm.then_inc(h_full, 1)

            with pe.Fori(0, NTT) as i:
                up(i, 0)
                pe.wait_ge(o_read, i + 1)
                up(i, 1)
                for o in range(2):
                    pe.matmul(ps_o[:, o, 0:TT], b2[:, o * 128:o * 128 + 128], cw_t[:, bass.ds(i * TT, TT)], start=True, stop=False)
                for m in range(M):
                    e, hb = divmod(m, HB)
                    if m + 2 < M:
                        up(i, m + 2)
                    pe.wait_ge(hw_done, i * M + m + 1)
                    for o in range(2):
                        mm = pe.matmul(ps_o[:, o, 0:TT], w2[:, e, hb, o * 128:o * 128 + 128], hw[m % 3][:, :],
                                       start=False, stop=m == M - 1)
                mm.then_inc(o_full, 1)

        @block.scalar
        def _(act):
            act.wait_ge(step_done, 3)
            act.activation(ex[:, :, :], dif[:, :, :], ACT.Exp).then_inc(ex_done, 1)
            act.activation(ex2[:, :, :], dif2[:, :, :], ACT.Exp).then_inc(ex_done, 1)
            act.wait_ge(loaded, 16 * (3 + 3 * E))
            with act.Fori(0, NTT) as i:
                for m in range(M):
                    e, hb = divmod(m, HB)
                    act.wait_ge(h_full, i * M + m + 1)
                    act.activation(hg[m % 3][:, :], ps_h[m % 3][:, 0:TT], ACT.Gelu, bias=b1[:, e, hb:hb + 1]).then_inc(g_done, 1)

        @block.vector
        def _(dve):
            dve.wait_ge(gate_full, 1)
            dve.wait_ge(loaded, 16 * (3 + 3 * E))
            logits = ps_g[:, 0:KB * E].rearrange("p (j e) -> p j e", e=E)
            dve.tensor_tensor(lg[:, :, :], logits, gb[:, :].unsqueeze(1).to_broadcast([128, KB, E]), ALU.add).then_inc(step_done, 1)
            dve.wait_ge(step_done, 1)
            for j in range(KB):
                last = dve.max(top[:, j, :], lg[:, j, :])
            last.then_inc(step_done, 1)
            dve.wait_ge(step_done, 2)
            dve.tensor_tensor(dif[:, :, :], lg[:, :, :], wide(top[:, :, 0:1]), ALU.subtract)
            dve.tensor_tensor(dif2[:, :, :], top[:, :, 0:2], top[:, :, 0:1].to_broadcast([128, KB, 2]), ALU.subtract).then_inc(step_done, 1)
            for j in range(KB):
                last = dve.max_index(idx[:, j, :], top[:, j, :], lg[:, j, :])
            last.then_inc(step_done, 1)
            dve.wait_ge(step_done, 4)
            dve.tensor_copy(pick[:, :, :], idx[:, :, 0:2]).then_inc(step_done, 1)
            dve.wait_ge(ex_done, 2)
            dve.tensor_reduce(sm[:, :, :], ex[:, :, :], AX.X, ALU.add).then_inc(step_done, 1)
            dve.wait_ge(step_done, 6)
            dve.reciprocal(inv[:, :, :], sm[:, :, :]).then_inc(step_done, 1)
            dve.wait_ge(step_done, 7)
            dve.tensor_tensor(v2[:, :, :], ex2[:, :, :], inv[:, :, :].to_broadcast([128, KB, 2]), ALU.mult).then_inc(step_done, 1)
            dve.wait_ge(step_done, 8)
            dve.wait_ge(iota_done, 1)
            num = iota[:, :].unsqueeze(1).to_broadcast([128, KB, E])
            dve.tensor_tensor(cw[:, :, :], num, wide(pick[:, :, 0:1]), ALU.is_equal)
            dve.tensor_tensor(cw2[:, :, :], num, wide(pick[:, :, 1:2]), ALU.is_equal).then_inc(step_done, 1)
            dve.wait_ge(step_done, 9)
            dve.tensor_tensor(cw[:, :, :], cw[:, :, :], wide(v2[:, :, 0:1]), ALU.mult).then_inc(step_done, 1)
            dve.tensor_tensor(cw2[:, :, :], cw2[:, :, :], wide(v2[:, :, 1:2]), ALU.mult).then_inc(step_done, 1)
            dve.wait_ge(step_done, 11)
            dve.tensor_tensor(cw[:, :, :], cw[:, :, :], cw2[:, :, :], ALU.add).then_inc(step_done, 1)
            for n in range(KB // 4):
                dve.wait_ge(turned, n + 1)
                dve.tensor_copy(cw_t[:, n * 512:n * 512 + 512], ps_w[n % 2][0:E, :]).then_inc(moved, 1)
            with dve.Fori(0, NTT // 2) as i:
                for k in range(2):
                    for m in range(M):
                        e, hb = divmod(m, HB)
                        if hb == 0:
                            dve.wait_ge(w_full, i * (2 * E) + k * E + e + 1)
                        dve.wait_ge(g_done, i * (2 * M) + k * M + m + 1)
                        dve.tensor_tensor(hw[m % 3][:, :], hg[m % 3][:, :], ps_w[e % 2][:, 0:TT], ALU.mult).then_inc(hw_done, 1)
                    dve.wait_ge(o_full, i * 2 + k + 1)
                    dve.wait_ge(gone[k], i * 16 + 16)
                    dve.tensor_tensor(res[:, k, :, :], ps_o[:, :, 0:TT], x1[:, :, bass.ds(i * (2 * TT) + k * TT, TT)],
                                      ALU.add).then_inc(o_read, 1)


def conv_attn_hybrid_kernel(nc, x, w0, w1, out):
    dram = lambda name, shape, dt=F32: nc.dram_tensor(name, shape, dt).ap()
    P = {
        "xn": dram("xn_dram", (B, C, L)),
        "rec": dram("rec_dram", (U, STEPS, 128, G + 1)),
        "parts": dram("parts_dram", (U, STEPS, 3, 128, 2, WC), BF16),
        "bc": dram("bc_dram", (U, STEPS, 2 * N, WC)),
        "y": dram("y_dram", (U, STEPS, 128, WC)),
        "z": dram("z_dram", (B, C, L)),
        "zn": dram("zn_dram", (B, C, L)),
    }
    with ExitStack() as ctx:
        s = Space(nc, ctx, "keep")
        shapes = {
            "ident": [128, 128], "ones_c": [128, 128], "ones_d": [128, 128], "ones": [128, 128], "eps": [128, 1], "ln_2_20": [128, 1],
            "sum_sel": [128, 2 * D - J], "exp_sel": [E, E, 128], "rec": [128, STEPS, G + 1],
            "w_eff": [128, K, D], "w_bc": [128, K, 2 * N], "w_pair": [128, 3, D], "w_one": [DM, 3, D],
            "dt_b": [D, K], "conv_b": [D, 1], "onorm_g": [D, 1], "onorm_b": [D, 1], "out_W": [D, DM], "d_sum": [D, 1],
            "ln_g": [128, 2], "ln_b": [128, 2], "proj_b": [128, 2], "proj_W": [128, 2, C], "skip": [DM, 1],
        }
        keep = {name: s.sb(name, shape) for name, shape in shapes.items()}
        keep["parts_sel"] = s.sb("parts_sel", [96, 4, J, N], BF16)
        setup_phase(nc, P, w0, keep)
        norm_phase(nc, "norm0", x.rearrange("b c y x -> b c (y x)"), P["xn"], keep)
        with ExitStack() as mamba:
            xs = mamba.enter_context(nc.sbuf_tensor("xs", [128, U * L], F32))
            conv_phase(nc, P, keep, xs)
            delta_phase(nc, P, keep, xs)
            scan_phase(nc, P, keep)
            merge_phase(nc, P, keep, xs)
        norm_phase(nc, "norm1", P["z"], P["zn"], keep)
        x1, f_t, o_t = (s.sb(n, [128, 2, NT]) for n in ("x1", "f_t", "o_t"))
        den = s.sb("den", [128, KB, NTT])
        project_phase(nc, P, keep, x1, f_t)
        attention_phase(nc, keep, f_t, o_t, den)
        blend_phase(nc, keep, x1, f_t, o_t, den)
        expert_phase(nc, w1, keep, x1, o_t, f_t, out)


_L0 = ["ln_g", "ln_b", "skip_scale", "proj_W", "proj_b", "in_W", "conv_W", "conv_b", "x_proj_W", "dt_W", "dt_b",
       "A_logs", "Ds", "onorm_g", "onorm_b", "out_W"]
_L1 = ["gate_w", "gate_b", "W1", "b1", "W2", "b2"]


def kernel(**inputs):
    import numpy as _np
    import concourse.bacc as _bacc
    from concourse.bass_utils import run_bass_kernel_spmd as _run

    nc = _bacc.Bacc("TRN2", target_bir_lowering=False, num_devices=1)
    arrays, args = {}, {}
    for name, value in inputs.items():
        a = _np.ascontiguousarray(value)
        arrays[f"in_{name}"] = a
        args[name] = nc.dram_tensor(f"in_{name}", a.shape, mybir.dt.from_np(a.dtype), kind="ExternalInput").ap()
    out = nc.dram_tensor("out_x", (B, C, H, W), F32, kind="ExternalOutput").ap()
    conv_attn_hybrid_kernel(nc, args["x"], {n: args[f"L0_conv_{n}"] for n in _L0}, {n: args[f"L1_ffn_{n}"] for n in _L1}, out)
    r = _run(nc, [arrays], core_ids=[0])
    return r.results[0]["out_x"]
```

```python
import math
from contextlib import ExitStack

import concourse.bass as bass
from concourse import mybir

F32 = mybir.dt.float32
BF16 = mybir.dt.bfloat16
F32R = mybir.dt.float32r
U32 = mybir.dt.uint32
ALU = mybir.AluOpType
ACT = mybir.ActivationFunctionType
AX = mybir.AxisListType

B, C, H, W = 2, 256, 48, 48
L = H * W
NT = B * L
BR = 4
U = B * BR
DM = C // BR
D = 128
K = 4
R, N = 4, 16
WC = 768
NCH = L // WC
HW_ = WC // 2
STEPS = K * NCH
NKC = U * STEPS
J = 128 // N
G = D // J
TT = 384
NTT = NT // TT
TPI = L // TT
KB = NT // 128
E, HF = 8, 512
HB = HF // 128


class Space:

    def __init__(self, nc, ctx, tag):
        self.nc, self.ctx, self.tag = nc, ctx, tag

    def sb(self, name, shape, dt=F32):
        return self.ctx.enter_context(self.nc.sbuf_tensor(f"{self.tag}_{name}", shape, dt))

    def ps(self, name, shape, dt=F32):
        return self.ctx.enter_context(self.nc.psum_tensor(f"{self.tag}_{name}", shape, dt))

    def sem(self, name):
        return self.ctx.enter_context(self.nc.semaphore(f"{self.tag}_{name}"))


def products(pe, out, highs, lows, start, stop):
    (wh, xh), (wl, xl) = highs, lows
    pe.matmul(out, wl, xh, start=start, stop=False)
    pe.matmul(out, wh, xl, start=False, stop=False)
    return pe.matmul(out, wh, xh, start=False, stop=stop)


def setup_phase(nc, P, w, keep):
    with ExitStack() as ctx:
        s = Space(nc, ctx, "setup")
        dts_rows = s.sb("dts_rows", [R, K, D])
        dtw_t = s.sb("dtw_t", [R, K, D])
        bc_rows = s.sb("bc_rows", [2 * N, K, D])
        conv_taps = s.sb("conv_taps", [128, D, 9])
        in_w2 = s.sb("in_w2", [128, D])
        ds4 = s.sb("ds4", [D, K])
        a_log = s.sb("a_log", [128, K, G])
        a_exp = s.sb("a_exp", [128, K, G])
        ps_w = s.ps("ps_w", [128, 4, 512])
        loaded, ones_set, ident_set = s.sem("loaded"), s.sem("ones_set"), s.sem("ident_set")
        weff_ps, bc_ps, exp_done, a_done = s.sem("weff_ps"), s.sem("bc_ps"), s.sem("exp_done"), s.sem("a_done")
        rec_out, pool_set, dve_done = s.sem("rec_out"), s.sem("pool_set"), s.sem("dve_done")
        loads = []
        loads.append((dts_rows[:, :, :], w["x_proj_W"][:, 0:R, :].rearrange("k c d -> c k d")))
        loads.append((dtw_t[:, :, :], w["dt_W"].rearrange("k d r -> r k d")))
        loads.append((bc_rows[:, :, :], w["x_proj_W"][:, R:, :].rearrange("k c d -> c k d")))
        for half in range(2):
            loads.append((in_w2[64 * half:64 * half + 64, :], w["in_W"]))
        loads.append((conv_taps[:, :, :], w["conv_W"].rearrange("d a y x -> (a d) (y x)").partition_broadcast(128)))
        loads.append((ds4[:, :], w["Ds"].rearrange("(k d) -> d k", k=K)))
        loads.append((keep["dt_b"][:, :], w["dt_b"].rearrange("k d -> d k")))
        loads.append((keep["conv_b"][:, :], w["conv_b"].rearrange("(d a) -> d a", a=1)))
        loads.append((keep["onorm_g"][:, :], w["onorm_g"].rearrange("(d a) -> d a", a=1)))
        loads.append((keep["onorm_b"][:, :], w["onorm_b"].rearrange("(d a) -> d a", a=1)))
        loads.append((keep["out_W"][:, :], w["out_W"]))
        loads.append((keep["ln_g"][:, :], w["ln_g"].rearrange("(h p) -> p h", h=2)))
        loads.append((keep["ln_b"][:, :], w["ln_b"].rearrange("(h p) -> p h", h=2)))
        loads.append((keep["proj_b"][:, :], w["proj_b"].rearrange("(h p) -> p h", h=2)))
        loads.append((keep["proj_W"][:, :, :], w["proj_W"].rearrange("(h p) n -> p h n", h=2)))
        loads.append((keep["skip"][:, :], w["skip_scale"].partition_broadcast(64)))
        a_src = w["A_logs"].rearrange("(k g j) n -> j n k g", k=K, j=J)
        for j in range(J):
            for k in range(K):
                loads.append((a_log[N * j:N * j + N, k, :], a_src[j, :, k, :]))
        n_loads = len(loads)
        block = ctx.enter_context(nc.Block())

        @block.sync
        def _(sp):
            for dst, src in loads:
                sp.dma_start(dst, src, allow_slow_non_contiguous=True).then_inc(loaded, 16)
            sp.wait_ge(a_done, 1)
            sp.wait_ge(dve_done, 1)
            with sp.Fori(0, U) as u:
                sp.dma_start(P["rec"][u].rearrange("s p f -> p s f"), keep["rec"][:, :, :]).then_inc(rec_out, 16)
            sp.wait_ge(rec_out, 16 * U)

        @block.gpsimd
        def _(pool):
            pool.memset(keep["ident"][:, :], 0.0).then_inc(ones_set, 1)
            pool.memset(keep["ones_c"][:, :], 1.0 / C).then_inc(pool_set, 1)
            pool.memset(keep["ones_d"][:, :], 1.0 / D).then_inc(pool_set, 1)
            pool.memset(keep["ones"][:, :], 1.0).then_inc(pool_set, 1)
            pool.memset(keep["eps"][:, :], 1e-5).then_inc(pool_set, 1)
            pool.memset(keep["ln_2_20"][:, :], 20 * math.log(2.0))
            pool.memset(keep["parts_sel"][:, :, :, :], 0.0).then_inc(ones_set, 1)
            pool.memset(keep["sum_sel"][:, :], 1.0).then_inc(ones_set, 1)
            pool.memset(keep["exp_sel"][:, :, :], 0.0).then_inc(ones_set, 1)
            pool.wait_ge(ones_set, 4)
            pool.affine_select(out=keep["ident"][:, :], in_=keep["ident"][:, :], compare_op=ALU.not_equal,
                               fill=1.0, base=0, pattern=[[-1, 128]], channel_multiplier=1).then_inc(ident_set, 1)
            for part in range(3):
                pool.wait_ge(ident_set, part + 1)
                v = keep["parts_sel"][:, :, :, :]
                pool.affine_select(out=v, in_=v, compare_op=ALU.not_equal, fill=1.0, base=-32 * part,
                                   pattern=[[-J, 4], [-1, J], [0, N]], channel_multiplier=1).then_inc(ident_set, 1)
            v = keep["sum_sel"][:, :]
            pool.affine_select(out=v, in_=v, compare_op=ALU.is_ge, fill=0.0, base=N * (D - J),
                               pattern=[[-N, 2 * D - J]], channel_multiplier=1).then_inc(ident_set, 1)
            pool.wait_ge(ident_set, 5)
            pool.affine_select(out=v, in_=v, compare_op=ALU.is_ge, fill=0.0, base=N - 1 - N * (D - J),
                               pattern=[[N, 2 * D - J]], channel_multiplier=-1).then_inc(ident_set, 1)
            v = keep["exp_sel"][:, :, :]
            pool.affine_select(out=v, in_=v, compare_op=ALU.not_equal, fill=1.0, base=0,
                               pattern=[[-1, E], [0, 128]], channel_multiplier=1).then_inc(ident_set, 1)

        @block.tensor
        def _(pe):
            pe.wait_ge(loaded, 16 * n_loads)
            for k in range(K):
                mm = pe.matmul(ps_w[:, k, 0:D], dts_rows[:, k, :], dtw_t[:, k, :], start=True, stop=True)
            mm.then_inc(weff_ps, 1)
            pe.wait_ge(ident_set, 1)
            pe.wait_ge(dve_done, 1)
            for k in range(K):
                mm = pe.transpose(ps_w[:, k, 256:256 + 2 * N], bc_rows[:, k, :], keep["ident"][0:2 * N, 0:2 * N])
            mm.then_inc(bc_ps, 1)

        @block.scalar
        def _(act):
            act.wait_ge(loaded, 16 * n_loads)
            act.activation(a_exp[:, :, :], a_log[:, :, :], ACT.Exp).then_inc(exp_done, 1)

        @block.vector
        def _(dve):
            dve.memset(keep["rec"][:, :, G:G + 1], 1.0).then_inc(pool_set, 1)
            dve.wait_ge(weff_ps, 1)
            dve.tensor_copy(keep["w_eff"][:, :, :], ps_w[:, :, 0:D]).then_inc(dve_done, 1)
            dve.wait_ge(exp_done, 1)
            dve.wait_ge(pool_set, 5)
            for c in range(NCH):
                rec = keep["rec"][:, :, :].rearrange("p (k c) f -> p k c f", c=NCH)
                last = dve.tensor_scalar(rec[:, :, c, 0:G], a_exp[:, :, :], -1.0, None, ALU.mult)
            dve.memset(rec[:, :, NCH - 1, G:G + 1], 0.0).then_inc(a_done, 1)
            for dy in range(3):
                for half in range(2):
                    p = slice(64 * half, 64 * half + 64)
                    dve.tensor_tensor(keep["w_pair"][p, dy, :], in_w2[p, :], conv_taps[p, :, 3 * dy + half], ALU.mult)
                dve.tensor_tensor(keep["w_one"][:, dy, :], in_w2[0:64, :], conv_taps[0:64, :, 3 * dy + 2], ALU.mult)
            dve.tensor_reduce(keep["d_sum"][:, :], ds4[:, :], AX.X, ALU.add)
            dve.wait_ge(bc_ps, 1)
            dve.tensor_copy(keep["w_bc"][:, :, :], ps_w[:, :, 256:256 + 2 * N])


def norm_phase(nc, tag, src, dst, keep):
    LN = 3
    with ExitStack() as ctx:
        s = Space(nc, ctx, tag)
        x = s.sb("x", [128, LN, 2, TT])
        xc = s.sb("xc", [128, LN, 2, TT])
        sq = s.sb("sq", [128, LN, 2, TT])
        sd = s.sb("sd", [128, LN, TT])
        rs = s.sb("rs", [128, LN, TT])
        ps_m = s.ps("ps_m", [128, LN, 512])
        ps_v = s.ps("ps_v", [128, LN, 512])
        came = [s.sem(f"came{i}") for i in range(LN)]
        link = [s.sem(f"link{i}") for i in range(LN)]
        gone = [s.sem(f"gone{i}") for i in range(LN)]
        STEP = 8
        block = ctx.enter_context(nc.Block())
        sv = src.rearrange("b (h p) (i t) -> b i p h t", h=2, t=TT)
        dv = dst.rearrange("b (h p) (i t) -> b i p h t", h=2, t=TT)

        @block.sync
        def _(sp):
            for ln in range(LN):
                sp.sem_inc(link[ln], 1)
                sp.sem_inc(gone[ln], 16)
            with sp.Fori(0, B) as b:
                with sp.Fori(0, TPI // LN) as i:
                    for ln in range(LN):
                        sp.wait_ge(link[ln], b * (STEP * TPI // LN) + i * STEP + 1)
                        sp.dma_start(x[:, ln, :, :], sv[b, i * LN + ln]).then_inc(came[ln], 16)
                    for ln in range(LN):
                        sp.wait_ge(link[ln], b * (STEP * TPI // LN) + i * STEP + STEP + 1)
                        sp.dma_start(dv[b, i * LN + ln], sq[:, ln, :, :]).then_inc(gone[ln], 16)
            for ln in range(LN):
                sp.wait_ge(gone[ln], 16 * (NTT // LN) + 16)

        @block.tensor
        def _(pe):
            with pe.Fori(0, NTT // LN) as i:
                for ln in range(LN):
                    pe.wait_ge(came[ln], i * 16 + 16)
                    for h in range(2):
                        mm = pe.matmul(ps_m[:, ln, 0:TT], keep["ones_c"][:, :], x[:, ln, h, :], start=h == 0, stop=h == 1)
                    mm.then_inc(link[ln], 1)
                for ln in range(LN):
                    pe.wait_ge(link[ln], i * STEP + 4)
                    for h in range(2):
                        mm = pe.matmul(ps_v[:, ln, 0:TT], keep["ones_c"][:, :], sq[:, ln, h, :], start=h == 0, stop=h == 1)
                    mm.then_inc(link[ln], 1)

        @block.vector
        def _(dve):
            with dve.Fori(0, NTT // LN) as i:
                for ln in range(LN):
                    dve.wait_ge(link[ln], i * STEP + 2)
                    mean = ps_m[:, ln, 0:TT].unsqueeze(1).to_broadcast([128, 2, TT])
                    dve.tensor_tensor(xc[:, ln, :, :], x[:, ln, :, :], mean, ALU.subtract).then_inc(link[ln], 1)
                for ln in range(LN):
                    dve.wait_ge(link[ln], i * STEP + 7)
                    inv = rs[:, ln, :].unsqueeze(1).to_broadcast([128, 2, TT])
                    dve.tensor_tensor(xc[:, ln, :, :], xc[:, ln, :, :], inv, ALU.mult).then_inc(link[ln], 1)

        @block.scalar
        def _(act):
            with act.Fori(0, NTT // LN) as i:
                for ln in range(LN):
                    act.wait_ge(link[ln], i * STEP + 3)
                    act.wait_ge(gone[ln], i * 16 + 16)
                    act.activation(sq[:, ln, :, :], xc[:, ln, :, :], ACT.Square).then_inc(link[ln], 1)
                for ln in range(LN):
                    act.wait_ge(link[ln], i * STEP + 5)
                    act.activation(sd[:, ln, :], ps_v[:, ln, 0:TT], ACT.Ln, bias=keep["eps"][:, 0:1]).then_inc(link[ln], 1)
                for ln in range(LN):
                    act.wait_ge(link[ln], i * STEP + 6)
                    act.activation(rs[:, ln, :], sd[:, ln, :], ACT.Exp, scale=-0.5).then_inc(link[ln], 1)
                for ln in range(LN):
                    act.wait_ge(link[ln], i * STEP + 8)
                    for h in range(2):
                        last = act.activation(sq[:, ln, h, :], xc[:, ln, h, :], ACT.Identity,
                                              scale=keep["ln_g"][:, h:h + 1], bias=keep["ln_b"][:, h:h + 1])
                    last.then_inc(link[ln], 1)


def conv_phase(nc, P, keep, xs):
    with ExitStack() as ctx:
        s = Space(nc, ctx, "conv")
        pad = s.sb("pad", [128, 2, H + 2, W + 2])
        ps_c = s.ps("ps_c", [128, 4, 512])
        cleared, came, full, out = s.sem("cleared"), [s.sem("came0"), s.sem("came1")], s.sem("full"), s.sem("out")
        TU = TPI
        CR = 2 * TU
        block = ctx.enter_context(nc.Block())
        src = P["xn"].rearrange("b (r c) l -> (b r) c l", r=BR)

        @block.sync
        def _(sp):
            sp.wait_ge(cleared, 1)
            with sp.Fori(0, U // 2) as i:
                for k in range(2):
                    sp.wait_ge(out, i * (2 * TU) + (CR - TU + k * TU))
                    img = src[i * 2 + k].rearrange("c (h w) -> c h w", h=H)
                    for half in range(2):
                        sp.dma_start(pad[64 * half:64 * half + 64, k, 1:H + 1, 1 - half:W + 1 - half], img).then_inc(came[k], 16)

        @block.tensor
        def _(pe):
            with pe.Fori(0, U // 2) as i:
                for k in range(2):
                    pe.wait_ge(came[k], i * 32 + 32)
                    for t in range(TU):
                        n = k * TU + t
                        pe.wait_ge(out, i * (2 * TU) + (n + CR - 3))
                        o = ps_c[:, n % 4, 0:TT]
                        r0 = t * (TT // W)
                        for dy in range(3):
                            rows = slice(r0 + dy, r0 + dy + TT // W)
                            pe.matmul(o, keep["w_pair"][:, dy, :], pad[:, k, rows, 0:W], start=dy == 0, stop=False)
                            mm = pe.matmul(o, keep["w_one"][:, dy, :], pad[0:64, k, rows, 2:W + 2], start=False, stop=dy == 2)
                        mm.then_inc(full, 1)

        @block.vector
        def _(dve):
            dve.memset(pad[:, :, :, :], 0.0).then_inc(cleared, 1)

        @block.scalar
        def _(act):
            act.sem_inc(out, CR)
            with act.Fori(0, U // 2) as i:
                for n in range(2 * TU):
                    act.wait_ge(full, i * (2 * TU) + n + 1)
                    act.activation(xs[:, bass.ds(i * (2 * L) + n * TT, TT)], ps_c[:, n % 4, 0:TT], ACT.Silu,
                                   bias=keep["conv_b"][:, 0:1]).then_inc(out, 1)


def scan_order(x, k, at, size):
    if k % 2 == 0:
        return x[:, L - 1 - at:(L - 1 - at - size) if L - 1 - at - size >= 0 else None:-1] if k == 2 else x[:, at:at + size]
    v = x.rearrange("p (h w) -> p w h", h=H)
    w0, nw = at // H, size // H
    if k == 1:
        return v[:, w0:w0 + nw, :]
    lo = W - 1 - w0 - nw
    return v[:, W - 1 - w0:(lo if lo >= 0 else None):-1, ::-1]


def like(x, view):
    return x if len(view.shape) == 2 else x.rearrange("p (a b) -> p a b", b=H)


def delta_phase(nc, P, keep, xs):
    with ExitStack() as ctx:
        s = Space(nc, ctx, "delta")
        xu = s.sb("xu", [128, L])
        two = lambda name, dt=F32: [s.sb(f"{name}{i}", [128, WC], dt) for i in range(2)]
        mag, pos, ex, lg = two("mag"), two("pos"), two("ex"), two("lg")
        dm, co, sm = two("dm"), two("co"), two("sm")
        delta, du, rd, ru = two("delta"), two("du"), two("rd"), two("ru")
        parts = [s.sb(f"parts{i}", [128, 3, 2, WC], BF16) for i in range(2)]
        bc = [s.sb(f"bc{i}", [2 * N, WC]) for i in range(2)]
        ps_a = [s.ps(f"ps_a{i}", [128, 2, 512]) for i in range(2)]
        ps_b = [s.ps(f"ps_b{i}", [2 * N, 2, 512]) for i in range(2)]
        x_here, x_used = s.sem("x_here"), s.sem("x_used")
        a_full, a_read, b_full, b_read = s.sem("a_full"), s.sem("a_read"), s.sem("b_full"), s.sem("b_read")
        mag_done, ex_done, lg_done, hid_done, hiu_done = (s.sem(x) for x in ("mag_done", "ex_done", "lg_done", "hid_done", "hiu_done"))
        dm_done, co_done, sm_done, delta_done, du_done = (s.sem(x) for x in ("dm_done", "co_done", "sm_done", "delta_done", "du_done"))
        rd_done, midd_done, midu_done, ru_done, lo_done = (s.sem(x) for x in ("rd_done", "midd_done", "midu_done", "ru_done", "lo_done"))
        parts_out = [s.sem("parts_out0"), s.sem("parts_out1")]
        bc_out = [s.sem("bc_out0"), s.sem("bc_out1")]
        block = ctx.enter_context(nc.Block())
        HU = STEPS // 2

        @block.sync
        def _(sp):
            with sp.Fori(0, U) as u:
                for st in range(STEPS):
                    sp.wait_ge(b_read, u * STEPS + st + 1 + 2)
                    sp.dma_start(P["bc"][u, st], bc[st % 2][:, :]).then_inc(bc_out[st % 2], 16)
                    sp.wait_ge(lo_done, u * (2 * STEPS) + 2 * st + 2)
                    sp.dma_start(P["parts"][u, st].rearrange("a p t l -> p a (t l)"),
                                 parts[st % 2][:, :, :, :].rearrange("p a t l -> p a (t l)")).then_inc(parts_out[st % 2], 16)
            for k in range(2):
                sp.wait_ge(parts_out[k], 16 * U * HU + 16)
                sp.wait_ge(bc_out[k], 16 * U * HU + 16)

        @block.tensor
        def _(pe):
            with pe.Fori(0, U) as u:
                pe.wait_ge(x_here, u + 1)
                for st in range(STEPS):
                    k, c = divmod(st, NCH)
                    pe.wait_ge(a_read, u * STEPS + st + 1)
                    for h in range(2):
                        v = scan_order(xu[:, :], k, c * WC + h * HW_, HW_)
                        mm = pe.matmul(like(ps_a[st % 2][:, h, 0:HW_], v), keep["w_eff"][:, k, :], v, start=True, stop=True)
                    mm.then_inc(a_full, 1)
                    pe.wait_ge(b_read, u * STEPS + st + 1)
                    for h in range(2):
                        v = scan_order(xu[:, :], k, c * WC + h * HW_, HW_)
                        mm = pe.matmul(like(ps_b[st % 2][:, h, 0:HW_], v), keep["w_bc"][:, k, :], v, start=True, stop=True)
                    mm.then_inc(b_full, 1)

        @block.scalar
        def _(act):
            act.sem_inc(a_read, 2)
            act.sem_inc(b_read, 2)
            for k in range(2):
                act.sem_inc(parts_out[k], 16)
                act.sem_inc(bc_out[k], 16)

            def highs(u, st):
                act.wait_ge(parts_out[st % 2], u * (16 * HU) + 16 * (st // 2) + 16)
                act.wait_ge(delta_done, u * STEPS + st + 1)
                act.activation(parts[st % 2][:, 0, 0, :], delta[st % 2][:, :], ACT.Copy).then_inc(hid_done, 1)
                act.wait_ge(du_done, u * STEPS + st + 1)
                act.activation(parts[st % 2][:, 0, 1, :], du[st % 2][:, :], ACT.Copy).then_inc(hiu_done, 1)

            with act.Fori(0, U) as u:
                for st in range(STEPS):
                    k, i = st // NCH, st % 2
                    act.wait_ge(a_full, u * STEPS + st + 1)
                    halves = lambda x: x[:, :].rearrange("p (a b) -> p a b", a=2)
                    act.activation(halves(mag[i]), ps_a[i][:, :, 0:HW_], ACT.Abs, bias=keep["dt_b"][:, k:k + 1]).then_inc(mag_done, 1)
                    act.activation(halves(pos[i]), ps_a[i][:, :, 0:HW_], ACT.Relu, bias=keep["dt_b"][:, k:k + 1]).then_inc(a_read, 1)
                    act.wait_ge(mag_done, u * STEPS + st + 1)
                    act.activation(ex[i][:, :], mag[i][:, :], ACT.Exp, scale=-1.0).then_inc(ex_done, 1)
                    act.wait_ge(b_full, u * STEPS + st + 1)
                    act.wait_ge(bc_out[i], u * (16 * HU) + 16 * (st // 2) + 16)
                    act.activation(halves(bc[i]), ps_b[i][:, :, 0:HW_], ACT.Copy).then_inc(b_read, 1)
                    if st:
                        highs(u, st - 1)
                    act.wait_ge(dm_done, u * STEPS + st + 1)
                    act.activation(lg[i][:, :], dm[i][:, :], ACT.Ln, bias=1.0).then_inc(lg_done, 1)
                highs(u, STEPS - 1)

        @block.vector
        def _(dve):
            def rest_d(u, st):
                i = st % 2
                dve.wait_ge(hid_done, u * STEPS + st + 1)
                dve.tensor_tensor(rd[i][:, :], delta[i][:, :], parts[i][:, 0, 0, :], ALU.subtract).then_inc(rd_done, 1)

            def mid_d(u, st):
                i = st % 2
                dve.wait_ge(rd_done, u * STEPS + st + 1)
                dve.tensor_copy(parts[i][:, 1, 0, :], rd[i][:, :]).then_inc(midd_done, 1)

            def mid_u(u, st):
                i = st % 2
                dve.wait_ge(ru_done, u * STEPS + st + 1)
                dve.tensor_copy(parts[i][:, 1, 1, :], ru[i][:, :]).then_inc(midu_done, 1)

            with dve.Fori(0, U) as u:
                dve.wait_ge(a_read, u * STEPS + 2)
                dve.wait_ge(b_read, u * STEPS + 2)
                dve.tensor_copy(xu[:, :], xs[:, bass.ds(u * L, L)]).then_inc(x_here, 1)
                for st in range(STEPS):
                    k, c, i = st // NCH, st % NCH, st % 2
                    dve.wait_ge(ex_done, u * STEPS + st + 1)
                    dve.tensor_scalar(dm[i][:, :], ex[i][:, :], 1.0, -1.0, ALU.add, ALU.add).then_inc(dm_done, 1)
                    if st:
                        rest_d(u, st - 1)
                    dve.wait_ge(dm_done, u * STEPS + st + 1)
                    dve.tensor_tensor(co[i][:, :], ex[i][:, :], dm[i][:, :], ALU.subtract).then_inc(co_done, 1)
                    if st:
                        mid_d(u, st - 1)
                    dve.wait_ge(co_done, u * STEPS + st + 1)
                    dve.wait_ge(lg_done, u * STEPS + st + 1)
                    dve.tensor_tensor(sm[i][:, :], co[i][:, :], lg[i][:, :], ALU.add).then_inc(sm_done, 1)
                    if st:
                        mid_u(u, st - 1)
                    dve.wait_ge(sm_done, u * STEPS + st + 1)
                    dve.tensor_tensor(delta[i][:, :], sm[i][:, :], pos[i][:, :], ALU.add).then_inc(delta_done, 1)
                    v = scan_order(xu[:, :], k, c * WC, WC)
                    dve.wait_ge(delta_done, u * STEPS + st + 1)
                    dve.tensor_tensor(like(du[i][:, :], v), like(delta[i][:, :], v), v, ALU.mult).then_inc(du_done, 1)
                rest_d(u, STEPS - 1)
                mid_d(u, STEPS - 1)
                mid_u(u, STEPS - 1)

        @block.gpsimd
        def _(pool):
            with pool.Fori(0, U) as u:
                for st in range(STEPS):
                    i = st % 2
                    pool.wait_ge(hiu_done, u * STEPS + st + 1)
                    pool.tensor_tensor(ru[i][:, :], du[i][:, :], parts[i][:, 0, 1, :], ALU.subtract).then_inc(ru_done, 1)
                    pool.wait_ge(midd_done, u * STEPS + st + 1)
                    pool.tensor_tensor(parts[i][:, 2, 0, :], rd[i][:, :], parts[i][:, 1, 0, :], ALU.subtract).then_inc(lo_done, 1)
                    pool.wait_ge(midu_done, u * STEPS + st + 1)
                    pool.tensor_tensor(parts[i][:, 2, 1, :], ru[i][:, :], parts[i][:, 1, 1, :], ALU.subtract).then_inc(lo_done, 1)


def scan_phase(nc, P, keep):
    with ExitStack() as ctx:
        s = Space(nc, ctx, "scan")
        stack = [s.sb(f"stack{i}", [96, 4, 2, WC], BF16) for i in range(2)]
        b_rep = [s.sb(f"b_rep{i}", [128, WC]) for i in range(2)]
        c_rep = [s.sb(f"c_rep{i}", [128, WC]) for i in range(2)]
        rec = [s.sb(f"rec{i}", [128, G + 1]) for i in range(2)]
        bu = [s.sb(f"bu{i}", [128, WC]) for i in range(4)]
        h = [s.sb(f"h{i}", [128, WC]) for i in range(4)]
        hc = [s.sb(f"hc{i}", [128, WC]) for i in range(4)]
        y = [s.sb(f"y{i}", [128, WC]) for i in range(2)]
        h_last = s.sb("h_last", [128, G])
        ps_d = [s.ps(f"ps_d{i}", [128, 1024]) for i in range(2)]
        ps_u = s.ps("ps_u", [128, 1024])
        ps_y = s.ps("ps_y", [128, 1024])
        came = [s.sem(f"came{i}") for i in range(2)]
        y_out = [s.sem(f"y_out{i}") for i in range(2)]
        u_full, d_full, bu_done, exp_done, scan_done, hc_done, y_full, y_read, zeroed = (
            s.sem(x) for x in ("u_full", "d_full", "bu_done", "exp_done", "scan_done", "hc_done", "y_full", "y_read", "zeroed"))
        LOADS = 3 + 2 * J + 1
        TB = 2 * G
        NI = NKC // 2
        pieces = [(0, 512), (512, WC)]
        block = ctx.enter_context(nc.Block())
        recs = P["rec"].rearrange("u s p f -> (u s) p f")
        partsd = P["parts"].rearrange("u s a (q i) t l -> (u s) a i q t l", q=4)
        bcd = P["bc"].rearrange("u s n l -> (u s) n l")
        yd = P["y"].rearrange("u s p l -> (u s) p l")

        @block.sync
        def _(sp):
            for k in range(2):
                sp.sem_inc(y_out[k], 16)

            def store(i, cc):
                sp.wait_ge(y_read, i * 2 + (cc - 1))
                sp.dma_start(yd[i * 2 + (cc - 2)], y[cc % 2][:, :]).then_inc(y_out[cc % 2], 16)

            def step(i, first):
                for cc in range(2):
                    if not first:
                        sp.wait_ge(hc_done, i * TB + G * (cc - 1) + 3)
                    for a in range(3):
                        sp.dma_start(stack[cc][32 * a:32 * a + 32, :, :, :].rearrange("p q t l -> p q (t l)"),
                                     partsd[i * 2 + cc, a].rearrange("i q t l -> i q (t l)")).then_inc(came[cc], 16)
                    for j in range(J):
                        sp.dma_start(b_rep[cc][N * j:N * j + N, :], bcd[i * 2 + cc, 0:N]).then_inc(came[cc], 16)
                    for j in range(J):
                        sp.dma_start(c_rep[cc][N * j:N * j + N, :], bcd[i * 2 + cc, N:2 * N]).then_inc(came[cc], 16)
                    sp.dma_start(rec[cc][:, :], recs[i * 2 + cc]).then_inc(came[cc], 16)
                    if not first:
                        store(i, cc)

            step(0, True)
            with sp.Fori(1, NI) as i:
                step(i, False)
            store(NI, 0)
            store(NI, 1)
            for k in range(2):
                sp.wait_ge(y_out[k], 16 * NI + 16)

        @block.tensor
        def _(pe):
            def spread(dst, cc, g, which):
                for lo, hi in pieces:
                    mm = pe.matmul(dst[:, lo:hi], keep["parts_sel"][:, g % 4, :, :].rearrange("p j n -> p (j n)"),
                                   stack[cc][:, g // 4, which, lo:hi], start=True, stop=True)
                return mm

            def sum_states(i, t):
                g, cc = t % G, (t % TB) // G
                pe.wait_ge(hc_done, i * TB + t + 1)
                if g == 0:
                    pe.wait_ge(y_read, i * 2 + t // G)
                for lo, hi in pieces:
                    mm = pe.matmul(ps_y[:, lo:hi], keep["sum_sel"][:, D - J - J * g:2 * D - J - J * g],
                                   hc[t % 4][:, lo:hi],
                                   start=g == 0, stop=g == G - 1)
                if g == G - 1:
                    mm.then_inc(y_full, 1)

            def step(i, first):
                for t in range(TB):
                    cc, g = divmod(t, G)
                    if g == 0:
                        pe.wait_ge(came[cc], i * (16 * LOADS) + 16 * LOADS)
                    if t or not first:
                        pe.wait_ge(bu_done, i * TB + t)
                    spread(ps_u, cc, g, 1).then_inc(u_full, 1)
                    if t >= 3 or not first:
                        sum_states(i, t - 3)
                    if t >= 2 or not first:
                        pe.wait_ge(scan_done, i * TB + t - 1)
                    spread(ps_d[t % 2], cc, g, 0).then_inc(d_full, 1)

            step(0, True)
            with pe.Fori(1, NI) as i:
                step(i, False)
            for t in range(-3, 0):
                sum_states(NI, t)

        @block.scalar
        def _(act):
            def read_y(i, cc):
                act.wait_ge(y_full, i * 2 + cc)
                act.wait_ge(y_out[(cc + 1) % 2], i * 16 + 16 * ((cc + 1) // 2))
                act.activation(y[(cc + 1) % 2][:, :], ps_y[:, 0:WC], ACT.Copy).then_inc(y_read, 1)

            def step(i, first):
                for t in range(TB):
                    cc, g = divmod(t, G)
                    if g == 0:
                        act.wait_ge(came[cc], i * (16 * LOADS) + 16 * LOADS)
                    act.wait_ge(d_full, i * TB + t + 1)
                    act.activation(ps_d[t % 2][:, 0:WC], ps_d[t % 2][:, 0:WC], ACT.Exp, scale=rec[cc][:, g:g + 1]).then_inc(exp_done, 1)
                    if t >= 2 or not first:
                        b = (t - 2) % TB
                        act.activation(h_last[:, b % G:b % G + 1], h[b % 4][:, WC - 1:WC], ACT.Copy,
                                       scale=rec[b // G][:, G:G + 1]).then_inc(zeroed, 1)
                    if g == 2 and (cc or not first):
                        read_y(i, cc)

            step(0, True)
            with act.Fori(1, NI) as i:
                step(i, False)
            read_y(NI, 0)

        @block.vector
        def _(dve):
            def scan(i, t):
                b = t % TB
                dve.wait_ge(exp_done, i * TB + t + 1)
                dve.tensor_tensor_scan(h[b % 4][:, :], ps_d[b % 2][:, 0:WC], bu[b % 4][:, :], h_last[:, b % G:b % G + 1],
                                       ALU.mult, ALU.add).then_inc(scan_done, 1)

            def step(i, first):
                for t in range(TB):
                    cc, g = divmod(t, G)
                    if g == 0:
                        dve.wait_ge(came[cc], i * (16 * LOADS) + 16 * LOADS)
                    dve.wait_ge(u_full, i * TB + t + 1)
                    dve.tensor_tensor(bu[t % 4][:, :], ps_u[:, 0:WC], b_rep[cc][:, :], ALU.mult).then_inc(bu_done, 1)
                    if t or not first:
                        scan(i, t - 1)

            dve.memset(h_last[:, :], 0.0).then_inc(zeroed, 1)
            dve.wait_ge(zeroed, 1)
            step(0, True)
            with dve.Fori(1, NI) as i:
                step(i, False)
            dve.wait_ge(bu_done, NI * TB)
            scan(NI, -1)

        @block.gpsimd
        def _(pool):
            with pool.Fori(0, NI) as i:
                for t in range(TB):
                    cc, g = divmod(t, G)
                    if g == 0:
                        pool.wait_ge(came[cc], i * (16 * LOADS) + 16 * LOADS)
                    pool.wait_ge(scan_done, i * TB + t + 1)
                    pool.tensor_tensor(hc[t % 4][:, :], h[t % 4][:, :], c_rep[cc][:, :], ALU.mult).then_inc(hc_done, 1)


def merge_phase(nc, P, keep, xs):
    LN = 3
    LAST = 14
    with ExitStack() as ctx:
        s = Space(nc, ctx, "merge")
        y4 = s.sb("y4", [128, 2, K, L])
        xn = s.sb("xn", [DM, 2, L])
        lane = lambda name, p=128: [s.sb(f"{name}{i}", [p, TT]) for i in range(LN)]
        a, b, yy, yc, sq, sd = (lane(n) for n in ("a", "b", "yy", "yc", "sq", "sd"))
        rs, ya, z = sd, sq, yc
        ps_s = [s.ps(f"ps_s{i}", [128, 512]) for i in range(LN)]
        ps_z = [s.ps(f"ps_z{i}", [128, 512]) for i in range(LN)]
        came = [s.sem(f"came{i}") for i in range(2)]
        link = [s.sem(f"link{i}") for i in range(LN)]
        gone = [s.sem(f"gone{i}") for i in range(LN)]
        TL = TPI // LN
        PU = TL * LAST
        block = ctx.enter_context(nc.Block())
        yd = P["y"].rearrange("u (k c) p l -> u k p c l", k=K)
        xnd = P["xn"].rearrange("b (r c) l -> (b r) c l", r=BR)
        zd = P["z"].rearrange("b (r c) l -> (b r) c l", r=BR)

        @block.sync
        def _(sp):
            for ln in range(LN):
                sp.sem_inc(link[ln], PU + 1)
                sp.sem_inc(gone[ln], 16)
            with sp.Fori(0, U // 2) as i:
                for k in range(2):
                    for ln in range(LN):
                        sp.wait_ge(link[ln], i * (2 * PU) + k * PU + 1)
                    for d in range(K):
                        sp.dma_start(y4[:, k, d, :].rearrange("p (c l) -> p c l", c=NCH), yd[i * 2 + k, d]).then_inc(came[k], 16)
                    sp.dma_start(xn[:, k, :], xnd[i * 2 + k]).then_inc(came[k], 16)

        @block.gpsimd
        def _(pool):
            with pool.Fori(0, U // 2) as i:
                for k in range(2):
                    pool.wait_ge(came[k], i * (16 * (K + 1)) + 16 * (K + 1))
                    for t in range(TPI):
                        ln, n = t % LN, k * PU + (t // LN) * LAST + PU + 1
                        pool.wait_ge(link[ln], i * (2 * PU) + n)
                        v1 = scan_order(y4[:, k, 1, :], 1, t * TT, TT)
                        v3 = scan_order(y4[:, k, 3, :], 3, t * TT, TT)
                        pool.tensor_tensor(like(b[ln][:, :], v1), v1, v3, ALU.add).then_inc(link[ln], 1)

        @block.vector
        def _(dve):
            with dve.Fori(0, U // 2) as i:
                for k in range(2):
                    dve.wait_ge(came[k], i * (16 * (K + 1)) + 16 * (K + 1))
                    for g in range(TL):
                        base = i * (2 * PU) + (k * PU + g * LAST + PU + 1)
                        for ln in range(LN):
                            at = (g * LN + ln) * TT
                            dve.wait_ge(link[ln], base + 1)
                            dve.tensor_tensor(a[ln][:, :], y4[:, k, 0, at:at + TT], scan_order(y4[:, k, 2, :], 2, at, TT), ALU.add).then_inc(link[ln], 1)
                        for ln in range(LN):
                            at = (g * LN + ln) * TT
                            dve.wait_ge(link[ln], base + 2)
                            dve.scalar_tensor_tensor(yy[ln][:, :], xs[:, bass.ds(i * (2 * L) + (k * L + at), TT)], keep["d_sum"][:, 0:1],
                                                     a[ln][:, :], ALU.mult, ALU.add).then_inc(link[ln], 1)
                        for ln in range(LN):
                            dve.wait_ge(link[ln], base + 3)
                            dve.tensor_tensor(a[ln][:, :], yy[ln][:, :], b[ln][:, :], ALU.add).then_inc(link[ln], 1)
                        for ln in range(LN):
                            dve.wait_ge(link[ln], base + 5)
                            dve.wait_ge(gone[ln], i * (32 * TL) + 16 * (k * TL + g) + 16)
                            dve.tensor_tensor(yc[ln][:, :], a[ln][:, :], ps_s[ln][:, 0:TT], ALU.subtract).then_inc(link[ln], 1)
                        for ln in range(LN):
                            dve.wait_ge(link[ln], base + 10)
                            dve.tensor_tensor(yy[ln][:, :], yc[ln][:, :], rs[ln][:, :], ALU.mult).then_inc(link[ln], 1)
                        for ln in range(LN):
                            at = (g * LN + ln) * TT
                            dve.wait_ge(link[ln], base + 13)
                            dve.scalar_tensor_tensor(z[ln][0:DM, :], xn[:, k, at:at + TT], keep["skip"][:, 0:1], ps_z[ln][0:DM, 0:TT],
                                                     ALU.mult, ALU.add).then_inc(link[ln], 1)

        @block.tensor
        def _(pe):
            with pe.Fori(0, U // 2) as i:
                for k in range(2):
                    for g in range(TL):
                        base = i * (2 * PU) + (k * PU + g * LAST + PU + 1)
                        for ln in range(LN):
                            pe.wait_ge(link[ln], base + 4)
                            pe.matmul(ps_s[ln][:, 0:TT], keep["ones_d"][:, :], a[ln][:, :], start=True, stop=True).then_inc(link[ln], 1)
                        for ln in range(LN):
                            pe.wait_ge(link[ln], base + 7)
                            pe.matmul(ps_s[ln][:, 0:TT], keep["ones_d"][:, :], sq[ln][:, :], start=True, stop=True).then_inc(link[ln], 1)
                        for ln in range(LN):
                            pe.wait_ge(link[ln], base + 12)
                            pe.matmul(ps_z[ln][0:DM, 0:TT], keep["out_W"][:, :], ya[ln][:, :], start=True, stop=True).then_inc(link[ln], 1)

        @block.scalar
        def _(act):
            with act.Fori(0, U // 2) as i:
                for k in range(2):
                    for g in range(TL):
                        base = i * (2 * PU) + (k * PU + g * LAST + PU + 1)
                        for ln in range(LN):
                            act.wait_ge(link[ln], base + 6)
                            act.activation(sq[ln][:, :], yc[ln][:, :], ACT.Square).then_inc(link[ln], 1)
                        for ln in range(LN):
                            act.wait_ge(link[ln], base + 8)
                            act.activation(sd[ln][:, :], ps_s[ln][:, 0:TT], ACT.Ln, bias=keep["eps"][:, 0:1]).then_inc(link[ln], 1)
                        for ln in range(LN):
                            act.wait_ge(link[ln], base + 9)
                            act.activation(rs[ln][:, :], sd[ln][:, :], ACT.Exp, scale=-0.5).then_inc(link[ln], 1)
                        for ln in range(LN):
                            act.wait_ge(link[ln], base + 11)
                            act.activation(ya[ln][:, :], yy[ln][:, :], ACT.Identity, scale=keep["onorm_g"][:, 0:1],
                                           bias=keep["onorm_b"][:, 0:1]).then_inc(link[ln], 1)
                        for ln in range(LN):
                            act.wait_ge(link[ln], base + 14)
                            act.dma_start(zd[i * 2 + k, :, (g * LN + ln) * TT:(g * LN + ln + 1) * TT], z[ln][0:DM, :]).then_inc(gone[ln], 16)
            for ln in range(LN):
                act.wait_ge(gone[ln], 16 * U * TL + 16)


def project_phase(nc, P, keep, f_hi, f_lo):
    LN = 2
    LAST = 17
    with ExitStack() as ctx:
        s = Space(nc, ctx, "proj")
        zn = s.sb("zn", [128, LN, 2, TT])
        x1, xc, sq, xh = (s.sb(n, [128, LN, 2, TT]) for n in ("x1", "xc", "sq", "xh"))
        sd, rs, ln2, lm, inv = (s.sb(n, [128, LN, TT]) for n in ("sd", "rs", "ln2", "lm", "inv"))
        ps_x = s.ps("ps_x", [128, LN, 2, 512])
        ps_s = s.ps("ps_s", [128, LN, 512])
        came = [s.sem(f"came{i}") for i in range(LN)]
        gone = [s.sem(f"gone{i}") for i in range(LN)]
        link = [s.sem(f"link{i}") for i in range(LN)]
        block = ctx.enter_context(nc.Block())
        zv = P["zn"].rearrange("b (h p) (i t) -> b i p h t", h=2, t=TT)
        at = lambda x, i, ln: x[:, :, bass.ds(i * (LN * TT) + ln * TT, TT)]
        both = lambda x: x.unsqueeze(1).to_broadcast([128, 2, TT])

        @block.sync
        def _(sp):
            for ln in range(LN):
                sp.sem_inc(link[ln], 1)
                sp.sem_inc(gone[ln], 16)
            with sp.Fori(0, B) as b:
                with sp.Fori(0, TPI // LN) as i:
                    for ln in range(LN):
                        sp.wait_ge(link[ln], b * (LAST * TPI // LN) + i * LAST + 1)
                        sp.dma_start(zn[:, ln, :, :], zv[b, i * LN + ln]).then_inc(came[ln], 16)
                    for ln in range(LN):
                        sp.wait_ge(link[ln], b * (LAST * TPI // LN) + i * LAST + 3)
                        sp.dma_start(P["x1"][b * TPI + i * LN + ln], x1[:, ln, :, :]).then_inc(gone[ln], 16)
            for ln in range(LN):
                sp.wait_ge(gone[ln], 16 * (NTT // LN) + 16)

        @block.tensor
        def _(pe):
            with pe.Fori(0, NTT // LN) as i:
                for ln in range(LN):
                    pe.wait_ge(came[ln], i * 16 + 16)
                    for o in range(2):
                        for h in range(2):
                            mm = pe.matmul(ps_x[:, ln, o, 0:TT], keep["proj_W"][:, h, o * 128:o * 128 + 128], zn[:, ln, h, :],
                                           start=h == 0, stop=h == 1)
                    mm.then_inc(link[ln], 1)
                for ln in range(LN):
                    pe.wait_ge(link[ln], i * LAST + 3)
                    for h in range(2):
                        mm = pe.matmul(ps_s[:, ln, 0:TT], keep["ones_c"][:, :], x1[:, ln, h, :], start=h == 0, stop=h == 1)
                    mm.then_inc(link[ln], 1)
                for ln in range(LN):
                    pe.wait_ge(link[ln], i * LAST + 6)
                    for h in range(2):
                        mm = pe.matmul(ps_s[:, ln, 0:TT], keep["ones_c"][:, :], sq[:, ln, h, :], start=h == 0, stop=h == 1)
                    mm.then_inc(link[ln], 1)
                for ln in range(LN):
                    pe.wait_ge(link[ln], i * LAST + 11)
                    for h in range(2):
                        mm = pe.matmul(ps_s[:, ln, 0:TT], keep["ones"][:, :], sq[:, ln, h, :], start=h == 0, stop=h == 1)
                    mm.then_inc(link[ln], 1)

        @block.scalar
        def _(act):
            with act.Fori(0, NTT // LN) as i:
                for ln in range(LN):
                    act.wait_ge(link[ln], i * LAST + 2)
                    act.wait_ge(gone[ln], i * 16 + 16)
                    for h in range(2):
                        last = act.activation(x1[:, ln, h, :], ps_x[:, ln, h, 0:TT], ACT.Identity, bias=keep["proj_b"][:, h:h + 1])
                    last.then_inc(link[ln], 1)
                for ln in range(LN):
                    act.wait_ge(link[ln], i * LAST + 5)
                    act.activation(sq[:, ln, :, :], xc[:, ln, :, :], ACT.Square).then_inc(link[ln], 1)
                for ln in range(LN):
                    act.wait_ge(link[ln], i * LAST + 7)
                    act.activation(sd[:, ln, :], ps_s[:, ln, 0:TT], ACT.Ln, bias=keep["eps"][:, 0:1]).then_inc(link[ln], 1)
                for ln in range(LN):
                    act.wait_ge(link[ln], i * LAST + 8)
                    act.activation(rs[:, ln, :], sd[:, ln, :], ACT.Exp, scale=-0.5).then_inc(link[ln], 1)
                for ln in range(LN):
                    act.wait_ge(link[ln], i * LAST + 10)
                    act.activation(sq[:, ln, :, :], xh[:, ln, :, :], ACT.Square).then_inc(link[ln], 1)
                for ln in range(LN):
                    act.wait_ge(link[ln], i * LAST + 13)
                    act.activation(ln2[:, ln, :], lm[:, ln, :], ACT.Ln, scale=2.0 ** 40).then_inc(link[ln], 1)
                for ln in range(LN):
                    act.wait_ge(link[ln], i * LAST + 14)
                    act.activation(inv[:, ln, :], ln2[:, ln, :], ACT.Exp, scale=-0.5, bias=keep["ln_2_20"][:, 0:1]).then_inc(link[ln], 1)
                for ln in range(LN):
                    act.wait_ge(link[ln], i * LAST + 16)
                    act.activation(at(f_hi, i, ln), xc[:, ln, :, :], ACT.Copy).then_inc(link[ln], 1)

        @block.vector
        def _(dve):
            with dve.Fori(0, NTT // LN) as i:
                for ln in range(LN):
                    dve.wait_ge(link[ln], i * LAST + 4)
                    dve.tensor_tensor(xc[:, ln, :, :], x1[:, ln, :, :], both(ps_s[:, ln, 0:TT]), ALU.subtract).then_inc(link[ln], 1)
                for ln in range(LN):
                    dve.wait_ge(link[ln], i * LAST + 9)
                    dve.tensor_tensor(xh[:, ln, :, :], xc[:, ln, :, :], both(rs[:, ln, :]), ALU.mult).then_inc(link[ln], 1)
                for ln in range(LN):
                    dve.wait_ge(link[ln], i * LAST + 12)
                    dve.tensor_scalar(lm[:, ln, :], ps_s[:, ln, 0:TT], 1e-24, None, ALU.max).then_inc(link[ln], 1)
                for ln in range(LN):
                    dve.wait_ge(link[ln], i * LAST + 15)
                    dve.tensor_tensor(xc[:, ln, :, :], xh[:, ln, :, :], both(inv[:, ln, :]), ALU.mult).then_inc(link[ln], 1)
                for ln in range(LN):
                    dve.wait_ge(link[ln], i * LAST + 17)
                    dve.tensor_tensor(at(f_lo, i, ln), xc[:, ln, :, :], at(f_hi, i, ln).bitcast(F32), ALU.subtract).then_inc(link[ln], 1)


def attention_phase(nc, keep, f_hi, f_lo, o_t, den):
    with ExitStack() as ctx:
        s = Space(nc, ctx, "attn")
        t_hi = s.sb("t_hi", [128, KB, C], F32R)
        t_lo = s.sb("t_lo", [128, KB, C], F32R)
        e = [s.sb(f"e{i}", [128, TT]) for i in range(4)]
        e_hi = [s.sb(f"e_hi{i}", [128, TT], F32R) for i in range(4)]
        e_lo = [s.sb(f"e_lo{i}", [128, TT], F32R) for i in range(4)]
        ps_s = [s.ps(f"ps_s{i}", [128, 512]) for i in range(4)]
        ps_o = s.ps("ps_o", [128, 2, 512])
        turned, moved = s.sem("turned"), s.sem("moved")
        hi_done, lo_done = s.sem("hi_done"), s.sem("lo_done")
        s_full, e_done, o_full, o_read = s.sem("s_full"), s.sem("e_done"), s.sem("o_full"), s.sem("o_read")
        block = ctx.enter_context(nc.Block())

        @block.tensor
        def _(pe):
            for n in range(KB):
                if n >= 4:
                    pe.wait_ge(moved, n - 3)
                f = f_hi if n < KB // 2 else f_lo
                for q in range(4):
                    j, h = 2 * (n % (KB // 2)) + q // 2, q % 2
                    mm = pe.transpose(ps_s[n % 4][:, q * 128:q * 128 + 128], f[:, h, j * 128:j * 128 + 128].bitcast(F32), keep["ident"][:, :])
                mm.then_inc(turned, 1)
            pe.wait_ge(moved, KB)

            def scores(q, j):
                for h in range(2):
                    keys, tokens = slice(j * 128, j * 128 + 128), bass.ds(q * TT, TT)
                    mm = products(pe, ps_s[j % 4][:, 0:TT], (f_hi[:, h, keys], f_hi[:, h, tokens]),
                                  (f_lo[:, h, keys], f_lo[:, h, tokens]), h == 0, h == 1)
                mm.then_inc(s_full, 1)

            pe.sem_inc(o_read, 1)
            with pe.Fori(0, NTT) as q:
                scores(q, 0)
                scores(q, 1)
                for j in range(KB):
                    if j + 2 < KB:
                        scores(q, j + 2)
                    if j == 0:
                        pe.wait_ge(o_read, q + 1)
                    pe.wait_ge(lo_done, q * KB + j + 1)
                    for o in range(2):
                        ch = slice(o * 128, o * 128 + 128)
                        mm = products(pe, ps_o[:, o, 0:TT], (t_hi[:, j, ch], e_hi[j % 4][:, :]),
                                      (t_lo[:, j, ch], e_lo[j % 4][:, :]), j == 0, j == KB - 1)
                mm.then_inc(o_full, 1)

        @block.scalar
        def _(act):
            with act.Fori(0, NTT) as q:
                for j in range(KB):
                    act.wait_ge(s_full, q * KB + j + 1)
                    act.activation(e[j % 4][:, :], ps_s[j % 4][:, 0:TT], ACT.Exp,
                                   accum_out=den[:, j, bass.ds(q, 1)]).then_inc(e_done, 1)

        @block.vector
        def _(dve):
            for n in range(KB):
                dve.wait_ge(turned, n + 1)
                t, j = (t_hi if n < KB // 2 else t_lo), 2 * (n % (KB // 2))
                dve.tensor_copy(t[:, j:j + 2, :].rearrange("p a c -> p (a c)"), ps_s[n % 4][:, :]).then_inc(moved, 1)
            with dve.Fori(0, NTT) as q:
                for j in range(KB):
                    dve.wait_ge(e_done, q * KB + j + 1)
                    dve.tensor_copy(e_hi[j % 4][:, :], e[j % 4][:, :]).then_inc(hi_done, 1)
                dve.wait_ge(o_full, q + 1)
                dve.tensor_copy(o_t[:, :, bass.ds(q * TT, TT)], ps_o[:, :, 0:TT]).then_inc(o_read, 1)

        @block.gpsimd
        def _(pool):
            with pool.Fori(0, NTT) as q:
                for j in range(KB):
                    pool.wait_ge(hi_done, q * KB + j + 1)
                    pool.tensor_tensor(e_lo[j % 4][:, :], e[j % 4][:, :], e_hi[j % 4][:, :].bitcast(F32), ALU.subtract).then_inc(lo_done, 1)


def blend_phase(nc, P, keep, f_hi, f_lo, o_t, den):
    LN = 2
    LAST = 19
    with ExitStack() as ctx:
        s = Space(nc, ctx, "blend")
        den_sum, den_inv, den_w = (s.sb(n, [128, KB]) for n in ("den_sum", "den_inv", "den_w"))
        dg = s.sb("dg", [128, LN, TT // 128, 128])
        aa, mm_, sq, xc = (s.sb(n, [128, LN, 2, TT]) for n in ("aa", "mm_", "sq", "xc"))
        ln2, lm, inv, sd, rs = (s.sb(n, [128, LN, TT]) for n in ("ln2", "lm", "inv", "sd", "rs"))
        ps_b = s.ps("ps_b", [128, LN, 512])
        ps_s = s.ps("ps_s", [128, LN, 512])
        summed = s.sem("summed")
        x1 = s.sb("x1", [128, LN, 2, TT])
        came = [s.sem(f"came{i}") for i in range(LN)]
        gone = [s.sem(f"gone{i}") for i in range(LN)]
        link = [s.sem(f"link{i}") for i in range(LN)]
        block = ctx.enter_context(nc.Block())
        at = lambda x, i, ln: x[:, :, bass.ds(i * (LN * TT) + ln * TT, TT)]
        both = lambda x: x.unsqueeze(1).to_broadcast([128, 2, TT])
        BL = TT // 128

        @block.sync
        def _(sp):
            for ln in range(LN):
                sp.sem_inc(gone[ln], 16)
            with sp.Fori(0, NTT // LN) as i:
                for ln in range(LN):
                    sp.wait_ge(gone[ln], i * 16 + 16)
                    sp.dma_start(x1[:, ln, :, :], P["x1"][i * LN + ln]).then_inc(came[ln], 16)
                for ln in range(LN):
                    sp.wait_ge(link[ln], i * LAST + 15)
                    sp.dma_start(P["x2"][i * LN + ln], x1[:, ln, :, :]).then_inc(gone[ln], 16)
            for ln in range(LN):
                sp.wait_ge(gone[ln], 16 * (NTT // LN) + 16)

        @block.vector
        def _(dve):
            dve.tensor_reduce(den_sum[:, :], den[:, :, :], AX.X, ALU.add).then_inc(summed, 1)
            dve.wait_ge(summed, 1)
            dve.reciprocal(den_inv[:, :], den_sum[:, :]).then_inc(summed, 1)
            dve.wait_ge(summed, 2)
            dve.tensor_scalar(den_w[:, :], den_inv[:, :], 1.0 - 0.8, None, ALU.mult).then_inc(summed, 1)
            dve.wait_ge(summed, 3)
            for ln in range(LN):
                dve.sem_inc(link[ln], 1)
            with dve.Fori(0, NTT // LN) as i:
                for ln in range(LN):
                    dve.wait_ge(link[ln], i * LAST + 1)
                    w = den_w[:, bass.ds(i * (LN * BL) + ln * BL, BL)].unsqueeze(2).to_broadcast([128, BL, 128])
                    eye = keep["ident"][:, :].unsqueeze(1).to_broadcast([128, BL, 128])
                    dve.tensor_tensor(dg[:, ln, :, :], eye, w, ALU.mult).then_inc(link[ln], 1)
                for ln in range(LN):
                    dve.wait_ge(link[ln], i * LAST + 3)
                    dve.tensor_tensor(aa[:, ln, :, :], at(o_t, i, ln), both(ps_b[:, ln, 0:TT]), ALU.mult).then_inc(link[ln], 1)
                for ln in range(LN):
                    dve.wait_ge(link[ln], i * LAST + 4)
                    dve.scalar_tensor_tensor(mm_[:, ln, :, :], at(f_lo, i, ln).bitcast(F32), 0.8, aa[:, ln, :, :], ALU.mult, ALU.add).then_inc(link[ln], 1)
                for ln in range(LN):
                    dve.wait_ge(link[ln], i * LAST + 5)
                    dve.scalar_tensor_tensor(mm_[:, ln, :, :], at(f_hi, i, ln).bitcast(F32), 0.8, mm_[:, ln, :, :], ALU.mult, ALU.add).then_inc(link[ln], 1)
                for ln in range(LN):
                    dve.wait_ge(link[ln], i * LAST + 8)
                    dve.tensor_scalar(lm[:, ln, :], ps_s[:, ln, 0:TT], 1e-24, None, ALU.max).then_inc(link[ln], 1)
                for ln in range(LN):
                    dve.wait_ge(link[ln], i * LAST + 11)
                    dve.tensor_tensor(aa[:, ln, :, :], mm_[:, ln, :, :], both(inv[:, ln, :]), ALU.mult).then_inc(link[ln], 1)
                for ln in range(LN):
                    dve.wait_ge(link[ln], i * LAST + 12)
                    dve.wait_ge(came[ln], i * 16 + 16)
                    dve.tensor_tensor(x1[:, ln, :, :], x1[:, ln, :, :], aa[:, ln, :, :], ALU.add).then_inc(link[ln], 1)
                for ln in range(LN):
                    dve.wait_ge(link[ln], i * LAST + 14)
                    dve.tensor_tensor(xc[:, ln, :, :], x1[:, ln, :, :], both(ps_s[:, ln, 0:TT]), ALU.subtract).then_inc(link[ln], 1)
                for ln in range(LN):
                    dve.wait_ge(link[ln], i * LAST + 19)
                    dve.tensor_tensor(at(o_t, i, ln), xc[:, ln, :, :], both(rs[:, ln, :]), ALU.mult).then_inc(link[ln], 1)

        @block.tensor
        def _(pe):
            with pe.Fori(0, NTT // LN) as i:
                for ln in range(LN):
                    pe.wait_ge(link[ln], i * LAST + 2)
                    pe.matmul(ps_b[:, ln, 0:TT], keep["ones"][:, :], dg[:, ln, :, :].rearrange("p a b -> p (a b)"),
                              start=True, stop=True).then_inc(link[ln], 1)
                for ln in range(LN):
                    pe.wait_ge(link[ln], i * LAST + 7)
                    for h in range(2):
                        mm = pe.matmul(ps_s[:, ln, 0:TT], keep["ones"][:, :], sq[:, ln, h, :], start=h == 0, stop=h == 1)
                    mm.then_inc(link[ln], 1)
                for ln in range(LN):
                    pe.wait_ge(link[ln], i * LAST + 13)
                    for h in range(2):
                        mm = pe.matmul(ps_s[:, ln, 0:TT], keep["ones_c"][:, :], x1[:, ln, h, :], start=h == 0, stop=h == 1)
                    mm.then_inc(link[ln], 1)
                for ln in range(LN):
                    pe.wait_ge(link[ln], i * LAST + 16)
                    for h in range(2):
                        mm = pe.matmul(ps_s[:, ln, 0:TT], keep["ones_c"][:, :], sq[:, ln, h, :], start=h == 0, stop=h == 1)
                    mm.then_inc(link[ln], 1)

        @block.scalar
        def _(act):
            with act.Fori(0, NTT // LN) as i:
                for ln in range(LN):
                    act.wait_ge(link[ln], i * LAST + 6)
                    act.activation(sq[:, ln, :, :], mm_[:, ln, :, :], ACT.Square).then_inc(link[ln], 1)
                for ln in range(LN):
                    act.wait_ge(link[ln], i * LAST + 9)
                    act.activation(ln2[:, ln, :], lm[:, ln, :], ACT.Ln, scale=2.0 ** 40).then_inc(link[ln], 1)
                for ln in range(LN):
                    act.wait_ge(link[ln], i * LAST + 10)
                    act.activation(inv[:, ln, :], ln2[:, ln, :], ACT.Exp, scale=-0.5, bias=keep["ln_2_20"][:, 0:1]).then_inc(link[ln], 1)
                for ln in range(LN):
                    act.wait_ge(link[ln], i * LAST + 15)
                    act.activation(sq[:, ln, :, :], xc[:, ln, :, :], ACT.Square).then_inc(link[ln], 1)
                for ln in range(LN):
                    act.wait_ge(link[ln], i * LAST + 17)
                    act.activation(sd[:, ln, :], ps_s[:, ln, 0:TT], ACT.Ln, bias=keep["eps"][:, 0:1]).then_inc(link[ln], 1)
                for ln in range(LN):
                    act.wait_ge(link[ln], i * LAST + 18)
                    act.activation(rs[:, ln, :], sd[:, ln, :], ACT.Exp, scale=-0.5).then_inc(link[ln], 1)


def gate_phase(nc, P, w, keep, xl, we):
    with ExitStack() as ctx:
        s = Space(nc, ctx, "gate")
        raw = [s.sb(f"raw{i}", [128, 2 * HF]) for i in range(3)]
        gw = s.sb("gw", [128, 2, E])
        gb = s.sb("gb", [128, E])
        cw_t = [s.sb(f"cw_t{i}", [E, 512]) for i in range(2)]
        small = lambda name, n=E, dt=F32: s.sb(name, [128, KB, n], dt)
        lg, top, dif, ex, cw, cw2 = (small(n) for n in ("lg", "top", "dif", "ex", "cw", "cw2"))
        idx = small("idx", E, U32)
        dif2, ex2, v2, pick = (small(n, 2) for n in ("dif2", "ex2", "v2", "pick"))
        sm, inv = small("sm", 1), small("inv", 1)
        iota = s.sb("iota", [128, E])
        ps_t = [s.ps(f"ps_t{i}", [128, 512]) for i in range(2)]
        ps_g = s.ps("ps_g", [128, 512])
        loaded, gate_full, step_done, ex_done = s.sem("loaded"), s.sem("gate_full"), s.sem("step_done"), s.sem("ex_done")
        iota_done, turned, moved, stored = s.sem("iota_done"), s.sem("turned"), s.sem("moved"), [s.sem("stored0"), s.sem("stored1")]
        raw_here = [s.sem(f"raw_here{i}") for i in range(3)]
        hi_cut, lo_cut, small_loads = s.sem("hi_cut"), s.sem("lo_cut"), s.sem("small_loads")
        srcs = []
        for e in range(E):
            srcs.append((w["W1"][e].rearrange("(h p) n -> p h n", h=2), 2, we["w1_hi"][:, e, :, :], we["w1_lo"][:, e, :, :]))
            srcs.append((w["W2"][e].rearrange("(h p) n -> p h n", h=HB), HB, we["w2_hi"][:, e, :, :], we["w2_lo"][:, e, :, :]))
        block = ctx.enter_context(nc.Block())
        wide = lambda x: x.to_broadcast([128, KB, E])

        @block.sync
        def _(sp):
            sp.dma_start(gw[:, :, :], w["gate_w"].rearrange("(h p) e -> p h e", h=2)).then_inc(loaded, 16)
            sp.dma_start(gb[:, :], w["gate_b"].partition_broadcast(128)).then_inc(loaded, 16)
            sp.dma_start(we["b2"][:, :], w["b2"]).then_inc(small_loads, 16)
            for e in range(E):
                sp.dma_start(we["b1"][:, e, :], w["b1"][e].rearrange("(h p) -> p h", h=HB), allow_slow_non_contiguous=True).then_inc(small_loads, 16)
            for n, (src, parts, _, _) in enumerate(srcs):
                if n >= 3:
                    sp.wait_ge(lo_cut, n - 2)
                sp.dma_start(raw[n % 3][:, :].rearrange("p (h n) -> p h n", h=parts), src).then_inc(raw_here[n % 3], 16)
            for n in range(KB // 4):
                sp.wait_ge(moved, n + 1)
                sp.dma_start(P["cw"][:, n * 512:n * 512 + 512], cw_t[n % 2][:, :]).then_inc(stored[n % 2], 16)
            for k in range(2):
                sp.wait_ge(stored[k], 16 * ((KB // 4 + 1 - k) // 2))
            sp.wait_ge(small_loads, 16 * (1 + E))

        @block.gpsimd
        def _(pool):
            for n in range(E):
                last = pool.memset(iota[:, n:n + 1], float(n))
            last.then_inc(iota_done, 1)
            for n, (_, parts, hi, lo) in enumerate(srcs):
                pool.wait_ge(hi_cut, n + 1)
                v = raw[n % 3][:, :].rearrange("p (h n) -> p h n", h=parts)
                pool.tensor_tensor(lo, v, hi.bitcast(F32), ALU.subtract).then_inc(lo_cut, 1)

        @block.tensor
        def _(pe):
            pe.wait_ge(loaded, 32)
            for j in range(KB):
                for h in range(2):
                    mm = pe.matmul(ps_g[:, j * E:j * E + E], xl[:, h, j * 128:j * 128 + 128], gw[:, h, :], start=h == 0, stop=h == 1)
            mm.then_inc(gate_full, 1)
            pe.wait_ge(step_done, 12)
            for n in range(KB // 4):
                if n >= 2:
                    pe.wait_ge(moved, n - 1)
                for q in range(4):
                    j = 4 * n + q
                    mm = pe.transpose(ps_t[n % 2][0:E, q * 128:q * 128 + 128], cw[:, j, :], keep["ident"][:, :])
                mm.then_inc(turned, 1)

        @block.scalar
        def _(act):
            for n, (_, parts, hi, _) in enumerate(srcs):
                if n == 8:
                    act.wait_ge(step_done, 3)
                    act.activation(ex[:, :, :], dif[:, :, :], ACT.Exp).then_inc(ex_done, 1)
                    act.activation(ex2[:, :, :], dif2[:, :, :], ACT.Exp).then_inc(ex_done, 1)
                act.wait_ge(raw_here[n % 3], 16 * (n // 3 + 1))
                act.activation(hi, raw[n % 3][:, :].rearrange("p (h n) -> p h n", h=parts), ACT.Copy).then_inc(hi_cut, 1)

        @block.vector
        def _(dve):
            dve.wait_ge(gate_full, 1)
            logits = ps_g[:, 0:KB * E].rearrange("p (j e) -> p j e", e=E)
            dve.tensor_tensor(lg[:, :, :], logits, gb[:, :].unsqueeze(1).to_broadcast([128, KB, E]), ALU.add).then_inc(step_done, 1)
            dve.wait_ge(step_done, 1)
            for j in range(KB):
                last = dve.max(top[:, j, :], lg[:, j, :])
            last.then_inc(step_done, 1)
            dve.wait_ge(step_done, 2)
            dve.tensor_tensor(dif[:, :, :], lg[:, :, :], wide(top[:, :, 0:1]), ALU.subtract)
            dve.tensor_tensor(dif2[:, :, :], top[:, :, 0:2], top[:, :, 0:1].to_broadcast([128, KB, 2]), ALU.subtract).then_inc(step_done, 1)
            for j in range(KB):
                last = dve.max_index(idx[:, j, :], top[:, j, :], lg[:, j, :])
            last.then_inc(step_done, 1)
            dve.wait_ge(step_done, 4)
            dve.tensor_copy(pick[:, :, :], idx[:, :, 0:2]).then_inc(step_done, 1)
            dve.wait_ge(ex_done, 2)
            dve.tensor_reduce(sm[:, :, :], ex[:, :, :], AX.X, ALU.add).then_inc(step_done, 1)
            dve.wait_ge(step_done, 6)
            dve.reciprocal(inv[:, :, :], sm[:, :, :]).then_inc(step_done, 1)
            dve.wait_ge(step_done, 7)
            dve.tensor_tensor(v2[:, :, :], ex2[:, :, :], inv[:, :, :].to_broadcast([128, KB, 2]), ALU.mult).then_inc(step_done, 1)
            dve.wait_ge(step_done, 8)
            dve.wait_ge(iota_done, 1)
            num = iota[:, :].unsqueeze(1).to_broadcast([128, KB, E])
            dve.tensor_tensor(cw[:, :, :], num, wide(pick[:, :, 0:1]), ALU.is_equal)
            dve.tensor_tensor(cw2[:, :, :], num, wide(pick[:, :, 1:2]), ALU.is_equal).then_inc(step_done, 1)
            dve.wait_ge(step_done, 9)
            dve.tensor_tensor(cw[:, :, :], cw[:, :, :], wide(v2[:, :, 0:1]), ALU.mult).then_inc(step_done, 1)
            dve.tensor_tensor(cw2[:, :, :], cw2[:, :, :], wide(v2[:, :, 1:2]), ALU.mult).then_inc(step_done, 1)
            dve.wait_ge(step_done, 11)
            dve.tensor_tensor(cw[:, :, :], cw[:, :, :], cw2[:, :, :], ALU.add).then_inc(step_done, 1)
            for n in range(KB // 4):
                dve.wait_ge(turned, n + 1)
                if n >= 2:
                    dve.wait_ge(stored[n % 2], 16 * (n // 2))
                dve.tensor_copy(cw_t[n % 2][:, :], ps_t[n % 2][0:E, :]).then_inc(moved, 1)


def expert_phase(nc, P, keep, xl, we, out):
    with ExitStack() as ctx:
        s = Space(nc, ctx, "moe")
        cw = s.sb("cw", [E, 2, TT])
        x2 = s.sb("x2", [128, 2, 2, TT])
        x_hi = s.sb("x_hi", [128, 2, TT], F32R)
        x_lo = s.sb("x_lo", [128, 2, TT], F32R)
        ring = lambda name, dt=F32: [s.sb(f"{name}{i}", [128, TT], dt) for i in range(4)]
        hg, h_hi, h_lo = ring("hg"), ring("h_hi", F32R), ring("h_lo", F32R)
        ps_h = [s.ps(f"ps_h{i}", [128, 512]) for i in range(4)]
        ps_w = [s.ps(f"ps_w{i}", [128, 512]) for i in range(2)]
        ps_o = s.ps("ps_o", [128, 2, 512])
        here = [s.sem(f"here{k}") for k in range(2)]
        x_cut, h_full, g_done, w_full, hw_done, hi_done, lo_done, o_full, o_read = (
            s.sem(n) for n in ("x_cut", "h_full", "g_done", "w_full", "hw_done", "hi_done", "lo_done", "o_full", "o_read"))
        gone = [s.sem(f"gone{k}") for k in range(2)]
        M = E * HB
        block = ctx.enter_context(nc.Block())
        ov = out.rearrange("b (h p) y x -> b p h (y x)", h=2)

        @block.sync
        def _(sp):
            def load(t, k):
                sp.wait_ge(gone[k], t * 8 + (16 - 8 * k))
                sp.dma_start(cw[:, k, :], P["cw"][:, bass.ds(t * TT, TT)]).then_inc(here[k], 16)
                sp.dma_start(x2[:, k, :, :], P["x2"][t]).then_inc(here[k], 16)

            def image(b, last):
                for n in range(TPI):
                    if not last or n + 1 < TPI:
                        load(b * TPI + (n + 1), (n + 1) % 2)
                    sp.wait_ge(o_read, b * TPI + n + 3)
                    sp.dma_start(ov[b, :, :, n * TT:n * TT + TT], x2[:, n % 2, :, :]).then_inc(gone[n % 2], 16)

            sp.sem_inc(o_read, 2)
            for k in range(2):
                sp.sem_inc(gone[k], 16)
            load(0, 0)
            with sp.Fori(0, B - 1) as b:
                image(b, False)
            image(B - 1, True)
            for k in range(2):
                sp.wait_ge(gone[k], 16 * (NTT // 2) + 16)

        @block.tensor
        def _(pe):
            def up(k, m):
                e, hb = divmod(m, HB)
                for h in range(2):
                    cols = slice(hb * 128, hb * 128 + 128)
                    mm = products(pe, ps_h[m % 4][:, 0:TT], (we["w1_hi"][:, e, h, cols], x_hi[:, h, :]),
                                  (we["w1_lo"][:, e, h, cols], x_lo[:, h, :]), h == 0, h == 1)
                mm.then_inc(h_full, 1)
                if hb == 0:
                    pe.matmul(ps_w[e % 2][:, 0:TT], keep["exp_sel"][:, e, :], cw[:, k, :], start=True, stop=True).then_inc(w_full, 1)

            def start(i, k):
                pe.wait_ge(x_cut, i * 4 + 2 * k + 2)
                pe.wait_ge(here[k % 2], i * 32 + 32 * (k // 2) + 32)
                up(k % 2, 0)

            def pair(i, last):
                for k in range(2):
                    up(k, 1)
                    pe.wait_ge(o_read, i * 2 + k + 2)
                    for o in range(2):
                        pe.matmul(ps_o[:, o, 0:TT], we["b2"][:, o * 128:o * 128 + 128], cw[:, k, :], start=True, stop=False)
                    for m in range(M):
                        e, hb = divmod(m, HB)
                        if m + 2 < M:
                            up(k, m + 2)
                        elif m == M - 1 and not (last and k):
                            start(i, k + 1)
                        pe.wait_ge(lo_done, i * (2 * M) + k * M + m + 1)
                        for o in range(2):
                            cols = slice(o * 128, o * 128 + 128)
                            mm = products(pe, ps_o[:, o, 0:TT], (we["w2_hi"][:, e, hb, cols], h_hi[m % 4][:, :]),
                                          (we["w2_lo"][:, e, hb, cols], h_lo[m % 4][:, :]), False, m == M - 1)
                    mm.then_inc(o_full, 1)

            start(0, 0)
            with pe.Fori(0, NTT // 2 - 1) as i:
                pair(i, False)
            pair(NTT // 2 - 1, True)

        @block.scalar
        def _(act):
            def cut(t):
                act.activation(x_hi[:, :, :], xl[:, :, bass.ds(t * TT, TT)], ACT.Copy).then_inc(x_cut, 1)

            def high(t, m):
                act.wait_ge(hw_done, t * M + m + 1)
                act.activation(h_hi[m % 4][:, :], hg[m % 4][:, :], ACT.Copy).then_inc(hi_done, 1)

            def tile(t, last):
                for m in range(M):
                    e, hb = divmod(m, HB)
                    act.wait_ge(h_full, t * M + m + 1)
                    act.activation(hg[m % 4][:, :], ps_h[m % 4][:, 0:TT], ACT.Gelu, bias=we["b1"][:, e, hb:hb + 1]).then_inc(g_done, 1)
                    if m == M - 1 and not last:
                        cut(t + 1)
                    if m:
                        high(t, m - 1)
                high(t, M - 1)

            cut(0)
            with act.Fori(0, NTT - 1) as t:
                tile(t, False)
            tile(NTT - 1, True)

        @block.gpsimd
        def _(pool):
            pool.sem_inc(hi_done, 1)
            with pool.Fori(0, NTT) as i:
                for m in range(M):
                    pool.wait_ge(hi_done, i * M + m + 2)
                    pool.tensor_tensor(h_lo[m % 4][:, :], hg[m % 4][:, :], h_hi[m % 4][:, :].bitcast(F32), ALU.subtract).then_inc(lo_done, 1)

        @block.vector
        def _(dve):
            def cut(t):
                dve.wait_ge(x_cut, t * 2 + 1)
                dve.tensor_tensor(x_lo[:, :, :], xl[:, :, bass.ds(t * TT, TT)], x_hi[:, :, :].bitcast(F32), ALU.subtract).then_inc(x_cut, 1)

            def pair(i, last):
                for k in range(2):
                    for m in range(M):
                        e, hb = divmod(m, HB)
                        if hb == 0:
                            dve.wait_ge(w_full, i * (2 * E) + k * E + e + 1)
                        dve.wait_ge(g_done, i * (2 * M) + k * M + m + 1)
                        dve.tensor_tensor(hg[m % 4][:, :], hg[m % 4][:, :], ps_w[e % 2][:, 0:TT], ALU.mult).then_inc(hw_done, 1)
                    if not (last and k):
                        cut(i * 2 + (k + 1))
                    dve.wait_ge(o_full, i * 2 + k + 1)
                    dve.wait_ge(here[k], i * 32 + 32)
                    dve.tensor_tensor(x2[:, k, :, :], ps_o[:, :, 0:TT], x2[:, k, :, :], ALU.add).then_inc(o_read, 1)

            cut(0)
            with dve.Fori(0, NTT // 2 - 1) as i:
                pair(i, False)
            pair(NTT // 2 - 1, True)


def conv_attn_hybrid_kernel(nc, x, w0, w1, out):
    dram = lambda name, shape, dt=F32: nc.dram_tensor(name, shape, dt).ap()
    P = {
        "xn": dram("xn_dram", (B, C, L)),
        "rec": dram("rec_dram", (U, STEPS, 128, G + 1)),
        "parts": dram("parts_dram", (U, STEPS, 3, 128, 2, WC), BF16),
        "bc": dram("bc_dram", (U, STEPS, 2 * N, WC)),
        "y": dram("y_dram", (U, STEPS, 128, WC)),
        "z": dram("z_dram", (B, C, L)),
        "zn": dram("zn_dram", (B, C, L)),
        "x1": dram("x1_dram", (NTT, 128, 2, TT)),
        "x2": dram("x2_dram", (NTT, 128, 2, TT)),
        "cw": dram("cw_dram", (E, NT)),
    }
    with ExitStack() as ctx:
        s = Space(nc, ctx, "keep")
        shapes = {
            "ident": [128, 128], "ones_c": [128, 128], "ones": [128, 128], "eps": [128, 1], "ln_2_20": [128, 1],
            "exp_sel": [E, E, 128], "ln_g": [128, 2], "ln_b": [128, 2], "proj_b": [128, 2], "proj_W": [128, 2, C],
        }
        scan_shapes = {
            "ones_d": [128, 128], "sum_sel": [128, 2 * D - J], "rec": [128, STEPS, G + 1],
            "w_eff": [128, K, D], "w_bc": [128, K, 2 * N], "w_pair": [128, 3, D], "w_one": [DM, 3, D],
            "dt_b": [D, K], "conv_b": [D, 1], "onorm_g": [D, 1], "onorm_b": [D, 1], "out_W": [D, DM], "d_sum": [D, 1],
            "skip": [DM, 1],
        }
        keep = {name: s.sb(name, shape) for name, shape in shapes.items()}
        with ExitStack() as mamba:
            m = Space(nc, mamba, "layer0")
            keep |= {name: m.sb(name, shape) for name, shape in scan_shapes.items()}
            keep["parts_sel"] = m.sb("parts_sel", [96, 4, J, N], BF16)
            setup_phase(nc, P, w0, keep)
            norm_phase(nc, "norm0", x.rearrange("b c y x -> b c (y x)"), P["xn"], keep)
            xs = m.sb("xs", [128, U * L])
            conv_phase(nc, P, keep, xs)
            delta_phase(nc, P, keep, xs)
            scan_phase(nc, P, keep)
            merge_phase(nc, P, keep, xs)
        norm_phase(nc, "norm1", P["z"], P["zn"], keep)
        o_t = s.sb("o_t", [128, 2, NT])
        with ExitStack() as attn:
            f_hi, f_lo = (attn.enter_context(nc.sbuf_tensor(n, [128, 2, NT], F32R)) for n in ("f_hi", "f_lo"))
            den = attn.enter_context(nc.sbuf_tensor("den", [128, KB, NTT], F32))
            project_phase(nc, P, keep, f_hi, f_lo)
            attention_phase(nc, keep, f_hi, f_lo, o_t, den)
            blend_phase(nc, P, keep, f_hi, f_lo, o_t, den)
        we = {n: s.sb(n, [128, E, 2, HF], F32R) for n in ("w1_hi", "w1_lo")}
        we |= {n: s.sb(n, [128, E, HB, C], F32R) for n in ("w2_hi", "w2_lo")}
        we["b1"], we["b2"] = s.sb("b1", [128, E, HB]), s.sb("b2", [E, C])
        gate_phase(nc, P, w1, keep, o_t, we)
        expert_phase(nc, P, keep, o_t, we, out)


_L0 = ["ln_g", "ln_b", "skip_scale", "proj_W", "proj_b", "in_W", "conv_W", "conv_b", "x_proj_W", "dt_W", "dt_b",
       "A_logs", "Ds", "onorm_g", "onorm_b", "out_W"]
_L1 = ["gate_w", "gate_b", "W1", "b1", "W2", "b2"]


def kernel(**inputs):
    import numpy as _np
    import concourse.bacc as _bacc
    from concourse.bass_utils import run_bass_kernel_spmd as _run

    nc = _bacc.Bacc("TRN2", target_bir_lowering=False, num_devices=1)
    arrays, args = {}, {}
    for name, value in inputs.items():
        a = _np.ascontiguousarray(value)
        arrays[f"in_{name}"] = a
        args[name] = nc.dram_tensor(f"in_{name}", a.shape, mybir.dt.from_np(a.dtype), kind="ExternalInput").ap()
    out = nc.dram_tensor("out_x", (B, C, H, W), F32, kind="ExternalOutput").ap()
    conv_attn_hybrid_kernel(nc, args["x"], {n: args[f"L0_conv_{n}"] for n in _L0}, {n: args[f"L1_ffn_{n}"] for n in _L1}, out)
    r = _run(nc, [arrays], core_ids=[0])
    return r.results[0]["out_x"]
```

```python
import math
from contextlib import ExitStack

import concourse.bass as bass
from concourse import mybir

F32 = mybir.dt.float32
BF16 = mybir.dt.bfloat16
F32R = mybir.dt.float32r
U32 = mybir.dt.uint32
ALU = mybir.AluOpType
ACT = mybir.ActivationFunctionType
AX = mybir.AxisListType

B, C, H, W = 2, 256, 48, 48
L = H * W
NT = B * L
BR = 4
U = B * BR
DM = C // BR
D = 128
K = 4
R, N = 4, 16
WC = 768
NCH = L // WC
HW_ = WC // 2
STEPS = K * NCH
NKC = U * STEPS
J = 128 // N
G = D // J
TT = 384
NTT = NT // TT
TPI = L // TT
KB = NT // 128
E, HF = 8, 512
HB = HF // 128


class Space:

    def __init__(self, nc, ctx, tag):
        self.nc, self.ctx, self.tag = nc, ctx, tag

    def sb(self, name, shape, dt=F32):
        return self.ctx.enter_context(self.nc.sbuf_tensor(f"{self.tag}_{name}", shape, dt))

    def ps(self, name, shape, dt=F32):
        return self.ctx.enter_context(self.nc.psum_tensor(f"{self.tag}_{name}", shape, dt))

    def sem(self, name):
        return self.ctx.enter_context(self.nc.semaphore(f"{self.tag}_{name}"))


def products(pe, out, highs, lows, start, stop):
    (wh, xh), (wl, xl) = highs, lows
    pe.matmul(out, wl, xh, start=start, stop=False)
    pe.matmul(out, wh, xl, start=False, stop=False)
    return pe.matmul(out, wh, xh, start=False, stop=stop)


def setup_phase(nc, P, w, keep):
    with ExitStack() as ctx:
        s = Space(nc, ctx, "setup")
        dts_rows = s.sb("dts_rows", [R, K, D])
        dtw_t = s.sb("dtw_t", [R, K, D])
        bc_rows = s.sb("bc_rows", [2 * N, K, D])
        conv_taps = s.sb("conv_taps", [128, D, 9])
        in_w2 = s.sb("in_w2", [128, D])
        ds4 = s.sb("ds4", [D, K])
        a_log = s.sb("a_log", [128, K, G])
        a_exp = s.sb("a_exp", [128, K, G])
        sel_f32 = s.sb("sel_f32", [64, 4, J, N])
        ps_w = s.ps("ps_w", [128, 4, 512])
        loaded, ones_set, ident_set = s.sem("loaded"), s.sem("ones_set"), s.sem("ident_set")
        weff_ps, bc_ps, exp_done, a_done = s.sem("weff_ps"), s.sem("bc_ps"), s.sem("exp_done"), s.sem("a_done")
        rec_out, pool_set, dve_done = s.sem("rec_out"), s.sem("pool_set"), s.sem("dve_done")
        loads = []
        loads.append((dts_rows[:, :, :], w["x_proj_W"][:, 0:R, :].rearrange("k c d -> c k d")))
        loads.append((dtw_t[:, :, :], w["dt_W"].rearrange("k d r -> r k d")))
        loads.append((bc_rows[:, :, :], w["x_proj_W"][:, R:, :].rearrange("k c d -> c k d")))
        for half in range(2):
            loads.append((in_w2[64 * half:64 * half + 64, :], w["in_W"]))
        loads.append((conv_taps[:, :, :], w["conv_W"].rearrange("d a y x -> (a d) (y x)").partition_broadcast(128)))
        loads.append((ds4[:, :], w["Ds"].rearrange("(k d) -> d k", k=K)))
        loads.append((keep["dt_b"][:, :], w["dt_b"].rearrange("k d -> d k")))
        loads.append((keep["conv_b"][:, :], w["conv_b"].rearrange("(d a) -> d a", a=1)))
        loads.append((keep["onorm_g"][:, :], w["onorm_g"].rearrange("(d a) -> d a", a=1)))
        loads.append((keep["onorm_b"][:, :], w["onorm_b"].rearrange("(d a) -> d a", a=1)))
        loads.append((keep["out_W"][:, :], w["out_W"]))
        loads.append((keep["ln_g"][:, :], w["ln_g"].rearrange("(h p) -> p h", h=2)))
        loads.append((keep["ln_b"][:, :], w["ln_b"].rearrange("(h p) -> p h", h=2)))
        loads.append((keep["proj_b"][:, :], w["proj_b"].rearrange("(h p) -> p h", h=2)))
        loads.append((keep["proj_W"][:, :, :], w["proj_W"].rearrange("(h p) n -> p h n", h=2)))
        loads.append((keep["skip"][:, :], w["skip_scale"].partition_broadcast(64)))
        a_src = w["A_logs"].rearrange("(k g j) n -> j n k g", k=K, j=J)
        for j in range(J):
            for k in range(K):
                loads.append((a_log[N * j:N * j + N, k, :], a_src[j, :, k, :]))
        n_loads = len(loads)
        block = ctx.enter_context(nc.Block())

        @block.sync
        def _(sp):
            for dst, src in loads:
                sp.dma_start(dst, src, allow_slow_non_contiguous=True).then_inc(loaded, 16)
            sp.wait_ge(a_done, 1)
            sp.wait_ge(dve_done, 1)
            with sp.Fori(0, U) as u:
                sp.dma_start(P["rec"][u].rearrange("s p f -> p s f"), keep["rec"][:, :, :]).then_inc(rec_out, 16)
            sp.wait_ge(rec_out, 16 * U)

        @block.gpsimd
        def _(pool):
            pool.memset(keep["ident"][:, :], 0.0).then_inc(ones_set, 1)
            pool.memset(keep["ones_c"][:, :], 1.0 / C).then_inc(pool_set, 1)
            pool.memset(keep["ones_d"][:, :], 1.0 / D).then_inc(pool_set, 1)
            pool.memset(keep["ones"][:, :], 1.0).then_inc(pool_set, 1)
            pool.memset(keep["eps"][:, :], 1e-5).then_inc(pool_set, 1)
            pool.memset(keep["ln_2_20"][:, :], 20 * math.log(2.0))
            pool.memset(sel_f32[:, :, :, :], 0.0).then_inc(ones_set, 1)
            pool.memset(keep["sum_sel"][:, :], 1.0).then_inc(ones_set, 1)
            pool.memset(keep["exp_sel"][:, :, :], 0.0).then_inc(ones_set, 1)
            pool.wait_ge(ones_set, 4)
            pool.affine_select(out=keep["ident"][:, :], in_=keep["ident"][:, :], compare_op=ALU.not_equal,
                               fill=1.0, base=0, pattern=[[-1, 128]], channel_multiplier=1).then_inc(ident_set, 1)
            for part in range(2):
                pool.wait_ge(ident_set, part + 1)
                v = sel_f32[:, :, :, :]
                pool.affine_select(out=v, in_=v, compare_op=ALU.not_equal, fill=1.0, base=-32 * part,
                                   pattern=[[-J, 4], [-1, J], [0, N]], channel_multiplier=1).then_inc(ident_set, 1)
            v = keep["sum_sel"][:, :]
            pool.affine_select(out=v, in_=v, compare_op=ALU.is_ge, fill=0.0, base=N * (D - J),
                               pattern=[[-N, 2 * D - J]], channel_multiplier=1).then_inc(ident_set, 1)
            pool.wait_ge(ident_set, 4)
            pool.tensor_copy(keep["parts_sel"][:, :, :, :], sel_f32[:, :, :, :])
            pool.affine_select(out=v, in_=v, compare_op=ALU.is_ge, fill=0.0, base=N - 1 - N * (D - J),
                               pattern=[[N, 2 * D - J]], channel_multiplier=-1).then_inc(ident_set, 1)
            v = keep["exp_sel"][:, :, :]
            pool.affine_select(out=v, in_=v, compare_op=ALU.not_equal, fill=1.0, base=0,
                               pattern=[[-1, E], [0, 128]], channel_multiplier=1).then_inc(ident_set, 1)

        @block.tensor
        def _(pe):
            pe.wait_ge(loaded, 16 * n_loads)
            for k in range(K):
                mm = pe.matmul(ps_w[:, k, 0:D], dts_rows[:, k, :], dtw_t[:, k, :], start=True, stop=True)
            mm.then_inc(weff_ps, 1)
            pe.wait_ge(ident_set, 1)
            pe.wait_ge(dve_done, 1)
            for k in range(K):
                mm = pe.transpose(ps_w[:, k, 256:256 + 2 * N], bc_rows[:, k, :], keep["ident"][0:2 * N, 0:2 * N])
            mm.then_inc(bc_ps, 1)

        @block.scalar
        def _(act):
            act.wait_ge(loaded, 16 * n_loads)
            act.activation(a_exp[:, :, :], a_log[:, :, :], ACT.Exp).then_inc(exp_done, 1)

        @block.vector
        def _(dve):
            dve.memset(keep["rec"][:, :, G:G + 1], 1.0).then_inc(pool_set, 1)
            dve.wait_ge(weff_ps, 1)
            dve.tensor_copy(keep["w_eff"][:, :, :], ps_w[:, :, 0:D]).then_inc(dve_done, 1)
            dve.wait_ge(exp_done, 1)
            dve.wait_ge(pool_set, 5)
            for c in range(NCH):
                rec = keep["rec"][:, :, :].rearrange("p (k c) f -> p k c f", c=NCH)
                last = dve.tensor_scalar(rec[:, :, c, 0:G], a_exp[:, :, :], -1.0, None, ALU.mult)
            dve.memset(rec[:, :, NCH - 1, G:G + 1], 0.0).then_inc(a_done, 1)
            for dy in range(3):
                for half in range(2):
                    p = slice(64 * half, 64 * half + 64)
                    dve.tensor_tensor(keep["w_pair"][p, dy, :], in_w2[p, :], conv_taps[p, :, 3 * dy + half], ALU.mult)
                dve.tensor_tensor(keep["w_one"][:, dy, :], in_w2[0:64, :], conv_taps[0:64, :, 3 * dy + 2], ALU.mult)
            dve.tensor_reduce(keep["d_sum"][:, :], ds4[:, :], AX.X, ALU.add)
            dve.wait_ge(bc_ps, 1)
            dve.tensor_copy(keep["w_bc"][:, :, :], ps_w[:, :, 256:256 + 2 * N])


def norm_phase(nc, tag, src, dst, keep):
    LN = 6
    with ExitStack() as ctx:
        s = Space(nc, ctx, tag)
        x = s.sb("x", [128, LN, 2, TT])
        xc = s.sb("xc", [128, LN, 2, TT])
        sq = s.sb("sq", [128, LN, 2, TT])
        sd = s.sb("sd", [128, LN, TT])
        rs = s.sb("rs", [128, LN, TT])
        ps_m = s.ps("ps_m", [128, LN, 512])
        ps_v = ps_m
        came = [s.sem(f"came{i}") for i in range(LN)]
        link = [s.sem(f"link{i}") for i in range(LN)]
        gone = [s.sem(f"gone{i}") for i in range(LN)]
        STEP = 8
        block = ctx.enter_context(nc.Block())
        sv = src.rearrange("b (h p) (i t) -> b i p h t", h=2, t=TT)
        dv = dst.rearrange("b (h p) (i t) -> b i p h t", h=2, t=TT)

        @block.sync
        def _(sp):
            for ln in range(LN):
                sp.sem_inc(link[ln], 1)
                sp.sem_inc(gone[ln], 16)
            with sp.Fori(0, B) as b:
                with sp.Fori(0, TPI // LN) as i:
                    for ln in range(LN):
                        sp.wait_ge(link[ln], b * (STEP * TPI // LN) + i * STEP + 1)
                        sp.dma_start(x[:, ln, :, :], sv[b, i * LN + ln]).then_inc(came[ln], 16)
                    for ln in range(LN):
                        sp.wait_ge(link[ln], b * (STEP * TPI // LN) + i * STEP + STEP + 1)
                        sp.dma_start(dv[b, i * LN + ln], sq[:, ln, :, :]).then_inc(gone[ln], 16)
            for ln in range(LN):
                sp.wait_ge(gone[ln], 16 * (NTT // LN) + 16)

        @block.tensor
        def _(pe):
            with pe.Fori(0, NTT // LN) as i:
                for ln in range(LN):
                    pe.wait_ge(came[ln], i * 16 + 16)
                    for h in range(2):
                        mm = pe.matmul(ps_m[:, ln, 0:TT], keep["ones_c"][:, :], x[:, ln, h, :], start=h == 0, stop=h == 1)
                    mm.then_inc(link[ln], 1)
                for ln in range(LN):
                    pe.wait_ge(link[ln], i * STEP + 4)
                    for h in range(2):
                        mm = pe.matmul(ps_v[:, ln, 0:TT], keep["ones_c"][:, :], sq[:, ln, h, :], start=h == 0, stop=h == 1)
                    mm.then_inc(link[ln], 1)

        @block.vector
        def _(dve):
            with dve.Fori(0, NTT // LN) as i:
                for ln in range(LN):
                    dve.wait_ge(link[ln], i * STEP + 2)
                    mean = ps_m[:, ln, 0:TT].unsqueeze(1).to_broadcast([128, 2, TT])
                    dve.tensor_tensor(xc[:, ln, :, :], x[:, ln, :, :], mean, ALU.subtract).then_inc(link[ln], 1)
                for ln in range(LN):
                    dve.wait_ge(link[ln], i * STEP + 7)
                    inv = rs[:, ln, :].unsqueeze(1).to_broadcast([128, 2, TT])
                    dve.tensor_tensor(xc[:, ln, :, :], xc[:, ln, :, :], inv, ALU.mult).then_inc(link[ln], 1)

        @block.scalar
        def _(act):
            with act.Fori(0, NTT // LN) as i:
                for ln in range(LN):
                    act.wait_ge(link[ln], i * STEP + 3)
                    act.wait_ge(gone[ln], i * 16 + 16)
                    act.activation(sq[:, ln, :, :], xc[:, ln, :, :], ACT.Square).then_inc(link[ln], 1)
                for ln in range(LN):
                    act.wait_ge(link[ln], i * STEP + 5)
                    act.activation(sd[:, ln, :], ps_v[:, ln, 0:TT], ACT.Ln, bias=keep["eps"][:, 0:1]).then_inc(link[ln], 1)
                for ln in range(LN):
                    act.wait_ge(link[ln], i * STEP + 6)
                    act.activation(rs[:, ln, :], sd[:, ln, :], ACT.Exp, scale=-0.5).then_inc(link[ln], 1)
                for ln in range(LN):
                    act.wait_ge(link[ln], i * STEP + 8)
                    for h in range(2):
                        last = act.activation(sq[:, ln, h, :], xc[:, ln, h, :], ACT.Identity,
                                              scale=keep["ln_g"][:, h:h + 1], bias=keep["ln_b"][:, h:h + 1])
                    last.then_inc(link[ln], 1)


def scan_order(x, k, at, size):
    if k % 2 == 0:
        return x[:, L - 1 - at:(L - 1 - at - size) if L - 1 - at - size >= 0 else None:-1] if k == 2 else x[:, at:at + size]
    v = x.rearrange("p (h w) -> p w h", h=H)
    w0, nw = at // H, size // H
    if k == 1:
        return v[:, w0:w0 + nw, :]
    lo = W - 1 - w0 - nw
    return v[:, W - 1 - w0:(lo if lo >= 0 else None):-1, ::-1]


def like(x, view):
    return x if len(view.shape) == 2 else x.rearrange("p (a b) -> p a b", b=H)


def delta_phase(nc, P, keep):
    with ExitStack() as ctx:
        s = Space(nc, ctx, "delta")
        pad = s.sb("pad", [128, 2, H + 2, W + 2])
        xu = [s.sb(f"xu{i}", [128, L]) for i in range(2)]
        two = lambda name, dt=F32: [s.sb(f"{name}{i}", [128, WC], dt) for i in range(2)]
        mag, pos, ex, lg = two("mag"), two("pos"), two("ex"), two("lg")
        dm, co, sm = two("dm"), two("co"), two("sm")
        delta, du = two("delta"), two("du")
        parts = [s.sb(f"parts{i}", [128, 2, 2, WC], F32R) for i in range(2)]
        bc = [s.sb(f"bc{i}", [2 * N, WC]) for i in range(2)]
        ps_a = [s.ps(f"ps_a{i}", [128, 2, 512]) for i in range(2)]
        ps_b = s.ps("ps_b", [2 * N, 2, 512])
        ps_c = s.ps("ps_c", [128, 2, 512])
        cleared, conv_full, x_done = s.sem("cleared"), s.sem("conv_full"), s.sem("x_done")
        img_here = [s.sem("img_here0"), s.sem("img_here1")]
        xs_out = [s.sem("xs_out0"), s.sem("xs_out1")]
        a_full, a_read, b_full, b_read = s.sem("a_full"), s.sem("a_read"), s.sem("b_full"), s.sem("b_read")
        mag_done, ex_done, lg_done, hid_done, hiu_done = (s.sem(x) for x in ("mag_done", "ex_done", "lg_done", "hid_done", "hiu_done"))
        dm_done, co_done, sm_done, delta_done, du_done = (
            s.sem(x) for x in ("dm_done", "co_done", "sm_done", "delta_done", "du_done"))
        lo_done = s.sem("lo_done")
        parts_out = [s.sem("parts_out0"), s.sem("parts_out1")]
        bc_out = [s.sem("bc_out0"), s.sem("bc_out1")]
        block = ctx.enter_context(nc.Block())
        HU = STEPS // 2
        UP = U // 2
        src = P["xn"].rearrange("b (r c) l -> (b r) c l", r=BR)

        @block.sync
        def _(sp):
            def load_image(n, k):
                img = src[n].rearrange("c (h w) -> c h w", h=H)
                for half in range(2):
                    sp.dma_start(pad[64 * half:64 * half + 64, k, 1:H + 1, 1 - half:W + 1 - half], img).then_inc(img_here[k], 16)

            def pair(i, last):
                for k in range(2):
                    sp.wait_ge(x_done, i * (2 * TPI) + TPI * k + TPI)
                    sp.dma_start(P["xs"][i * 2 + k], xu[k][:, :]).then_inc(xs_out[k], 16)
                    if not last:
                        load_image(i * 2 + (k + 2), k)
                    for st in range(STEPS):
                        at = i * (2 * STEPS) + k * STEPS + st
                        sp.wait_ge(b_read, at + 1 + 2)
                        sp.dma_start(P["bc"][i * 2 + k, st], bc[st % 2][:, :]).then_inc(bc_out[st % 2], 16)
                        sp.wait_ge(lo_done, i * (4 * STEPS) + 2 * (k * STEPS + st) + 2)
                        sp.dma_start(P["parts"][i * 2 + k, st].rearrange("a p t l -> p a (t l)"),
                                     parts[st % 2][:, :, :, :].bitcast(F32).rearrange("p a t l -> p a (t l)")).then_inc(parts_out[st % 2], 16)

            sp.wait_ge(cleared, 1)
            for k in range(2):
                load_image(k, k)
            with sp.Fori(0, UP - 1) as i:
                pair(i, False)
            pair(UP - 1, True)
            for k in range(2):
                sp.wait_ge(parts_out[k], 16 * U * HU + 16)
                sp.wait_ge(bc_out[k], 16 * U * HU + 16)
                sp.wait_ge(xs_out[k], 16 * UP + 16)

        @block.tensor
        def _(pe):
            def convolve(i, k, t):
                o = ps_c[:, t % 2, 0:TT]
                r0 = t * (TT // W)
                for dy in range(3):
                    rows = slice(r0 + dy, r0 + dy + TT // W)
                    pe.matmul(o, keep["w_pair"][:, dy, :], pad[:, k % 2, rows, 0:W], start=dy == 0, stop=False)
                    mm = pe.matmul(o, keep["w_one"][:, dy, :], pad[0:64, k % 2, rows, 2:W + 2], start=False, stop=dy == 2)
                mm.then_inc(conv_full, 1)

            def pair(i, last):
                for k in range(2):
                    pe.wait_ge(x_done, i * (2 * TPI) + TPI * k + TPI)
                    for st in range(STEPS):
                        d, c = divmod(st, NCH)
                        at = i * (2 * STEPS) + k * STEPS + st
                        pe.wait_ge(a_read, at + 1)
                        for h in range(2):
                            v = scan_order(xu[k][:, :], d, c * WC + h * HW_, HW_)
                            mm = pe.matmul(like(ps_a[st % 2][:, h, 0:HW_], v), keep["w_eff"][:, d, :], v, start=True, stop=True)
                        mm.then_inc(a_full, 1)
                        pe.wait_ge(b_read, at + 2)
                        for h in range(2):
                            v = scan_order(xu[k][:, :], d, c * WC + h * HW_, HW_)
                            mm = pe.matmul(like(ps_b[:, h, 0:HW_], v), keep["w_bc"][:, d, :], v, start=True, stop=True)
                        mm.then_inc(b_full, 1)
                        if st % 2 == 0 and not (last and k):
                            if st == 0:
                                pe.wait_ge(img_here[(k + 1) % 2], i * 32 + 32 * k + 32)
                            t = st // 2
                            pe.wait_ge(x_done, i * (2 * TPI) + TPI * k + TPI + t - 1)
                            convolve(i, k + 1, t)

            pe.wait_ge(img_here[0], 32)
            for t in range(TPI):
                if t >= 2:
                    pe.wait_ge(x_done, t - 1)
                convolve(0, 0, t)
            with pe.Fori(0, UP - 1) as i:
                pair(i, False)
            pair(UP - 1, True)

        @block.scalar
        def _(act):
            def silu(k, t):
                act.activation(xu[k][:, t * TT:t * TT + TT], ps_c[:, t % 2, 0:TT], ACT.Silu, bias=keep["conv_b"][:, 0:1]).then_inc(x_done, 1)

            def pair(i, last):
                for k in range(2):
                    for st in range(STEPS):
                        d, j = st // NCH, st % 2
                        at = i * (2 * STEPS) + k * STEPS + st
                        stored = i * (32 * HU) + 16 * (k * HU + st // 2) + 16
                        act.wait_ge(a_full, at + 1)
                        halves = lambda x: x[:, :].rearrange("p (a b) -> p a b", a=2)
                        act.activation(halves(mag[j]), ps_a[j][:, :, 0:HW_], ACT.Abs, bias=keep["dt_b"][:, d:d + 1]).then_inc(mag_done, 1)
                        act.wait_ge(mag_done, at + 1)
                        act.activation(ex[j][:, :], mag[j][:, :], ACT.Exp, scale=-1.0).then_inc(ex_done, 1)
                        act.wait_ge(b_full, at + 1)
                        act.wait_ge(bc_out[j], stored)
                        act.activation(halves(bc[j]), ps_b[:, :, 0:HW_], ACT.Copy).then_inc(b_read, 1)
                        act.wait_ge(dm_done, at + 1)
                        act.activation(lg[j][:, :], dm[j][:, :], ACT.Ln, bias=1.0).then_inc(lg_done, 1)
                        if st % 2 == 1 and not (last and k):
                            t = st // 2
                            act.wait_ge(conv_full, i * (2 * TPI) + TPI * k + TPI + t + 1)
                            if t == 0:
                                act.wait_ge(xs_out[(k + 1) % 2], i * 16 + 16 * k + 16)
                            silu((k + 1) % 2, t)

            act.sem_inc(b_read, 2)
            for k in range(2):
                act.sem_inc(parts_out[k], 16)
                act.sem_inc(bc_out[k], 16)
                act.sem_inc(xs_out[k], 16)
            for t in range(TPI):
                act.wait_ge(conv_full, t + 1)
                silu(0, t)
            with act.Fori(0, UP - 1) as i:
                pair(i, False)
            pair(UP - 1, True)

        @block.vector
        def _(dve):
            def high_u(i, k, st):
                j = st % 2
                dve.wait_ge(du_done, i * (2 * STEPS) + k * STEPS + st + 1)
                dve.tensor_copy(parts[j][:, 0, 1, :], du[j][:, :]).then_inc(hiu_done, 1)

            dve.memset(pad[:, :, :, :], 0.0).then_inc(cleared, 1)
            dve.sem_inc(a_read, 2)
            with dve.Fori(0, UP) as i:
                for k in range(2):
                    for st in range(STEPS):
                        d, c, j = st // NCH, st % NCH, st % 2
                        at = i * (2 * STEPS) + k * STEPS + st
                        stored = i * (32 * HU) + 16 * (k * HU + st // 2) + 16
                        dve.wait_ge(mag_done, at + 1)
                        dve.tensor_scalar(pos[j][:, :].rearrange("p (a b) -> p a b", a=2), ps_a[j][:, :, 0:HW_],
                                          keep["dt_b"][:, d:d + 1], 0.0, ALU.add, ALU.max).then_inc(a_read, 1)
                        dve.wait_ge(ex_done, at + 1)
                        dve.tensor_scalar(dm[j][:, :], ex[j][:, :], 1.0, -1.0, ALU.add, ALU.add).then_inc(dm_done, 1)
                        if st:
                            high_u(i, k, st - 1)
                        dve.wait_ge(dm_done, at + 1)
                        dve.tensor_tensor(co[j][:, :], ex[j][:, :], dm[j][:, :], ALU.subtract).then_inc(co_done, 1)
                        dve.wait_ge(co_done, at + 1)
                        dve.wait_ge(lg_done, at + 1)
                        dve.tensor_tensor(sm[j][:, :], co[j][:, :], lg[j][:, :], ALU.add).then_inc(sm_done, 1)
                        dve.wait_ge(sm_done, at + 1)
                        dve.wait_ge(parts_out[j], stored)
                        dve.tensor_tensor(delta[j][:, :], sm[j][:, :], pos[j][:, :], ALU.add).then_inc(delta_done, 1)
                        v = scan_order(xu[k][:, :], d, c * WC, WC)
                        dve.wait_ge(delta_done, at + 1)
                        dve.tensor_copy(parts[j][:, 0, 0, :], delta[j][:, :]).then_inc(hid_done, 1)
                        dve.tensor_tensor(like(du[j][:, :], v), like(delta[j][:, :], v), v, ALU.mult).then_inc(du_done, 1)
                    high_u(i, k, STEPS - 1)

        @block.gpsimd
        def _(pool):
            with pool.Fori(0, U) as u:
                for st in range(STEPS):
                    j = st % 2
                    pool.wait_ge(hid_done, u * STEPS + st + 1)
                    pool.tensor_tensor(parts[j][:, 1, 0, :], delta[j][:, :], parts[j][:, 0, 0, :].bitcast(F32), ALU.subtract).then_inc(lo_done, 1)
                    pool.wait_ge(hiu_done, u * STEPS + st + 1)
                    pool.tensor_tensor(parts[j][:, 1, 1, :], du[j][:, :], parts[j][:, 0, 1, :].bitcast(F32), ALU.subtract).then_inc(lo_done, 1)


def scan_phase(nc, P, keep):
    with ExitStack() as ctx:
        s = Space(nc, ctx, "scan")
        stack = [s.sb(f"stack{i}", [64, 4, 2, WC], F32R) for i in range(2)]
        b_rep = [s.sb(f"b_rep{i}", [128, WC]) for i in range(2)]
        c_rep = [s.sb(f"c_rep{i}", [128, WC]) for i in range(2)]
        rec = [s.sb(f"rec{i}", [128, G + 1]) for i in range(2)]
        bu = [s.sb(f"bu{i}", [128, WC]) for i in range(4)]
        h = [s.sb(f"h{i}", [128, WC]) for i in range(4)]
        hc = [s.sb(f"hc{i}", [128, WC]) for i in range(4)]
        y = [s.sb(f"y{i}", [128, WC]) for i in range(2)]
        h_last = s.sb("h_last", [128, G])
        ps_d = [s.ps(f"ps_d{i}", [128, 1024]) for i in range(2)]
        ps_u = s.ps("ps_u", [128, 1024])
        ps_y = s.ps("ps_y", [128, 1024])
        came = [s.sem(f"came{i}") for i in range(2)]
        y_out = [s.sem(f"y_out{i}") for i in range(2)]
        u_full, d_full, bu_done, exp_done, scan_done, hc_done, y_full, y_read, zeroed = (
            s.sem(x) for x in ("u_full", "d_full", "bu_done", "exp_done", "scan_done", "hc_done", "y_full", "y_read", "zeroed"))
        LOADS = 2 + 2 * J + 1
        TB = 2 * G
        NI = NKC // 2
        pieces = [(0, 512), (512, WC)]
        block = ctx.enter_context(nc.Block())
        recs = P["rec"].rearrange("u s p f -> (u s) p f")
        partsd = P["parts"].rearrange("u s a (q i) t l -> (u s) a i q t l", q=4)
        bcd = P["bc"].rearrange("u s n l -> (u s) n l")
        yd = P["y"].rearrange("u s p l -> (u s) p l")

        @block.sync
        def _(sp):
            for k in range(2):
                sp.sem_inc(y_out[k], 16)

            def store(i, cc):
                sp.wait_ge(y_read, i * 4 + 2 * (cc - 1))
                sp.dma_start(yd[i * 2 + (cc - 2)], y[cc % 2][:, :]).then_inc(y_out[cc % 2], 16)

            def step(i, first):
                for cc in range(2):
                    if not first:
                        sp.wait_ge(hc_done, i * TB + G * (cc - 1) + 3)
                    for a in range(2):
                        sp.dma_start(stack[cc][32 * a:32 * a + 32, :, :, :].bitcast(F32).rearrange("p q t l -> p q (t l)"),
                                     partsd[i * 2 + cc, a].rearrange("i q t l -> i q (t l)")).then_inc(came[cc], 16)
                    for j in range(J):
                        sp.dma_start(b_rep[cc][N * j:N * j + N, :], bcd[i * 2 + cc, 0:N]).then_inc(came[cc], 16)
                    for j in range(J):
                        sp.dma_start(c_rep[cc][N * j:N * j + N, :], bcd[i * 2 + cc, N:2 * N]).then_inc(came[cc], 16)
                    sp.dma_start(rec[cc][:, :], recs[i * 2 + cc]).then_inc(came[cc], 16)
                    if not first:
                        store(i, cc)

            step(0, True)
            with sp.Fori(1, NI) as i:
                step(i, False)
            store(NI, 0)
            store(NI, 1)
            for k in range(2):
                sp.wait_ge(y_out[k], 16 * NI + 16)

        @block.tensor
        def _(pe):
            def spread(dst, cc, g, which):
                for lo, hi in pieces:
                    mm = pe.matmul(dst[:, lo:hi], keep["parts_sel"][:, g % 4, :, :].rearrange("p j n -> p (j n)"),
                                   stack[cc][:, g // 4, which, lo:hi], start=True, stop=True)
                return mm

            def sum_states(i, t, first=False):
                g, cc = t % G, (t % TB) // G
                pe.wait_ge(hc_done, i * TB + t + 1)
                for n, (lo, hi) in enumerate(pieces):
                    if g == 0 and not (first and t == 0):
                        pe.wait_ge(y_read, i * 4 + 2 * (t // G) - 1 + n)
                    mm = pe.matmul(ps_y[:, lo:hi], keep["sum_sel"][:, D - J - J * g:2 * D - J - J * g],
                                   hc[t % 4][:, lo:hi],
                                   start=g == 0, stop=g == G - 1)
                    if g == G - 1:
                        mm.then_inc(y_full, 1)

            def step(i, first):
                for t in range(TB):
                    cc, g = divmod(t, G)
                    if g == 0:
                        pe.wait_ge(came[cc], i * (16 * LOADS) + 16 * LOADS)
                    if t or not first:
                        pe.wait_ge(bu_done, i * TB + t)
                    spread(ps_u, cc, g, 1).then_inc(u_full, 1)
                    if t >= 3 or not first:
                        sum_states(i, t - 3, first)
                    if t >= 2 or not first:
                        pe.wait_ge(scan_done, i * TB + t - 1)
                    spread(ps_d[t % 2], cc, g, 0).then_inc(d_full, 1)

            step(0, True)
            with pe.Fori(1, NI) as i:
                step(i, False)
            for t in range(-3, 0):
                sum_states(NI, t)

        @block.scalar
        def _(act):
            def read_y(i, cc):
                act.wait_ge(y_out[(cc + 1) % 2], i * 16 + 16 * ((cc + 1) // 2))
                for n, (lo, hi) in enumerate(pieces):
                    act.wait_ge(y_full, i * 4 + 2 * cc - 1 + n)
                    act.activation(y[(cc + 1) % 2][:, lo:hi], ps_y[:, lo:hi], ACT.Copy).then_inc(y_read, 1)

            def step(i, first):
                for t in range(TB):
                    cc, g = divmod(t, G)
                    if g == 0:
                        act.wait_ge(came[cc], i * (16 * LOADS) + 16 * LOADS)
                    if g == 2 and (cc or not first):
                        read_y(i, cc)
                    act.wait_ge(d_full, i * TB + t + 1)
                    act.activation(ps_d[t % 2][:, 0:WC], ps_d[t % 2][:, 0:WC], ACT.Exp, scale=rec[cc][:, g:g + 1]).then_inc(exp_done, 1)
                    if t >= 2 or not first:
                        b = (t - 2) % TB
                        act.activation(h_last[:, b % G:b % G + 1], h[b % 4][:, WC - 1:WC], ACT.Copy,
                                       scale=rec[b // G][:, G:G + 1]).then_inc(zeroed, 1)

            step(0, True)
            with act.Fori(1, NI) as i:
                step(i, False)
            read_y(NI, 0)

        @block.vector
        def _(dve):
            def scan(i, t):
                b = t % TB
                dve.wait_ge(exp_done, i * TB + t + 1)
                dve.tensor_tensor_scan(h[b % 4][:, :], ps_d[b % 2][:, 0:WC], bu[b % 4][:, :], h_last[:, b % G:b % G + 1],
                                       ALU.mult, ALU.add).then_inc(scan_done, 1)

            def step(i, first):
                for t in range(TB):
                    cc, g = divmod(t, G)
                    if g == 0:
                        dve.wait_ge(came[cc], i * (16 * LOADS) + 16 * LOADS)
                    dve.wait_ge(u_full, i * TB + t + 1)
                    dve.tensor_tensor(bu[t % 4][:, :], ps_u[:, 0:WC], b_rep[cc][:, :], ALU.mult).then_inc(bu_done, 1)
                    if t or not first:
                        scan(i, t - 1)

            dve.memset(h_last[:, :], 0.0).then_inc(zeroed, 1)
            dve.wait_ge(zeroed, 1)
            step(0, True)
            with dve.Fori(1, NI) as i:
                step(i, False)
            dve.wait_ge(bu_done, NI * TB)
            scan(NI, -1)

        @block.gpsimd
        def _(pool):
            with pool.Fori(0, NI) as i:
                for t in range(TB):
                    cc, g = divmod(t, G)
                    if g == 0:
                        pool.wait_ge(came[cc], i * (16 * LOADS) + 16 * LOADS)
                    pool.wait_ge(scan_done, i * TB + t + 1)
                    pool.tensor_tensor(hc[t % 4][:, :], h[t % 4][:, :], c_rep[cc][:, :], ALU.mult).then_inc(hc_done, 1)


def merge_phase(nc, P, keep):
    LN = 6
    LAST = 13
    with ExitStack() as ctx:
        s = Space(nc, ctx, "merge")
        y4 = s.sb("y4", [128, 2, K, L])
        xn = s.sb("xn", [DM, 2, L])
        xs = s.sb("xs", [128, 2, L])
        lane = lambda name, p=128: [s.sb(f"{name}{i}", [p, TT]) for i in range(LN)]
        a, b, yy, yc, sq, sd = (lane(n) for n in ("a", "b", "yy", "yc", "sq", "sd"))
        rs, ya, z = sd, sq, yc
        ps_s = [s.ps(f"ps_s{i}", [128, 512]) for i in range(LN)]
        ps_z = ps_s
        came = [s.sem(f"came{i}") for i in range(2)]
        link = [s.sem(f"link{i}") for i in range(LN)]
        gone = [s.sem(f"gone{i}") for i in range(LN)]
        b_done = s.sem("b_done")
        TL = TPI // LN
        PU = TL * LAST
        block = ctx.enter_context(nc.Block())
        yd = P["y"].rearrange("u (k c) p l -> u k p c l", k=K)
        xnd = P["xn"].rearrange("b (r c) l -> (b r) c l", r=BR)
        zd = P["z"].rearrange("b (r c) l -> (b r) c l", r=BR)

        @block.sync
        def _(sp):
            for ln in range(LN):
                sp.sem_inc(link[ln], PU + 1)
                sp.sem_inc(gone[ln], 16)
            with sp.Fori(0, U // 2) as i:
                for k in range(2):
                    for ln in range(LN):
                        sp.wait_ge(link[ln], i * (2 * PU) + k * PU + 1)
                    for d in range(K):
                        sp.dma_start(y4[:, k, d, :].rearrange("p (c l) -> p c l", c=NCH), yd[i * 2 + k, d]).then_inc(came[k], 16)
                    sp.dma_start(xn[:, k, :], xnd[i * 2 + k]).then_inc(came[k], 16)
                    sp.dma_start(xs[:, k, :], P["xs"][i * 2 + k]).then_inc(came[k], 16)

        @block.gpsimd
        def _(pool):
            with pool.Fori(0, U // 2) as i:
                for k in range(2):
                    pool.wait_ge(came[k], i * (16 * (K + 2)) + 16 * (K + 2))
                    for t in range(TPI):
                        pool.wait_ge(link[t % LN], i * (2 * PU) + k * PU + (t // LN) * LAST + PU - LAST + 4)
                        v1 = scan_order(y4[:, k, 1, :], 1, t * TT, TT)
                        v3 = scan_order(y4[:, k, 3, :], 3, t * TT, TT)
                        pool.tensor_tensor(like(b[t % LN][:, :], v1), v1, v3, ALU.add).then_inc(b_done, 1)

        @block.vector
        def _(dve):
            with dve.Fori(0, U // 2) as i:
                for k in range(2):
                    dve.wait_ge(came[k], i * (16 * (K + 2)) + 16 * (K + 2))
                    for g in range(TL):
                        base = i * (2 * PU) + (k * PU + g * LAST + PU + 1)
                        for ln in range(LN):
                            at = (g * LN + ln) * TT
                            dve.wait_ge(link[ln], base)
                            dve.tensor_tensor(a[ln][:, :], y4[:, k, 0, at:at + TT], scan_order(y4[:, k, 2, :], 2, at, TT), ALU.add).then_inc(link[ln], 1)
                        for ln in range(LN):
                            at = (g * LN + ln) * TT
                            dve.wait_ge(link[ln], base + 1)
                            dve.scalar_tensor_tensor(yy[ln][:, :], xs[:, k, at:at + TT], keep["d_sum"][:, 0:1],
                                                     a[ln][:, :], ALU.mult, ALU.add).then_inc(link[ln], 1)
                        for ln in range(LN):
                            dve.wait_ge(link[ln], base + 2)
                            dve.wait_ge(b_done, i * (2 * TPI) + k * TPI + g * LN + ln + 1)
                            dve.tensor_tensor(a[ln][:, :], yy[ln][:, :], b[ln][:, :], ALU.add).then_inc(link[ln], 1)
                        for ln in range(LN):
                            dve.wait_ge(link[ln], base + 4)
                            dve.wait_ge(gone[ln], i * (32 * TL) + 16 * (k * TL + g) + 16)
                            dve.tensor_tensor(yc[ln][:, :], a[ln][:, :], ps_s[ln][:, 0:TT], ALU.subtract).then_inc(link[ln], 1)
                        for ln in range(LN):
                            dve.wait_ge(link[ln], base + 9)
                            dve.tensor_tensor(yy[ln][:, :], yc[ln][:, :], rs[ln][:, :], ALU.mult).then_inc(link[ln], 1)
                        for ln in range(LN):
                            at = (g * LN + ln) * TT
                            dve.wait_ge(link[ln], base + 12)
                            dve.scalar_tensor_tensor(z[ln][0:DM, :], xn[:, k, at:at + TT], keep["skip"][:, 0:1], ps_z[ln][0:DM, 0:TT],
                                                     ALU.mult, ALU.add).then_inc(link[ln], 1)

        @block.tensor
        def _(pe):
            with pe.Fori(0, U // 2) as i:
                for k in range(2):
                    for g in range(TL):
                        base = i * (2 * PU) + (k * PU + g * LAST + PU + 1)
                        for ln in range(LN):
                            pe.wait_ge(link[ln], base + 3)
                            pe.matmul(ps_s[ln][:, 0:TT], keep["ones_d"][:, :], a[ln][:, :], start=True, stop=True).then_inc(link[ln], 1)
                        for ln in range(LN):
                            pe.wait_ge(link[ln], base + 6)
                            pe.matmul(ps_s[ln][:, 0:TT], keep["ones_d"][:, :], sq[ln][:, :], start=True, stop=True).then_inc(link[ln], 1)
                        for ln in range(LN):
                            pe.wait_ge(link[ln], base + 11)
                            pe.matmul(ps_z[ln][0:DM, 0:TT], keep["out_W"][:, :], ya[ln][:, :], start=True, stop=True).then_inc(link[ln], 1)

        @block.scalar
        def _(act):
            with act.Fori(0, U // 2) as i:
                for k in range(2):
                    for g in range(TL):
                        base = i * (2 * PU) + (k * PU + g * LAST + PU + 1)
                        for ln in range(LN):
                            act.wait_ge(link[ln], base + 5)
                            act.activation(sq[ln][:, :], yc[ln][:, :], ACT.Square).then_inc(link[ln], 1)
                        for ln in range(LN):
                            act.wait_ge(link[ln], base + 7)
                            act.activation(sd[ln][:, :], ps_s[ln][:, 0:TT], ACT.Ln, bias=keep["eps"][:, 0:1]).then_inc(link[ln], 1)
                        for ln in range(LN):
                            act.wait_ge(link[ln], base + 8)
                            act.activation(rs[ln][:, :], sd[ln][:, :], ACT.Exp, scale=-0.5).then_inc(link[ln], 1)
                        for ln in range(LN):
                            act.wait_ge(link[ln], base + 10)
                            act.activation(ya[ln][:, :], yy[ln][:, :], ACT.Identity, scale=keep["onorm_g"][:, 0:1],
                                           bias=keep["onorm_b"][:, 0:1]).then_inc(link[ln], 1)
                        for ln in range(LN):
                            act.wait_ge(link[ln], base + 13)
                            act.dma_start(zd[i * 2 + k, :, (g * LN + ln) * TT:(g * LN + ln + 1) * TT], z[ln][0:DM, :]).then_inc(gone[ln], 16)
            for ln in range(LN):
                act.wait_ge(gone[ln], 16 * U * TL + 16)


def project_phase(nc, P, keep, f_hi, f_lo):
    LN = 3
    LAST = 17
    with ExitStack() as ctx:
        s = Space(nc, ctx, "proj")
        zn = s.sb("zn", [128, LN, 2, TT])
        x1, xc, sq, xh = (s.sb(n, [128, LN, 2, TT]) for n in ("x1", "xc", "sq", "xh"))
        sd, rs, ln2, lm, inv = (s.sb(n, [128, LN, TT]) for n in ("sd", "rs", "ln2", "lm", "inv"))
        ps_x = s.ps("ps_x", [128, LN, 2, 512])
        ps_s = ps_x[:, :, 0, :]
        came = [s.sem(f"came{i}") for i in range(LN)]
        gone = [s.sem(f"gone{i}") for i in range(LN)]
        link = [s.sem(f"link{i}") for i in range(LN)]
        block = ctx.enter_context(nc.Block())
        zv = P["zn"].rearrange("b (h p) (i t) -> b i p h t", h=2, t=TT)
        at = lambda x, i, ln: x[:, :, bass.ds(i * (LN * TT) + ln * TT, TT)]
        both = lambda x: x.unsqueeze(1).to_broadcast([128, 2, TT])

        @block.sync
        def _(sp):
            for ln in range(LN):
                sp.sem_inc(link[ln], 1)
                sp.sem_inc(gone[ln], 16)
            with sp.Fori(0, B) as b:
                with sp.Fori(0, TPI // LN) as i:
                    for ln in range(LN):
                        sp.wait_ge(link[ln], b * (LAST * TPI // LN) + i * LAST + 1)
                        sp.dma_start(zn[:, ln, :, :], zv[b, i * LN + ln]).then_inc(came[ln], 16)
                    for ln in range(LN):
                        sp.wait_ge(link[ln], b * (LAST * TPI // LN) + i * LAST + 3)
                        sp.dma_start(P["x1"][b * TPI + i * LN + ln], x1[:, ln, :, :]).then_inc(gone[ln], 16)
            for ln in range(LN):
                sp.wait_ge(gone[ln], 16 * (NTT // LN) + 16)

        @block.tensor
        def _(pe):
            with pe.Fori(0, NTT // LN) as i:
                for ln in range(LN):
                    pe.wait_ge(came[ln], i * 16 + 16)
                    for o in range(2):
                        for h in range(2):
                            mm = pe.matmul(ps_x[:, ln, o, 0:TT], keep["proj_W"][:, h, o * 128:o * 128 + 128], zn[:, ln, h, :],
                                           start=h == 0, stop=h == 1)
                    mm.then_inc(link[ln], 1)
                for ln in range(LN):
                    pe.wait_ge(link[ln], i * LAST + 3)
                    for h in range(2):
                        mm = pe.matmul(ps_s[:, ln, 0:TT], keep["ones_c"][:, :], x1[:, ln, h, :], start=h == 0, stop=h == 1)
                    mm.then_inc(link[ln], 1)
                for ln in range(LN):
                    pe.wait_ge(link[ln], i * LAST + 6)
                    for h in range(2):
                        mm = pe.matmul(ps_s[:, ln, 0:TT], keep["ones_c"][:, :], sq[:, ln, h, :], start=h == 0, stop=h == 1)
                    mm.then_inc(link[ln], 1)
                for ln in range(LN):
                    pe.wait_ge(link[ln], i * LAST + 11)
                    for h in range(2):
                        mm = pe.matmul(ps_s[:, ln, 0:TT], keep["ones"][:, :], sq[:, ln, h, :], start=h == 0, stop=h == 1)
                    mm.then_inc(link[ln], 1)

        @block.scalar
        def _(act):
            with act.Fori(0, NTT // LN) as i:
                for ln in range(LN):
                    act.wait_ge(link[ln], i * LAST + 2)
                    act.wait_ge(gone[ln], i * 16 + 16)
                    for h in range(2):
                        last = act.activation(x1[:, ln, h, :], ps_x[:, ln, h, 0:TT], ACT.Identity, bias=keep["proj_b"][:, h:h + 1])
                    last.then_inc(link[ln], 1)
                for ln in range(LN):
                    act.wait_ge(link[ln], i * LAST + 5)
                    act.activation(sq[:, ln, :, :], xc[:, ln, :, :], ACT.Square).then_inc(link[ln], 1)
                for ln in range(LN):
                    act.wait_ge(link[ln], i * LAST + 7)
                    act.activation(sd[:, ln, :], ps_s[:, ln, 0:TT], ACT.Ln, bias=keep["eps"][:, 0:1]).then_inc(link[ln], 1)
                for ln in range(LN):
                    act.wait_ge(link[ln], i * LAST + 8)
                    act.activation(rs[:, ln, :], sd[:, ln, :], ACT.Exp, scale=-0.5).then_inc(link[ln], 1)
                for ln in range(LN):
                    act.wait_ge(link[ln], i * LAST + 10)
                    act.activation(sq[:, ln, :, :], xh[:, ln, :, :], ACT.Square).then_inc(link[ln], 1)
                for ln in range(LN):
                    act.wait_ge(link[ln], i * LAST + 13)
                    act.activation(ln2[:, ln, :], lm[:, ln, :], ACT.Ln, scale=2.0 ** 40).then_inc(link[ln], 1)
                for ln in range(LN):
                    act.wait_ge(link[ln], i * LAST + 14)
                    act.activation(inv[:, ln, :], ln2[:, ln, :], ACT.Exp, scale=-0.5, bias=keep["ln_2_20"][:, 0:1]).then_inc(link[ln], 1)
                for ln in range(LN):
                    act.wait_ge(link[ln], i * LAST + 16)
                    act.activation(at(f_hi, i, ln), xc[:, ln, :, :], ACT.Copy).then_inc(link[ln], 1)

        @block.vector
        def _(dve):
            with dve.Fori(0, NTT // LN) as i:
                for ln in range(LN):
                    dve.wait_ge(link[ln], i * LAST + 4)
                    dve.tensor_tensor(xc[:, ln, :, :], x1[:, ln, :, :], both(ps_s[:, ln, 0:TT]), ALU.subtract).then_inc(link[ln], 1)
                for ln in range(LN):
                    dve.wait_ge(link[ln], i * LAST + 9)
                    dve.tensor_tensor(xh[:, ln, :, :], xc[:, ln, :, :], both(rs[:, ln, :]), ALU.mult).then_inc(link[ln], 1)
                for ln in range(LN):
                    dve.wait_ge(link[ln], i * LAST + 12)
                    dve.tensor_scalar(lm[:, ln, :], ps_s[:, ln, 0:TT], 1e-24, None, ALU.max).then_inc(link[ln], 1)
                for ln in range(LN):
                    dve.wait_ge(link[ln], i * LAST + 15)
                    dve.tensor_tensor(xc[:, ln, :, :], xh[:, ln, :, :], both(inv[:, ln, :]), ALU.mult).then_inc(link[ln], 1)
                for ln in range(LN):
                    dve.wait_ge(link[ln], i * LAST + 17)
                    dve.tensor_tensor(at(f_lo, i, ln), xc[:, ln, :, :], at(f_hi, i, ln).bitcast(F32), ALU.subtract).then_inc(link[ln], 1)


def attention_phase(nc, keep, f_hi, f_lo, o_t, den):
    with ExitStack() as ctx:
        s = Space(nc, ctx, "attn")
        t_hi = s.sb("t_hi", [128, KB, C], F32R)
        t_lo = s.sb("t_lo", [128, KB, C], F32R)
        e = [s.sb(f"e{i}", [128, TT]) for i in range(4)]
        e_hi = [s.sb(f"e_hi{i}", [128, TT], F32R) for i in range(4)]
        e_lo = [s.sb(f"e_lo{i}", [128, TT], F32R) for i in range(4)]
        ps_s = [s.ps(f"ps_s{i}", [128, 512]) for i in range(4)]
        ps_o = s.ps("ps_o", [128, 2, 512])
        turned, moved = s.sem("turned"), s.sem("moved")
        hi_done, lo_done = s.sem("hi_done"), s.sem("lo_done")
        s_full, e_done, o_full, o_read = s.sem("s_full"), s.sem("e_done"), s.sem("o_full"), s.sem("o_read")
        block = ctx.enter_context(nc.Block())

        @block.tensor
        def _(pe):
            for n in range(KB):
                if n >= 4:
                    pe.wait_ge(moved, n - 3)
                f = f_hi if n < KB // 2 else f_lo
                for q in range(4):
                    j, h = 2 * (n % (KB // 2)) + q // 2, q % 2
                    mm = pe.transpose(ps_s[n % 4][:, q * 128:q * 128 + 128], f[:, h, j * 128:j * 128 + 128].bitcast(F32), keep["ident"][:, :])
                mm.then_inc(turned, 1)
            pe.wait_ge(moved, KB)

            def scores(q, j):
                for h in range(2):
                    keys, tokens = slice(j * 128, j * 128 + 128), bass.ds(q * TT, TT)
                    mm = products(pe, ps_s[j % 4][:, 0:TT], (f_hi[:, h, keys], f_hi[:, h, tokens]),
                                  (f_lo[:, h, keys], f_lo[:, h, tokens]), h == 0, h == 1)
                mm.then_inc(s_full, 1)

            pe.sem_inc(o_read, 1)
            with pe.Fori(0, NTT) as q:
                scores(q, 0)
                scores(q, 1)
                for j in range(KB):
                    if j + 2 < KB:
                        scores(q, j + 2)
                    if j == 0:
                        pe.wait_ge(o_read, q + 1)
                    pe.wait_ge(lo_done, q * KB + j + 1)
                    for o in range(2):
                        ch = slice(o * 128, o * 128 + 128)
                        mm = products(pe, ps_o[:, o, 0:TT], (t_hi[:, j, ch], e_hi[j % 4][:, :]),
                                      (t_lo[:, j, ch], e_lo[j % 4][:, :]), j == 0, j == KB - 1)
                mm.then_inc(o_full, 1)

        @block.scalar
        def _(act):
            with act.Fori(0, NTT) as q:
                for j in range(KB):
                    act.wait_ge(s_full, q * KB + j + 1)
                    act.activation(e[j % 4][:, :], ps_s[j % 4][:, 0:TT], ACT.Exp,
                                   accum_out=den[:, j, bass.ds(q, 1)]).then_inc(e_done, 1)

        @block.vector
        def _(dve):
            for n in range(KB):
                dve.wait_ge(turned, n + 1)
                t, j = (t_hi if n < KB // 2 else t_lo), 2 * (n % (KB // 2))
                dve.tensor_copy(t[:, j:j + 2, :].rearrange("p a c -> p (a c)"), ps_s[n % 4][:, :]).then_inc(moved, 1)
            with dve.Fori(0, NTT) as q:
                for j in range(KB):
                    dve.wait_ge(e_done, q * KB + j + 1)
                    dve.tensor_copy(e_hi[j % 4][:, :], e[j % 4][:, :]).then_inc(hi_done, 1)
                dve.wait_ge(o_full, q + 1)
                dve.tensor_copy(o_t[:, :, bass.ds(q * TT, TT)], ps_o[:, :, 0:TT]).then_inc(o_read, 1)

        @block.gpsimd
        def _(pool):
            with pool.Fori(0, NTT) as q:
                for j in range(KB):
                    pool.wait_ge(hi_done, q * KB + j + 1)
                    pool.tensor_tensor(e_lo[j % 4][:, :], e[j % 4][:, :], e_hi[j % 4][:, :].bitcast(F32), ALU.subtract).then_inc(lo_done, 1)


def blend_phase(nc, P, keep, f_hi, f_lo, o_t, den):
    LN = 3
    LAST = 19
    with ExitStack() as ctx:
        s = Space(nc, ctx, "blend")
        den_sum, den_inv, den_w = (s.sb(n, [128, KB]) for n in ("den_sum", "den_inv", "den_w"))
        dg = s.sb("dg", [128, LN, TT // 128, 128])
        aa, mm_, sq, xc = (s.sb(n, [128, LN, 2, TT]) for n in ("aa", "mm_", "sq", "xc"))
        ln2, lm, inv, sd, rs = (s.sb(n, [128, LN, TT]) for n in ("ln2", "lm", "inv", "sd", "rs"))
        ps_b = s.ps("ps_b", [128, LN, 512])
        ps_s = s.ps("ps_s", [128, LN, 512])
        summed = s.sem("summed")
        x1 = s.sb("x1", [128, LN, 2, TT])
        came = [s.sem(f"came{i}") for i in range(LN)]
        gone = [s.sem(f"gone{i}") for i in range(LN)]
        link = [s.sem(f"link{i}") for i in range(LN)]
        block = ctx.enter_context(nc.Block())
        at = lambda x, i, ln: x[:, :, bass.ds(i * (LN * TT) + ln * TT, TT)]
        both = lambda x: x.unsqueeze(1).to_broadcast([128, 2, TT])
        BL = TT // 128

        @block.sync
        def _(sp):
            for ln in range(LN):
                sp.sem_inc(gone[ln], 16)
            with sp.Fori(0, NTT // LN) as i:
                for ln in range(LN):
                    sp.wait_ge(gone[ln], i * 16 + 16)
                    sp.dma_start(x1[:, ln, :, :], P["x1"][i * LN + ln]).then_inc(came[ln], 16)
                for ln in range(LN):
                    sp.wait_ge(link[ln], i * LAST + 15)
                    sp.dma_start(P["x2"][i * LN + ln], x1[:, ln, :, :]).then_inc(gone[ln], 16)
            for ln in range(LN):
                sp.wait_ge(gone[ln], 16 * (NTT // LN) + 16)

        @block.vector
        def _(dve):
            dve.tensor_reduce(den_sum[:, :], den[:, :, :], AX.X, ALU.add).then_inc(summed, 1)
            dve.wait_ge(summed, 1)
            dve.reciprocal(den_inv[:, :], den_sum[:, :]).then_inc(summed, 1)
            dve.wait_ge(summed, 2)
            dve.tensor_scalar(den_w[:, :], den_inv[:, :], 1.0 - 0.8, None, ALU.mult).then_inc(summed, 1)
            dve.wait_ge(summed, 3)
            for ln in range(LN):
                dve.sem_inc(link[ln], 1)
            with dve.Fori(0, NTT // LN) as i:
                for ln in range(LN):
                    dve.wait_ge(link[ln], i * LAST + 1)
                    w = den_w[:, bass.ds(i * (LN * BL) + ln * BL, BL)].unsqueeze(2).to_broadcast([128, BL, 128])
                    eye = keep["ident"][:, :].unsqueeze(1).to_broadcast([128, BL, 128])
                    dve.tensor_tensor(dg[:, ln, :, :], eye, w, ALU.mult).then_inc(link[ln], 1)
                for ln in range(LN):
                    dve.wait_ge(link[ln], i * LAST + 3)
                    dve.tensor_tensor(aa[:, ln, :, :], at(o_t, i, ln), both(ps_b[:, ln, 0:TT]), ALU.mult).then_inc(link[ln], 1)
                for ln in range(LN):
                    dve.wait_ge(link[ln], i * LAST + 4)
                    dve.scalar_tensor_tensor(mm_[:, ln, :, :], at(f_lo, i, ln).bitcast(F32), 0.8, aa[:, ln, :, :], ALU.mult, ALU.add).then_inc(link[ln], 1)
                for ln in range(LN):
                    dve.wait_ge(link[ln], i * LAST + 5)
                    dve.scalar_tensor_tensor(mm_[:, ln, :, :], at(f_hi, i, ln).bitcast(F32), 0.8, mm_[:, ln, :, :], ALU.mult, ALU.add).then_inc(link[ln], 1)
                for ln in range(LN):
                    dve.wait_ge(link[ln], i * LAST + 8)
                    dve.tensor_scalar(lm[:, ln, :], ps_s[:, ln, 0:TT], 1e-24, None, ALU.max).then_inc(link[ln], 1)
                for ln in range(LN):
                    dve.wait_ge(link[ln], i * LAST + 11)
                    dve.tensor_tensor(aa[:, ln, :, :], mm_[:, ln, :, :], both(inv[:, ln, :]), ALU.mult).then_inc(link[ln], 1)
                for ln in range(LN):
                    dve.wait_ge(link[ln], i * LAST + 12)
                    dve.wait_ge(came[ln], i * 16 + 16)
                    dve.tensor_tensor(x1[:, ln, :, :], x1[:, ln, :, :], aa[:, ln, :, :], ALU.add).then_inc(link[ln], 1)
                for ln in range(LN):
                    dve.wait_ge(link[ln], i * LAST + 14)
                    dve.tensor_tensor(xc[:, ln, :, :], x1[:, ln, :, :], both(ps_s[:, ln, 0:TT]), ALU.subtract).then_inc(link[ln], 1)
                for ln in range(LN):
                    dve.wait_ge(link[ln], i * LAST + 19)
                    dve.tensor_tensor(at(o_t, i, ln), xc[:, ln, :, :], both(rs[:, ln, :]), ALU.mult).then_inc(link[ln], 1)

        @block.tensor
        def _(pe):
            with pe.Fori(0, NTT // LN) as i:
                for ln in range(LN):
                    pe.wait_ge(link[ln], i * LAST + 2)
                    pe.matmul(ps_b[:, ln, 0:TT], keep["ones"][:, :], dg[:, ln, :, :].rearrange("p a b -> p (a b)"),
                              start=True, stop=True).then_inc(link[ln], 1)
                for ln in range(LN):
                    pe.wait_ge(link[ln], i * LAST + 7)
                    for h in range(2):
                        mm = pe.matmul(ps_s[:, ln, 0:TT], keep["ones"][:, :], sq[:, ln, h, :], start=h == 0, stop=h == 1)
                    mm.then_inc(link[ln], 1)
                for ln in range(LN):
                    pe.wait_ge(link[ln], i * LAST + 13)
                    for h in range(2):
                        mm = pe.matmul(ps_s[:, ln, 0:TT], keep["ones_c"][:, :], x1[:, ln, h, :], start=h == 0, stop=h == 1)
                    mm.then_inc(link[ln], 1)
                for ln in range(LN):
                    pe.wait_ge(link[ln], i * LAST + 16)
                    for h in range(2):
                        mm = pe.matmul(ps_s[:, ln, 0:TT], keep["ones_c"][:, :], sq[:, ln, h, :], start=h == 0, stop=h == 1)
                    mm.then_inc(link[ln], 1)

        @block.scalar
        def _(act):
            with act.Fori(0, NTT // LN) as i:
                for ln in range(LN):
                    act.wait_ge(link[ln], i * LAST + 6)
                    act.activation(sq[:, ln, :, :], mm_[:, ln, :, :], ACT.Square).then_inc(link[ln], 1)
                for ln in range(LN):
                    act.wait_ge(link[ln], i * LAST + 9)
                    act.activation(ln2[:, ln, :], lm[:, ln, :], ACT.Ln, scale=2.0 ** 40).then_inc(link[ln], 1)
                for ln in range(LN):
                    act.wait_ge(link[ln], i * LAST + 10)
                    act.activation(inv[:, ln, :], ln2[:, ln, :], ACT.Exp, scale=-0.5, bias=keep["ln_2_20"][:, 0:1]).then_inc(link[ln], 1)
                for ln in range(LN):
                    act.wait_ge(link[ln], i * LAST + 15)
                    act.activation(sq[:, ln, :, :], xc[:, ln, :, :], ACT.Square).then_inc(link[ln], 1)
                for ln in range(LN):
                    act.wait_ge(link[ln], i * LAST + 17)
                    act.activation(sd[:, ln, :], ps_s[:, ln, 0:TT], ACT.Ln, bias=keep["eps"][:, 0:1]).then_inc(link[ln], 1)
                for ln in range(LN):
                    act.wait_ge(link[ln], i * LAST + 18)
                    act.activation(rs[:, ln, :], sd[:, ln, :], ACT.Exp, scale=-0.5).then_inc(link[ln], 1)


def gate_phase(nc, P, w, keep, xl, we):
    with ExitStack() as ctx:
        s = Space(nc, ctx, "gate")
        raw = [s.sb(f"raw{i}", [128, 2 * HF]) for i in range(3)]
        gw = s.sb("gw", [128, 2, E])
        gb = s.sb("gb", [128, E])
        cw_t = [s.sb(f"cw_t{i}", [E, 512]) for i in range(2)]
        small = lambda name, n=E, dt=F32: s.sb(name, [128, KB, n], dt)
        lg, top, dif, ex, cw, cw2 = (small(n) for n in ("lg", "top", "dif", "ex", "cw", "cw2"))
        idx = small("idx", E, U32)
        dif2, ex2, v2, pick = (small(n, 2) for n in ("dif2", "ex2", "v2", "pick"))
        sm, inv = small("sm", 1), small("inv", 1)
        iota = s.sb("iota", [128, E])
        ps_t = [s.ps(f"ps_t{i}", [128, 512]) for i in range(2)]
        ps_g = s.ps("ps_g", [128, 512])
        loaded, gate_full, step_done, ex_done = s.sem("loaded"), s.sem("gate_full"), s.sem("step_done"), s.sem("ex_done")
        iota_done, turned, moved, stored = s.sem("iota_done"), s.sem("turned"), s.sem("moved"), [s.sem("stored0"), s.sem("stored1")]
        raw_here = [s.sem(f"raw_here{i}") for i in range(3)]
        hi_cut, lo_cut, small_loads = s.sem("hi_cut"), s.sem("lo_cut"), s.sem("small_loads")
        srcs = []
        for e in range(E):
            srcs.append((w["W1"][e].rearrange("(h p) n -> p h n", h=2), 2, we["w1_hi"][:, e, :, :], we["w1_lo"][:, e, :, :]))
            srcs.append((w["W2"][e].rearrange("(h p) n -> p h n", h=HB), HB, we["w2_hi"][:, e, :, :], we["w2_lo"][:, e, :, :]))
        block = ctx.enter_context(nc.Block())
        wide = lambda x: x.to_broadcast([128, KB, E])

        @block.sync
        def _(sp):
            sp.dma_start(gw[:, :, :], w["gate_w"].rearrange("(h p) e -> p h e", h=2)).then_inc(loaded, 16)
            sp.dma_start(gb[:, :], w["gate_b"].partition_broadcast(128)).then_inc(loaded, 16)
            sp.dma_start(we["b2"][:, :], w["b2"]).then_inc(small_loads, 16)
            for e in range(E):
                sp.dma_start(we["b1"][:, e, :], w["b1"][e].rearrange("(h p) -> p h", h=HB), allow_slow_non_contiguous=True).then_inc(small_loads, 16)
            for n, (src, parts, _, _) in enumerate(srcs):
                if n >= 3:
                    sp.wait_ge(lo_cut, n - 2)
                sp.dma_start(raw[n % 3][:, :].rearrange("p (h n) -> p h n", h=parts), src).then_inc(raw_here[n % 3], 16)
            for n in range(KB // 4):
                sp.wait_ge(moved, n + 1)
                sp.dma_start(P["cw"][:, n * 512:n * 512 + 512], cw_t[n % 2][:, :]).then_inc(stored[n % 2], 16)
            for k in range(2):
                sp.wait_ge(stored[k], 16 * ((KB // 4 + 1 - k) // 2))
            sp.wait_ge(small_loads, 16 * (1 + E))

        @block.gpsimd
        def _(pool):
            for n in range(E):
                last = pool.memset(iota[:, n:n + 1], float(n))
            last.then_inc(iota_done, 1)
            for n, (_, parts, hi, lo) in enumerate(srcs):
                pool.wait_ge(hi_cut, n + 1)
                v = raw[n % 3][:, :].rearrange("p (h n) -> p h n", h=parts)
                pool.tensor_tensor(lo, v, hi.bitcast(F32), ALU.subtract).then_inc(lo_cut, 1)

        @block.tensor
        def _(pe):
            pe.wait_ge(loaded, 32)
            for j in range(KB):
                for h in range(2):
                    mm = pe.matmul(ps_g[:, j * E:j * E + E], xl[:, h, j * 128:j * 128 + 128], gw[:, h, :], start=h == 0, stop=h == 1)
            mm.then_inc(gate_full, 1)
            pe.wait_ge(step_done, 12)
            for n in range(KB // 4):
                if n >= 2:
                    pe.wait_ge(moved, n - 1)
                for q in range(4):
                    j = 4 * n + q
                    mm = pe.transpose(ps_t[n % 2][0:E, q * 128:q * 128 + 128], cw[:, j, :], keep["ident"][:, :])
                mm.then_inc(turned, 1)

        @block.scalar
        def _(act):
            for n, (_, parts, hi, _) in enumerate(srcs):
                if n == 8:
                    act.wait_ge(step_done, 3)
                    act.activation(ex[:, :, :], dif[:, :, :], ACT.Exp).then_inc(ex_done, 1)
                    act.activation(ex2[:, :, :], dif2[:, :, :], ACT.Exp).then_inc(ex_done, 1)
                act.wait_ge(raw_here[n % 3], 16 * (n // 3 + 1))
                act.activation(hi, raw[n % 3][:, :].rearrange("p (h n) -> p h n", h=parts), ACT.Copy).then_inc(hi_cut, 1)

        @block.vector
        def _(dve):
            dve.wait_ge(gate_full, 1)
            logits = ps_g[:, 0:KB * E].rearrange("p (j e) -> p j e", e=E)
            dve.tensor_tensor(lg[:, :, :], logits, gb[:, :].unsqueeze(1).to_broadcast([128, KB, E]), ALU.add).then_inc(step_done, 1)
            dve.wait_ge(step_done, 1)
            for j in range(KB):
                last = dve.max(top[:, j, :], lg[:, j, :])
            last.then_inc(step_done, 1)
            dve.wait_ge(step_done, 2)
            dve.tensor_tensor(dif[:, :, :], lg[:, :, :], wide(top[:, :, 0:1]), ALU.subtract)
            dve.tensor_tensor(dif2[:, :, :], top[:, :, 0:2], top[:, :, 0:1].to_broadcast([128, KB, 2]), ALU.subtract).then_inc(step_done, 1)
            for j in range(KB):
                last = dve.max_index(idx[:, j, :], top[:, j, :], lg[:, j, :])
            last.then_inc(step_done, 1)
            dve.wait_ge(step_done, 4)
            dve.tensor_copy(pick[:, :, :], idx[:, :, 0:2]).then_inc(step_done, 1)
            dve.wait_ge(ex_done, 2)
            dve.tensor_reduce(sm[:, :, :], ex[:, :, :], AX.X, ALU.add).then_inc(step_done, 1)
            dve.wait_ge(step_done, 6)
            dve.reciprocal(inv[:, :, :], sm[:, :, :]).then_inc(step_done, 1)
            dve.wait_ge(step_done, 7)
            dve.tensor_tensor(v2[:, :, :], ex2[:, :, :], inv[:, :, :].to_broadcast([128, KB, 2]), ALU.mult).then_inc(step_done, 1)
            dve.wait_ge(step_done, 8)
            dve.wait_ge(iota_done, 1)
            num = iota[:, :].unsqueeze(1).to_broadcast([128, KB, E])
            dve.tensor_tensor(cw[:, :, :], num, wide(pick[:, :, 0:1]), ALU.is_equal)
            dve.tensor_tensor(cw2[:, :, :], num, wide(pick[:, :, 1:2]), ALU.is_equal).then_inc(step_done, 1)
            dve.wait_ge(step_done, 9)
            dve.tensor_tensor(cw[:, :, :], cw[:, :, :], wide(v2[:, :, 0:1]), ALU.mult).then_inc(step_done, 1)
            dve.tensor_tensor(cw2[:, :, :], cw2[:, :, :], wide(v2[:, :, 1:2]), ALU.mult).then_inc(step_done, 1)
            dve.wait_ge(step_done, 11)
            dve.tensor_tensor(cw[:, :, :], cw[:, :, :], cw2[:, :, :], ALU.add).then_inc(step_done, 1)
            for n in range(KB // 4):
                dve.wait_ge(turned, n + 1)
                if n >= 2:
                    dve.wait_ge(stored[n % 2], 16 * (n // 2))
                dve.tensor_copy(cw_t[n % 2][:, :], ps_t[n % 2][0:E, :]).then_inc(moved, 1)


def expert_phase(nc, P, keep, xl, we, out):
    with ExitStack() as ctx:
        s = Space(nc, ctx, "moe")
        cw = s.sb("cw", [E, 2, TT])
        x2 = s.sb("x2", [128, 2, 2, TT])
        x_hi = s.sb("x_hi", [128, 2, TT], F32R)
        x_lo = s.sb("x_lo", [128, 2, TT], F32R)
        ring = lambda name, dt=F32: [s.sb(f"{name}{i}", [128, TT], dt) for i in range(4)]
        hg, h_hi, h_lo = ring("hg"), ring("h_hi", F32R), ring("h_lo", F32R)
        ps_h = [s.ps(f"ps_h{i}", [128, 512]) for i in range(4)]
        ps_w = [s.ps(f"ps_w{i}", [128, 512]) for i in range(2)]
        ps_o = s.ps("ps_o", [128, 2, 512])
        here = [s.sem(f"here{k}") for k in range(2)]
        x_cut, h_full, g_done, w_full, hw_done, hi_done, lo_done, o_full, o_read = (
            s.sem(n) for n in ("x_cut", "h_full", "g_done", "w_full", "hw_done", "hi_done", "lo_done", "o_full", "o_read"))
        gone = [s.sem(f"gone{k}") for k in range(2)]
        M = E * HB
        block = ctx.enter_context(nc.Block())
        ov = out.rearrange("b (h p) y x -> b p h (y x)", h=2)

        @block.sync
        def _(sp):
            def load(t, k):
                sp.wait_ge(gone[k], t * 8 + (16 - 8 * k))
                sp.dma_start(cw[:, k, :], P["cw"][:, bass.ds(t * TT, TT)]).then_inc(here[k], 16)
                sp.dma_start(x2[:, k, :, :], P["x2"][t]).then_inc(here[k], 16)

            def image(b, last):
                for n in range(TPI):
                    if not last or n + 1 < TPI:
                        load(b * TPI + (n + 1), (n + 1) % 2)
                    sp.wait_ge(o_read, b * TPI + n + 3)
                    sp.dma_start(ov[b, :, :, n * TT:n * TT + TT], x2[:, n % 2, :, :]).then_inc(gone[n % 2], 16)

            sp.sem_inc(o_read, 2)
            for k in range(2):
                sp.sem_inc(gone[k], 16)
            load(0, 0)
            with sp.Fori(0, B - 1) as b:
                image(b, False)
            image(B - 1, True)
            for k in range(2):
                sp.wait_ge(gone[k], 16 * (NTT // 2) + 16)

        @block.tensor
        def _(pe):
            def up(k, m):
                e, hb = divmod(m, HB)
                for h in range(2):
                    cols = slice(hb * 128, hb * 128 + 128)
                    mm = products(pe, ps_h[m % 4][:, 0:TT], (we["w1_hi"][:, e, h, cols], x_hi[:, h, :]),
                                  (we["w1_lo"][:, e, h, cols], x_lo[:, h, :]), h == 0, h == 1)
                mm.then_inc(h_full, 1)
                if hb == 0:
                    pe.matmul(ps_w[e % 2][:, 0:TT], keep["exp_sel"][:, e, :], cw[:, k, :], start=True, stop=True).then_inc(w_full, 1)

            def start(i, k):
                pe.wait_ge(x_cut, i * 4 + 2 * k + 2)
                pe.wait_ge(here[k % 2], i * 32 + 32 * (k // 2) + 32)
                up(k % 2, 0)

            def pair(i, last):
                for k in range(2):
                    up(k, 1)
                    pe.wait_ge(o_read, i * 2 + k + 2)
                    for o in range(2):
                        pe.matmul(ps_o[:, o, 0:TT], we["b2"][:, o * 128:o * 128 + 128], cw[:, k, :], start=True, stop=False)
                    for m in range(M):
                        e, hb = divmod(m, HB)
                        if m + 2 < M:
                            up(k, m + 2)
                        elif m == M - 1 and not (last and k):
                            start(i, k + 1)
                        pe.wait_ge(lo_done, i * (2 * M) + k * M + m + 1)
                        for o in range(2):
                            cols = slice(o * 128, o * 128 + 128)
                            mm = products(pe, ps_o[:, o, 0:TT], (we["w2_hi"][:, e, hb, cols], h_hi[m % 4][:, :]),
                                          (we["w2_lo"][:, e, hb, cols], h_lo[m % 4][:, :]), False, m == M - 1)
                    mm.then_inc(o_full, 1)

            start(0, 0)
            with pe.Fori(0, NTT // 2 - 1) as i:
                pair(i, False)
            pair(NTT // 2 - 1, True)

        @block.scalar
        def _(act):
            def cut(t):
                act.activation(x_hi[:, :, :], xl[:, :, bass.ds(t * TT, TT)], ACT.Copy).then_inc(x_cut, 1)

            def high(t, m):
                act.wait_ge(hw_done, t * M + m + 1)
                act.activation(h_hi[m % 4][:, :], hg[m % 4][:, :], ACT.Copy).then_inc(hi_done, 1)

            def tile(t, last):
                for m in range(M):
                    e, hb = divmod(m, HB)
                    act.wait_ge(h_full, t * M + m + 1)
                    act.activation(hg[m % 4][:, :], ps_h[m % 4][:, 0:TT], ACT.Gelu, bias=we["b1"][:, e, hb:hb + 1]).then_inc(g_done, 1)
                    if m == M - 1 and not last:
                        cut(t + 1)
                    if m:
                        high(t, m - 1)
                high(t, M - 1)

            cut(0)
            with act.Fori(0, NTT - 1) as t:
                tile(t, False)
            tile(NTT - 1, True)

        @block.gpsimd
        def _(pool):
            pool.sem_inc(hi_done, 1)
            with pool.Fori(0, NTT) as i:
                for m in range(M):
                    pool.wait_ge(hi_done, i * M + m + 2)
                    pool.tensor_tensor(h_lo[m % 4][:, :], hg[m % 4][:, :], h_hi[m % 4][:, :].bitcast(F32), ALU.subtract).then_inc(lo_done, 1)

        @block.vector
        def _(dve):
            def cut(t):
                dve.wait_ge(x_cut, t * 2 + 1)
                dve.tensor_tensor(x_lo[:, :, :], xl[:, :, bass.ds(t * TT, TT)], x_hi[:, :, :].bitcast(F32), ALU.subtract).then_inc(x_cut, 1)

            def pair(i, last):
                for k in range(2):
                    for m in range(M):
                        e, hb = divmod(m, HB)
                        if hb == 0:
                            dve.wait_ge(w_full, i * (2 * E) + k * E + e + 1)
                        dve.wait_ge(g_done, i * (2 * M) + k * M + m + 1)
                        dve.tensor_tensor(hg[m % 4][:, :], hg[m % 4][:, :], ps_w[e % 2][:, 0:TT], ALU.mult).then_inc(hw_done, 1)
                    if not (last and k):
                        cut(i * 2 + (k + 1))
                    dve.wait_ge(o_full, i * 2 + k + 1)
                    dve.wait_ge(here[k], i * 32 + 32)
                    dve.tensor_tensor(x2[:, k, :, :], ps_o[:, :, 0:TT], x2[:, k, :, :], ALU.add).then_inc(o_read, 1)

            cut(0)
            with dve.Fori(0, NTT // 2 - 1) as i:
                pair(i, False)
            pair(NTT // 2 - 1, True)


def conv_attn_hybrid_kernel(nc, x, w0, w1, out):
    dram = lambda name, shape, dt=F32: nc.dram_tensor(name, shape, dt).ap()
    P = {
        "xn": dram("xn_dram", (B, C, L)),
        "rec": dram("rec_dram", (U, STEPS, 128, G + 1)),
        "xs": dram("xs_dram", (U, 128, L)),
        "parts": dram("parts_dram", (U, STEPS, 2, 128, 2, WC)),
        "bc": dram("bc_dram", (U, STEPS, 2 * N, WC)),
        "y": dram("y_dram", (U, STEPS, 128, WC)),
        "z": dram("z_dram", (B, C, L)),
        "zn": dram("zn_dram", (B, C, L)),
        "x1": dram("x1_dram", (NTT, 128, 2, TT)),
        "x2": dram("x2_dram", (NTT, 128, 2, TT)),
        "cw": dram("cw_dram", (E, NT)),
    }
    with ExitStack() as ctx:
        s = Space(nc, ctx, "keep")
        shapes = {
            "ident": [128, 128], "ones_c": [128, 128], "ones": [128, 128], "eps": [128, 1], "ln_2_20": [128, 1],
            "exp_sel": [E, E, 128], "ln_g": [128, 2], "ln_b": [128, 2], "proj_b": [128, 2], "proj_W": [128, 2, C],
        }
        scan_shapes = {
            "ones_d": [128, 128], "sum_sel": [128, 2 * D - J], "rec": [128, STEPS, G + 1],
            "w_eff": [128, K, D], "w_bc": [128, K, 2 * N], "w_pair": [128, 3, D], "w_one": [DM, 3, D],
            "dt_b": [D, K], "conv_b": [D, 1], "onorm_g": [D, 1], "onorm_b": [D, 1], "out_W": [D, DM], "d_sum": [D, 1],
            "skip": [DM, 1],
        }
        keep = {name: s.sb(name, shape) for name, shape in shapes.items()}
        with ExitStack() as mamba:
            m = Space(nc, mamba, "layer0")
            keep |= {name: m.sb(name, shape) for name, shape in scan_shapes.items()}
            keep["parts_sel"] = m.sb("parts_sel", [64, 4, J, N], F32R)
            setup_phase(nc, P, w0, keep)
            norm_phase(nc, "norm0", x.rearrange("b c y x -> b c (y x)"), P["xn"], keep)
            delta_phase(nc, P, keep)
            scan_phase(nc, P, keep)
            merge_phase(nc, P, keep)
        norm_phase(nc, "norm1", P["z"], P["zn"], keep)
        o_t = s.sb("o_t", [128, 2, NT])
        with ExitStack() as attn:
            f_hi, f_lo = (attn.enter_context(nc.sbuf_tensor(n, [128, 2, NT], F32R)) for n in ("f_hi", "f_lo"))
            den = attn.enter_context(nc.sbuf_tensor("den", [128, KB, NTT], F32))
            project_phase(nc, P, keep, f_hi, f_lo)
            attention_phase(nc, keep, f_hi, f_lo, o_t, den)
            blend_phase(nc, P, keep, f_hi, f_lo, o_t, den)
        we = {n: s.sb(n, [128, E, 2, HF], F32R) for n in ("w1_hi", "w1_lo")}
        we |= {n: s.sb(n, [128, E, HB, C], F32R) for n in ("w2_hi", "w2_lo")}
        we["b1"], we["b2"] = s.sb("b1", [128, E, HB]), s.sb("b2", [E, C])
        gate_phase(nc, P, w1, keep, o_t, we)
        expert_phase(nc, P, keep, o_t, we, out)


_L0 = ["ln_g", "ln_b", "skip_scale", "proj_W", "proj_b", "in_W", "conv_W", "conv_b", "x_proj_W", "dt_W", "dt_b",
       "A_logs", "Ds", "onorm_g", "onorm_b", "out_W"]
_L1 = ["gate_w", "gate_b", "W1", "b1", "W2", "b2"]


def kernel(**inputs):
    import numpy as _np
    import concourse.bacc as _bacc
    from concourse.bass_utils import run_bass_kernel_spmd as _run

    nc = _bacc.Bacc("TRN2", target_bir_lowering=False, num_devices=1)
    arrays, args = {}, {}
    for name, value in inputs.items():
        a = _np.ascontiguousarray(value)
        arrays[f"in_{name}"] = a
        args[name] = nc.dram_tensor(f"in_{name}", a.shape, mybir.dt.from_np(a.dtype), kind="ExternalInput").ap()
    out = nc.dram_tensor("out_x", (B, C, H, W), F32, kind="ExternalOutput").ap()
    conv_attn_hybrid_kernel(nc, args["x"], {n: args[f"L0_conv_{n}"] for n in _L0}, {n: args[f"L1_ffn_{n}"] for n in _L1}, out)
    r = _run(nc, [arrays], core_ids=[0])
    return r.results[0]["out_x"]
```
